# Optimizing a Trainium2 kernel written in Bass

```python
import numpy as np
import jax
import jax.numpy as jnp

def _softmax(x, axis=-1):
    return jax.nn.softmax(x, axis=axis)

def _gelu(x):
    return jax.nn.gelu(x, approximate=True)

def _silu(x):
    return jax.nn.silu(x)

def _sigmoid(x):
    return jax.nn.sigmoid(x)

def _layernorm(x, axis=-1, eps=1e-05):
    m = jnp.mean(x, axis=axis, keepdims=True)
    v = jnp.var(x, axis=axis, keepdims=True)
    return (x - m) / jnp.sqrt(v + eps)

def _scatter_add(tgt, idx, src, axis=0):
    return tgt.at[idx].add(src)

def _segment_sum(src, seg, n):
    return jax.ops.segment_sum(src, seg, n)
kernel_name = 'mk_xattn_ffn_d2_seqx_r8_df4a0a'

def setup_inputs(seed: int=0):
    np.random.seed(seed)
    _w = jnp.asarray

    def _rec_inputs():
        import jax
        import jax.numpy as jnp
        _rk = jax.random.key(seed)
        x = 7.22e-05 + 1 * jax.random.normal(jax.random.fold_in(_rk, 1), (64, 64, 128), jnp.float32)
        _lenS = 64 - jax.random.randint(jax.random.fold_in(_rk, 7), (64,), 0, max(1, 64 // 4) + 1, jnp.int32)
        _lenS2 = 64 - jax.random.randint(jax.random.fold_in(_rk, 8), (64,), 0, max(1, 64 // 4) + 1, jnp.int32)
        _ctx_768P = jax.random.normal(jax.random.fold_in(_rk, 11), (64, 16, 96), jnp.float32)
        _ctx_768c = jax.random.dirichlet(jax.random.fold_in(_rk, 511), 0.3 * jnp.ones((16,), jnp.float32), (64, 64))
        _ctx_768t = jnp.einsum('bsk,bkd->bsd', _ctx_768c, _ctx_768P)
        _ctx_768t = _ctx_768t * jax.lax.rsqrt(jnp.mean(jnp.square(_ctx_768t)) + 1e-12) * 0.953939
        ctx_768 = 3.88148e-05 + 0.999967 * (_ctx_768t + 0.3 * jax.random.normal(jax.random.fold_in(_rk, 611), (64, 64, 96), jnp.float32))
        _validS = jnp.arange(64)[None, :] < _lenS[:, None]
        _validS2 = jnp.arange(64)[None, :] < _lenS2[:, None]
        _causal = jnp.tril(jnp.ones((64, 64), dtype=bool))
        mask_BxS_bf1 = jnp.ones((64, 64), dtype=bool)
        mask_BxS2_bf1 = jnp.ones((64, 64), dtype=bool)
        return (x, ctx_768, mask_BxS_bf1, mask_BxS2_bf1)
    x, ctx_768, mask_BxS_bf1, mask_BxS2_bf1 = _rec_inputs()

    def _L0_xattn_setup():
        import jax, jax.numpy as jnp
        import numpy as np
        B, T, DT, G, DV = (16, 64, 128, 72, 96)
        H, DH = (4, 32)
        INNER = H * DH
        HID = 4 * DT
        N_STATE = 64
        K_TOP = 32

        def layernorm(x, g, b, eps=1e-05):
            m = x.mean(-1, keepdims=True)
            v = x.var(-1, keepdims=True)
            return (x - m) * jax.lax.rsqrt(v + eps) * g + b

        def s4d(x, log_dt, A_re, A_im, C_re, C_im, D_skip):
            Bb, L, D = x.shape
            dt = jnp.exp(log_dt)
            A = A_re + 1j * A_im
            C = C_re + 1j * C_im
            dtA = dt[:, None] * A
            dC = C * (jnp.exp(dtA) - 1.0) / A
            powers = jnp.exp(dtA[:, :, None] * jnp.arange(L))
            K = 2.0 * jnp.einsum('dn,dnl->dl', dC, powers).real
            n = 2 * L
            Kf = jnp.fft.rfft(K, n=n, axis=-1)
            xf = jnp.fft.rfft(x, n=n, axis=1)
            y = jnp.fft.irfft(xf * Kf.T[None], n=n, axis=1)[:, :L]
            return y + x * D_skip
        key = jax.random.key(seed)
        ks = jax.random.split(key, 16)
        s = 0.02
        inp = {'x_text': jax.random.normal(ks[0], (B, T, DT), jnp.float32), 'x_vision': jax.random.normal(ks[1], (B, G, DV), jnp.float32), 'text_mask': jnp.ones((B, T), bool), 'vision_mask': jnp.ones((B, G), bool), 'Wq': jax.random.normal(ks[2], (DT, INNER), jnp.float32) * s, 'Wk': jax.random.normal(ks[3], (DV, INNER), jnp.float32) * s, 'Wv': jax.random.normal(ks[4], (DV, DT), jnp.float32) * s, 'W_film_in': jax.random.normal(ks[5], (DT, 2 * DT), jnp.float32) * s, 'b_film_in': jnp.zeros((2 * DT,), jnp.float32), 'W_film_out': jax.random.normal(ks[6], (DT, 2 * DT), jnp.float32) * s, 'b_film_out': jnp.zeros((2 * DT,), jnp.float32), 'g_norm_in': jnp.ones((DT,), jnp.float32), 'b_norm_in': jnp.zeros((DT,), jnp.float32), 'g_norm_out': jnp.ones((DT,), jnp.float32), 'b_norm_out': jnp.zeros((DT,), jnp.float32), 'g_ffn': jnp.ones((DT,), jnp.float32), 'b_ffn': jnp.zeros((DT,), jnp.float32), 'W1': jax.random.normal(ks[7], (DT, HID), jnp.float32) * s, 'b1': jnp.zeros((HID,), jnp.float32), 'W2': jax.random.normal(ks[8], (HID, DT), jnp.float32) * s, 'b2': jnp.zeros((DT,), jnp.float32), 'log_dt': jnp.log(0.001) + jax.random.uniform(ks[9], (DT,), jnp.float32) * (jnp.log(0.1) - jnp.log(0.001)), 'A_re': -0.5 * jnp.ones((DT, N_STATE), jnp.float32), 'A_im': jnp.tile(jnp.pi * jnp.arange(N_STATE, dtype=jnp.float32), (DT, 1)), 'C_re': jax.random.normal(ks[10], (DT, N_STATE), jnp.float32) * 0.5 ** 0.5, 'C_im': jax.random.normal(ks[11], (DT, N_STATE), jnp.float32) * 0.5 ** 0.5, 'D_skip': jax.random.normal(ks[12], (DT,), jnp.float32), 'mod_gate': jnp.array(0.5, jnp.float32)}
        return inp
    _L0_xattn_all = _L0_xattn_setup()
    _L0_xattn_in = {k: v for k, v in _L0_xattn_all.items() if k in ('Wq', 'Wk', 'Wv', 'W_film_in', 'b_film_in', 'W_film_out', 'b_film_out', 'g_norm_in', 'b_norm_in', 'g_norm_out', 'b_norm_out', 'g_ffn', 'b_ffn', 'W1', 'b1', 'W2', 'b2', 'log_dt', 'A_re', 'A_im', 'C_re', 'C_im', 'D_skip', 'mod_gate')}
    del _L0_xattn_all

    def _L0_ffn_setup():
        import jax, jax.numpy as jnp
        import numpy as np
        B, T, C, E, K, CAP, H = (8, 256, 128, 8, 2, 512, 512)
        key = jax.random.key(seed)
        ks = jax.random.split(key, 6)
        s = 0.02
        return {'x': jax.random.normal(ks[0], (B, T, C), jnp.float32), 'rw1': s * jax.random.normal(ks[1], (C, H), jnp.float32), 'rb1': jnp.zeros((H,), jnp.float32), 'rw2': s * jax.random.normal(ks[2], (H, E), jnp.float32), 'rb2': jnp.zeros((E,), jnp.float32), 'ew1': s * jax.random.normal(ks[3], (E, C, H), jnp.float32), 'eb1': jnp.zeros((E, H), jnp.float32), 'ew2': s * jax.random.normal(ks[4], (E, H, C), jnp.float32), 'eb2': jnp.zeros((E, C), jnp.float32)}
    _L0_ffn_all = _L0_ffn_setup()
    _L0_ffn_in = {k: v for k, v in _L0_ffn_all.items() if k in ('rw1', 'rb1', 'rw2', 'rb2', 'ew1', 'eb1', 'ew2', 'eb2')}
    del _L0_ffn_all

    def _L1_xattn_setup():
        import jax, jax.numpy as jnp
        import numpy as np
        B, LQ, LKV = (4, 64, 256)
        DQ, DKV, H = (128, 96, 16)
        HD = DQ // H
        key = jax.random.key(seed)
        ks = jax.random.split(key, 12)
        s_q = 1.0 / np.sqrt(DQ)
        s_kv = 1.0 / np.sqrt(DKV)
        return {'q': jax.random.normal(ks[0], (B, LQ, DQ), jnp.float32), 'kv': jax.random.normal(ks[1], (B, LKV, DKV), jnp.float32), 'Wq': jax.random.normal(ks[2], (DQ, DQ), jnp.float32) * s_q, 'bq': jnp.zeros((DQ,), jnp.float32), 'Wk': jax.random.normal(ks[3], (DKV, DQ), jnp.float32) * s_kv, 'bk': jnp.zeros((DQ,), jnp.float32), 'Wv': jax.random.normal(ks[4], (DKV, DQ), jnp.float32) * s_kv, 'bv': jnp.zeros((DQ,), jnp.float32), 'Wo': jax.random.normal(ks[5], (DQ, DQ), jnp.float32) * s_q, 'bo': jnp.zeros((DQ,), jnp.float32), 'scale': jnp.ones((1,), jnp.float32) * DQ ** (-0.5)}
    _L1_xattn_all = _L1_xattn_setup()
    _L1_xattn_in = {k: v for k, v in _L1_xattn_all.items() if k in ('Wq', 'bq', 'Wk', 'bk', 'Wv', 'bv', 'Wo', 'bo', 'scale')}
    del _L1_xattn_all

    def _L1_ffn_setup():
        import jax, jax.numpy as jnp
        import numpy as np
        DIM = 128
        HID = 256
        E = 8
        K = 2
        R = 16
        B_, S_ = (2, 128)

        def _lora_in(xf, W, b, A, B):
            base = jnp.einsum('td,ehd->teh', xf, W)
            low = jnp.einsum('ter,ehr->teh', jnp.einsum('td,erd->ter', xf, A), B)
            return base + low + b

        def _lora_out(g, W, b, A, B):
            base = jnp.einsum('teh,edh->ted', g, W)
            low = jnp.einsum('ter,edr->ted', jnp.einsum('teh,erh->ter', g, A), B)
            return base + low + b
        key = jax.random.key(seed)
        ks = jax.random.split(key, 14)
        n = lambda k, shape, scale: jax.random.normal(k, shape, jnp.float32) * scale
        inp = {'x': jax.random.normal(ks[0], (B_, S_, DIM), jnp.float32), 'Wg': n(ks[1], (E, DIM), DIM ** (-0.5)), 'W1': n(ks[2], (E, HID, DIM), DIM ** (-0.5)), 'b1': jnp.zeros((E, HID), jnp.float32), 'A1': n(ks[3], (E, R, DIM), DIM ** (-0.5)), 'B1': n(ks[4], (E, HID, R), 0.01), 'W2': n(ks[5], (E, DIM, HID), HID ** (-0.5)), 'b2': jnp.zeros((E, DIM), jnp.float32), 'A2': n(ks[6], (E, R, HID), HID ** (-0.5)), 'B2': n(ks[7], (E, DIM, R), 0.01), 'W3': n(ks[8], (E, HID, DIM), DIM ** (-0.5)), 'b3': jnp.zeros((E, HID), jnp.float32), 'A3': n(ks[9], (E, R, DIM), DIM ** (-0.5)), 'B3': n(ks[10], (E, HID, R), 0.01)}
        return inp
    _L1_ffn_all = _L1_ffn_setup()
    _L1_ffn_in = {k: v for k, v in _L1_ffn_all.items() if k in ('Wg', 'W1', 'b1', 'A1', 'B1', 'W2', 'b2', 'A2', 'B2', 'W3', 'b3', 'A3', 'B3')}
    del _L1_ffn_all
    return {'x': x, 'ctx_768': ctx_768, 'mask_BxS_bf1': mask_BxS_bf1, 'mask_BxS2_bf1': mask_BxS2_bf1, 'L0_xattn_Wq': _L0_xattn_in['Wq'], 'L0_xattn_Wk': _L0_xattn_in['Wk'], 'L0_xattn_Wv': _L0_xattn_in['Wv'], 'L0_xattn_W_film_in': _L0_xattn_in['W_film_in'], 'L0_xattn_b_film_in': _L0_xattn_in['b_film_in'], 'L0_xattn_W_film_out': _L0_xattn_in['W_film_out'], 'L0_xattn_b_film_out': _L0_xattn_in['b_film_out'], 'L0_xattn_g_norm_in': _L0_xattn_in['g_norm_in'], 'L0_xattn_b_norm_in': _L0_xattn_in['b_norm_in'], 'L0_xattn_g_norm_out': _L0_xattn_in['g_norm_out'], 'L0_xattn_b_norm_out': _L0_xattn_in['b_norm_out'], 'L0_xattn_g_ffn': _L0_xattn_in['g_ffn'], 'L0_xattn_b_ffn': _L0_xattn_in['b_ffn'], 'L0_xattn_W1': _L0_xattn_in['W1'], 'L0_xattn_b1': _L0_xattn_in['b1'], 'L0_xattn_W2': _L0_xattn_in['W2'], 'L0_xattn_b2': _L0_xattn_in['b2'], 'L0_xattn_log_dt': _L0_xattn_in['log_dt'], 'L0_xattn_A_re': _L0_xattn_in['A_re'], 'L0_xattn_A_im': _L0_xattn_in['A_im'], 'L0_xattn_C_re': _L0_xattn_in['C_re'], 'L0_xattn_C_im': _L0_xattn_in['C_im'], 'L0_xattn_D_skip': _L0_xattn_in['D_skip'], 'L0_xattn_mod_gate': _L0_xattn_in['mod_gate'], 'L0_ffn_rw1': _L0_ffn_in['rw1'], 'L0_ffn_rb1': _L0_ffn_in['rb1'], 'L0_ffn_rw2': _L0_ffn_in['rw2'], 'L0_ffn_rb2': _L0_ffn_in['rb2'], 'L0_ffn_ew1': _L0_ffn_in['ew1'], 'L0_ffn_eb1': _L0_ffn_in['eb1'], 'L0_ffn_ew2': _L0_ffn_in['ew2'], 'L0_ffn_eb2': _L0_ffn_in['eb2'], 'L1_xattn_Wq': _L1_xattn_in['Wq'], 'L1_xattn_bq': _L1_xattn_in['bq'], 'L1_xattn_Wk': _L1_xattn_in['Wk'], 'L1_xattn_bk': _L1_xattn_in['bk'], 'L1_xattn_Wv': _L1_xattn_in['Wv'], 'L1_xattn_bv': _L1_xattn_in['bv'], 'L1_xattn_Wo': _L1_xattn_in['Wo'], 'L1_xattn_bo': _L1_xattn_in['bo'], 'L1_xattn_scale': _L1_xattn_in['scale'], 'L1_ffn_Wg': _L1_ffn_in['Wg'], 'L1_ffn_W1': _L1_ffn_in['W1'], 'L1_ffn_b1': _L1_ffn_in['b1'], 'L1_ffn_A1': _L1_ffn_in['A1'], 'L1_ffn_B1': _L1_ffn_in['B1'], 'L1_ffn_W2': _L1_ffn_in['W2'], 'L1_ffn_b2': _L1_ffn_in['b2'], 'L1_ffn_A2': _L1_ffn_in['A2'], 'L1_ffn_B2': _L1_ffn_in['B2'], 'L1_ffn_W3': _L1_ffn_in['W3'], 'L1_ffn_b3': _L1_ffn_in['b3'], 'L1_ffn_A3': _L1_ffn_in['A3'], 'L1_ffn_B3': _L1_ffn_in['B3']}

def reference(x, ctx_768, mask_BxS_bf1, mask_BxS2_bf1, L0_xattn_Wq, L0_xattn_Wk, L0_xattn_Wv, L0_xattn_W_film_in, L0_xattn_b_film_in, L0_xattn_W_film_out, L0_xattn_b_film_out, L0_xattn_g_norm_in, L0_xattn_b_norm_in, L0_xattn_g_norm_out, L0_xattn_b_norm_out, L0_xattn_g_ffn, L0_xattn_b_ffn, L0_xattn_W1, L0_xattn_b1, L0_xattn_W2, L0_xattn_b2, L0_xattn_log_dt, L0_xattn_A_re, L0_xattn_A_im, L0_xattn_C_re, L0_xattn_C_im, L0_xattn_D_skip, L0_xattn_mod_gate, L0_ffn_rw1, L0_ffn_rb1, L0_ffn_rw2, L0_ffn_rb2, L0_ffn_ew1, L0_ffn_eb1, L0_ffn_ew2, L0_ffn_eb2, L1_xattn_Wq, L1_xattn_bq, L1_xattn_Wk, L1_xattn_bk, L1_xattn_Wv, L1_xattn_bv, L1_xattn_Wo, L1_xattn_bo, L1_xattn_scale, L1_ffn_Wg, L1_ffn_W1, L1_ffn_b1, L1_ffn_A1, L1_ffn_B1, L1_ffn_W2, L1_ffn_b2, L1_ffn_A2, L1_ffn_B2, L1_ffn_W3, L1_ffn_b3, L1_ffn_A3, L1_ffn_B3):
    import jax
    import jax.numpy as jnp

    def _L0_xattn_ref(x_text, x_vision, text_mask, vision_mask, Wq, Wk, Wv, W_film_in, b_film_in, W_film_out, b_film_out, g_norm_in, b_norm_in, g_norm_out, b_norm_out, g_ffn, b_ffn, W1, b1, W2, b2, log_dt, A_re, A_im, C_re, C_im, D_skip, mod_gate):
        import jax, jax.numpy as jnp
        import numpy as np
        B, T, DT, G, DV = (16, 64, 128, 72, 96)
        H, DH = (4, 32)
        INNER = H * DH
        HID = 4 * DT
        N_STATE = 64
        K_TOP = 32

        def layernorm(x, g, b, eps=1e-05):
            m = x.mean(-1, keepdims=True)
            v = x.var(-1, keepdims=True)
            return (x - m) * jax.lax.rsqrt(v + eps) * g + b

        def s4d(x, log_dt, A_re, A_im, C_re, C_im, D_skip):
            Bb, L, D = x.shape
            dt = jnp.exp(log_dt)
            A = A_re + 1j * A_im
            C = C_re + 1j * C_im
            dtA = dt[:, None] * A
            dC = C * (jnp.exp(dtA) - 1.0) / A
            powers = jnp.exp(dtA[:, :, None] * jnp.arange(L))
            K = 2.0 * jnp.einsum('dn,dnl->dl', dC, powers).real
            n = 2 * L
            Kf = jnp.fft.rfft(K, n=n, axis=-1)
            xf = jnp.fft.rfft(x, n=n, axis=1)
            y = jnp.fft.irfft(xf * Kf.T[None], n=n, axis=1)[:, :L]
            return y + x * D_skip
        Bb, Tt, D = x_text.shape
        Gg = x_vision.shape[1]
        Q = (x_text @ Wq).reshape(Bb, Tt, H, DH)
        K = (x_vision @ Wk).reshape(Bb, Gg, H, DH)
        scores = jnp.einsum('bthd,bghd->bhtg', Q, K) / np.sqrt(DH).astype(np.float32)
        scores = jnp.where(vision_mask[:, None, None, :], scores, -jnp.inf)
        topv, topi = jax.lax.top_k(scores, K_TOP)
        probs = jax.nn.softmax(topv, axis=-1)
        bi = jnp.arange(Bb)[:, None, None, None]
        hi = jnp.arange(H)[None, :, None, None]
        ti = jnp.arange(Tt)[None, None, :, None]
        attn = jnp.zeros_like(scores).at[bi, hi, ti, topi].set(probs)
        attn_mean = attn.mean(axis=1)
        V = x_vision @ Wv
        c_t = jnp.einsum('btg,bgd->btd', attn_mean, V)
        c_t = c_t * text_mask[..., None]
        x = layernorm(x_text, g_norm_in, b_norm_in)
        scale_in, shift_in = jnp.split(c_t @ W_film_in + b_film_in, 2, axis=-1)
        x = x * (1.0 + mod_gate * scale_in) + mod_gate * shift_in
        y = s4d(x, log_dt, A_re, A_im, C_re, C_im, D_skip)
        scale_out, shift_out = jnp.split(c_t @ W_film_out + b_film_out, 2, axis=-1)
        y = y * (1.0 + mod_gate * scale_out) + mod_gate * shift_out
        xt = x_text + y
        h = layernorm(xt, g_ffn, b_ffn)
        h = jax.nn.gelu(h @ W1 + b1, approximate=False) @ W2 + b2
        xt = xt + h
        return layernorm(xt, g_norm_out, b_norm_out)

    def _L0_ffn_ref(x, rw1, rb1, rw2, rb2, ew1, eb1, ew2, eb2):
        import jax, jax.numpy as jnp
        import numpy as np
        B, T, C, E, K, CAP, H = (8, 256, 128, 8, 2, 512, 512)
        Bx, Tx, Cx = x.shape
        N = Bx * Tx
        logits = jax.nn.relu(x @ rw1 + rb1) @ rw2 + rb2
        vals, ids = jax.lax.top_k(logits, K)
        probs = jax.nn.softmax(vals, axis=-1)
        ids_f = ids.reshape(N * K)
        probs_f = probs.reshape(N * K)
        xr = jnp.repeat(x.reshape(N, Cx), K, axis=0)
        m = jax.nn.one_hot(ids_f, E, dtype=jnp.int32)
        pos = jnp.cumsum(m, axis=0) - 1
        pos_tok = jnp.take_along_axis(pos, ids_f[:, None], axis=1)[:, 0]
        keep = (pos_tok < CAP).astype(x.dtype)
        pos_c = jnp.clip(pos_tok, 0, CAP - 1)
        disp = jnp.zeros((E, CAP, Cx), x.dtype).at[ids_f, pos_c].add(xr * keep[:, None])
        h = jax.nn.relu(jnp.einsum('enc,ech->enh', disp, ew1) + eb1[:, None, :])
        eo = jnp.einsum('enh,ehc->enc', h, ew2) + eb2[:, None, :]
        y = eo[ids_f, pos_c] * (probs_f * keep)[:, None]
        return y.reshape(Bx, Tx, K, Cx).sum(axis=2)

    def _L1_xattn_ref(q, kv, Wq, bq, Wk, bk, Wv, bv, Wo, bo, scale):
        import jax, jax.numpy as jnp
        import numpy as np
        B, LQ, LKV = (4, 64, 256)
        DQ, DKV, H = (128, 96, 16)
        HD = DQ // H
        b, lq, _ = q.shape
        lkv = kv.shape[1]
        qh = (q @ Wq + bq).reshape(b, lq, H, HD).transpose(0, 2, 1, 3)
        kh = (kv @ Wk + bk).reshape(b, lkv, H, HD).transpose(0, 2, 1, 3)
        vh = (kv @ Wv + bv).reshape(b, lkv, H, HD).transpose(0, 2, 1, 3)
        scores = jnp.einsum('bhqd,bhkd->bhqk', qh, kh) * scale[0]
        attn = jax.nn.softmax(scores, axis=-1)
        out = jnp.einsum('bhqk,bhkd->bhqd', attn, vh)
        out = out.transpose(0, 2, 1, 3).reshape(b, lq, DQ)
        return out @ Wo + bo

    def _L1_ffn_ref(x, Wg, W1, b1, A1, B1, W2, b2, A2, B2, W3, b3, A3, B3):
        import jax, jax.numpy as jnp
        import numpy as np
        DIM = 128
        HID = 256
        E = 8
        K = 2
        R = 16
        B_, S_ = (2, 128)

        def _lora_in(xf, W, b, A, B):
            base = jnp.einsum('td,ehd->teh', xf, W)
            low = jnp.einsum('ter,ehr->teh', jnp.einsum('td,erd->ter', xf, A), B)
            return base + low + b

        def _lora_out(g, W, b, A, B):
            base = jnp.einsum('teh,edh->ted', g, W)
            low = jnp.einsum('ter,edr->ted', jnp.einsum('teh,erh->ter', g, A), B)
            return base + low + b
        orig_shape = x.shape
        xf = x.reshape(-1, x.shape[-1])
        scores = jax.nn.softmax(xf @ Wg.T, axis=-1)
        expert_weights, expert_indices = jax.lax.top_k(scores, K)
        expert_weights = expert_weights / expert_weights.sum(-1, keepdims=True)
        gates = (jax.nn.one_hot(expert_indices, E, dtype=xf.dtype) * expert_weights[..., None]).sum(axis=1)
        h1 = _lora_in(xf, W1, b1, A1, B1)
        h3 = _lora_in(xf, W3, b3, A3, B3)
        g = jax.nn.silu(h1) * h3
        y_e = _lora_out(g, W2, b2, A2, B2)
        y = jnp.einsum('te,ted->td', gates, y_e)
        return y.reshape(orig_shape)
    x = x + _L0_xattn_ref(_layernorm(x, axis=-1), ctx_768, mask_BxS_bf1, mask_BxS2_bf1, L0_xattn_Wq, L0_xattn_Wk, L0_xattn_Wv, L0_xattn_W_film_in, L0_xattn_b_film_in, L0_xattn_W_film_out, L0_xattn_b_film_out, L0_xattn_g_norm_in, L0_xattn_b_norm_in, L0_xattn_g_norm_out, L0_xattn_b_norm_out, L0_xattn_g_ffn, L0_xattn_b_ffn, L0_xattn_W1, L0_xattn_b1, L0_xattn_W2, L0_xattn_b2, L0_xattn_log_dt, L0_xattn_A_re, L0_xattn_A_im, L0_xattn_C_re, L0_xattn_C_im, L0_xattn_D_skip, L0_xattn_mod_gate)
    x = x + _L0_ffn_ref(_layernorm(x, axis=-1), L0_ffn_rw1, L0_ffn_rb1, L0_ffn_rw2, L0_ffn_rb2, L0_ffn_ew1, L0_ffn_eb1, L0_ffn_ew2, L0_ffn_eb2)
    x = x + _L1_xattn_ref(_layernorm(x, axis=-1), ctx_768, L1_xattn_Wq, L1_xattn_bq, L1_xattn_Wk, L1_xattn_bk, L1_xattn_Wv, L1_xattn_bv, L1_xattn_Wo, L1_xattn_bo, L1_xattn_scale)
    x = x + _L1_ffn_ref(_layernorm(x, axis=-1), L1_ffn_Wg, L1_ffn_W1, L1_ffn_b1, L1_ffn_A1, L1_ffn_B1, L1_ffn_W2, L1_ffn_b2, L1_ffn_A2, L1_ffn_B2, L1_ffn_W3, L1_ffn_b3, L1_ffn_A3, L1_ffn_B3)
    return x

_drawn_inputs = setup_inputs


def setup_inputs(seed=0):
    import zlib

    import numpy as np

    out = dict(_drawn_inputs(seed))
    spreads = {'L0_xattn_b_film_in': (0.0, 0.1),
     'L0_xattn_b_film_out': (0.0, 0.1),
     'L0_xattn_g_norm_in': (1.0, 0.2),
     'L0_xattn_b_norm_in': (0.0, 0.1),
     'L0_xattn_g_norm_out': (1.0, 0.2),
     'L0_xattn_b_norm_out': (0.0, 0.1),
     'L0_xattn_g_ffn': (1.0, 0.6),
     'L0_xattn_b_ffn': (0.0, 0.8),
     'L0_xattn_b1': (0.0, 0.391),
     'L0_xattn_b2': (0.0, 0.1),
     'L0_xattn_A_re': (-0.5, 0.563),
     'L0_ffn_rb1': (0.0, 0.367),
     'L0_ffn_rb2': (0.0, 0.1),
     'L0_ffn_eb1': (0.0, 0.59),
     'L0_ffn_eb2': (0.0, 0.286),
     'L1_xattn_bq': (0.0, 0.713),
     'L1_xattn_bk': (0.0, 2.0),
     'L1_xattn_bv': (0.0, 0.1),
     'L1_xattn_bo': (0.0, 0.1),
     'L1_ffn_b1': (0.0, 0.331),
     'L1_ffn_b2': (0.0, 0.394),
     'L1_ffn_b3': (0.0, 0.364)}
    factors = {'L0_xattn_Wq': 8.0,
     'L0_xattn_Wk': 7.404,
     'L0_xattn_Wv': 3.086,
     'L0_xattn_W_film_in': 3.869,
     'L0_xattn_W_film_out': 4.143,
     'L0_ffn_ew1': 3.254,
     'L0_ffn_ew2': 2.68,
     'L1_ffn_A1': 6.045,
     'L1_ffn_B1': 6.042,
     'L1_ffn_A2': 6.332,
     'L1_ffn_B2': 6.322,
     'L1_ffn_A3': 6.316,
     'L1_ffn_B3': 6.324}
    for name, (base, spread) in spreads.items():
        noise = np.random.default_rng([zlib.crc32(name.encode()), seed]).standard_normal(out[name].shape)
        drawn = base * np.exp(spread * noise) if base else spread * noise
        out[name] = jnp.asarray(drawn.astype(out[name].dtype))
    for name, factor in factors.items():
        out[name] = (out[name] * factor).astype(out[name].dtype)
    return out
```

```python
from contextlib import ExitStack

import numpy as np
import concourse.bass as bass
from concourse import mybir

F32 = mybir.dt.float32
U8 = mybir.dt.uint8
ALU = mybir.AluOpType
ACT = mybir.ActivationFunctionType
AX = mybir.AxisListType

P = 128
B, T, D = 64, 64, 128
DC = 96
NT = B * T // P
TB = 4
NBLK = NT // TB
H0, DH0 = 4, 32
H1, DH1 = 16, 8
KTOP = 32
NS = 64
HID = 512
NE = 8
CAP = 512
HE = 256
R = 16
EPS = 1e-5
MASKED = -1e30
TAKEN = -3e38
TWO_PI = 2.0 * np.pi
ROUND = float(1.5 * 2 ** 23)

VEC = {}
for _name, _n in (("L0_xattn_b1", 4), ("L0_ffn_rb1", 4), ("L1_xattn_bq", 1), ("L1_xattn_bk", 1),
                  ("L1_xattn_bv", 1), ("L0_xattn_g_ffn", 1), ("L0_xattn_b_ffn", 1),
                  ("L0_xattn_log_dt", 1), ("L0_xattn_D_skip", 1), ("L0_ffn_eb1", 32),
                  ("L1_ffn_b1", 16), ("L1_ffn_b3", 16)):
    VEC[_name] = (sum(n for _, n in VEC.values()), _n)
NVEC = sum(n for _, n in VEC.values())


class Steps:

    def __init__(self, eng, sem):
        self.eng, self.sem, self.n = eng, sem, 0

    def did(self, ins):
        ins.then_inc(self.sem, 1)
        self.n += 1

    def wait(self):
        self.eng.wait_ge(self.sem, self.n)

    def then(self, ins):
        self.did(ins)
        self.wait()

    def passed(self):
        self.eng.sem_inc(self.sem, 1)
        self.n += 1
        self.wait()

    def clear(self):
        self.wait()
        self.eng.sem_clear(self.sem)
        self.n = 0


class Chip:

    def __init__(self, nc, ctx):
        self.nc, self.ctx = nc, ctx
        self.own, self.before = [], []

    def sb(self, name, shape, dt=F32, ctx=None):
        return (ctx or self.ctx).enter_context(self.nc.sbuf_tensor(name, shape, dt))

    def ps(self, name, shape, ctx, dt=F32):
        return ctx.enter_context(self.nc.psum_tensor(name, shape, dt))

    def sem(self, name):
        self.own.append(self.nc.alloc_semaphore(name=name))
        return self.own[-1]

    def end_phase(self):
        for h in self.own:
            self.nc.sync.sem_clear(h)
        for h in self.before:
            self.nc.release_semaphore(h)
        self.own, self.before = [], self.own


class Tile:

    def __init__(self, t, k, j, fixed):
        self.t, self.k, self.j, self.fixed = t, k, j, fixed

    def by(self, d):
        q = self.j + d
        return Tile(self.t + d, self.k + q // 2, q % 2, self.fixed)

    def real(self):
        return not self.fixed or 0 <= self.t < NT


def sweep(eng, slot, first, lo, hi, last):
    for t in range(first, lo):
        slot(Tile(t, t // 2, t % 2, True))
    with eng.Fori(0, (hi - lo) // 2) as i:
        for q in range(2):
            slot(Tile(i * 2 + (lo + q), i + (lo + q) // 2, (lo + q) % 2, False))
    for t in range(hi, last):
        slot(Tile(t, t // 2, t % 2, True))


def after(eng, sem, n):
    if not isinstance(n, int) or n > 0:
        eng.wait_ge(sem, n)


def wide(ap, shape):
    return ap.to_broadcast(shape)


def row_statistics(dve, step, src, stats):
    with dve.Fori(0, NT // 2) as i:
        for j in range(2):
            t = i * 2 + j
            dve.bn_stats(stats[:, t, :], src[:, t, :])
    step.then(dve.memset(step.scratch, 0.0))


def mean_and_variance(dve, step, stats, mean, var, tmp):
    me, m2e, mo, m2o = (stats[:, :, k] for k in (1, 2, 4, 5))
    dve.tensor_tensor(mean, me, mo, ALU.add)
    dve.tensor_tensor(tmp, me, mo, ALU.subtract)
    step.then(dve.tensor_tensor(var, m2e, m2o, ALU.add))
    dve.tensor_scalar(mean, mean, 0.5, None, ALU.mult)
    dve.tensor_scalar(var, var, 1.0 / D, None, ALU.mult)
    step.then(dve.tensor_tensor(tmp, tmp, tmp, ALU.mult))
    step.then(dve.scalar_tensor_tensor(var, tmp, 0.25, var, ALU.mult, ALU.add))


def setup(nc, C, A, G):
    with ExitStack() as ctx:
        vrow = C.sb("vrow", [NVEC, D], ctx=ctx)
        mk8 = C.sb("mk8", [P, NT, T], U8, ctx)
        tm8 = C.sb("tm8", [NT, P], U8, ctx)
        tmf = C.sb("tmf", [NT, P], ctx=ctx)
        kin = C.sb("kin", [P, 4, NS], ctx=ctx)
        film0 = C.sb("film0", [P, 512], ctx=ctx)
        frow0 = C.sb("frow0", [1, 512], ctx=ctx)
        kt = C.sb("kt", [P, 16, NS], ctx=ctx)
        zV = C.sb("zV", [P, 8, 2, NS], ctx=ctx)
        zU = C.sb("zU", [P, 8, 2, NS], ctx=ctx)
        big = C.sb("big", [P, 8, 2, NS], ctx=ctx)
        ctm = C.sb("ctm", [P, 2, 8, NS], ctx=ctx)
        kpad = C.sb("kpad", [P, P], ctx=ctx)
        st = C.sb("st", [P, NT, 6], ctx=ctx)
        tmp = C.sb("tmp", [P, NT], ctx=ctx)
        var = C.sb("var", [P, NT], ctx=ctx)
        var2 = C.sb("var2", [P, NT], ctx=ctx)
        psv = C.ps("psv", [P, 512], ctx)
        pst = C.ps("pst", [P, 512], ctx)
        s = {n: C.sem("setup_" + n) for n in (
            "x", "kin", "vec", "masks", "film", "rest", "zero", "ident", "vec_ps", "vec_sb",
            "exp", "args", "trig", "var", "rms", "kpad", "kd", "dve", "act", "pool", "tmf", "tm_ps")}

        with nc.Block() as block:

            @block.sync
            def _(sp):
                sp.dma_start(kin[:, 0, :], A["L0_xattn_A_re"]).then_inc(s["kin"], 16)
                sp.dma_start(kin[:, 1, :], A["L0_xattn_A_im"]).then_inc(s["kin"], 16)
                sp.dma_start(kin[:, 2, :], A["L0_xattn_C_re"]).then_inc(s["kin"], 16)
                sp.dma_start(kin[:, 3, :], A["L0_xattn_C_im"]).then_inc(s["kin"], 16)
                for name, (at, n) in VEC.items():
                    src = A[name]
                    if len(src.shape) == 1:
                        src = src.rearrange("(c p) -> c p", p=D)
                    else:
                        src = src.rearrange("e (c p) -> (e c) p", p=D)
                    sp.dma_start(vrow[at:at + n, :], src).then_inc(s["vec"], 16)
                xv = A["x"].rearrange("(n b) t d -> (b t) n d", b=2)
                for k in range(4):
                    sp.dma_start(G.X[:, 8 * k:8 * k + 8, :], xv[:, 8 * k:8 * k + 8, :]).then_inc(s["x"], 16)
                for k, name in enumerate(("L0_xattn_W_film_in", "L0_xattn_W_film_out")):
                    sp.dma_start(film0[:, 256 * k:256 * k + 256], A[name]).then_inc(s["film"], 16)
                for k, name in enumerate(("L0_xattn_b_film_in", "L0_xattn_b_film_out")):
                    sp.dma_start(frow0[:, 256 * k:256 * k + 256],
                                 A[name].rearrange("(a n) -> a n", a=1)).then_inc(s["film"], 16)
                sp.dma_start(G.mg[:], A["L0_xattn_mod_gate"].partition_broadcast(P)).then_inc(s["film"], 16)
                m = A["mask_BxS2_bf1"]
                for b2 in range(2):
                    src = bass.AP(m.tensor, b2 * T, [[0, T], [2 * T, NT], [1, T]])
                    sp.dma_start(mk8[T * b2:T * b2 + T, :, :], src).then_inc(s["masks"], 16)
                sp.dma_start(tm8[:], A["mask_BxS_bf1"].rearrange("(n b) t -> n (b t)", b=2)).then_inc(s["masks"], 16)
                loads = [(G.gin[:], A["L0_xattn_g_norm_in"].partition_broadcast(P)),
                         (G.bin[:], A["L0_xattn_b_norm_in"].partition_broadcast(P)),
                         (G.wq[:], A["L0_xattn_Wq"]), (G.wk[:], A["L0_xattn_Wk"]), (G.wv[:], A["L0_xattn_Wv"])]
                for dst, src in loads:
                    sp.dma_start(dst, src).then_inc(s["rest"], 16)
                sp.wait_ge(s["rest"], 16 * len(loads))
                sp.wait_ge(s["kpad"], 1)
                sp.dma_start(G.kd, kpad[:]).then_inc(s["kd"], 16)
                sp.wait_ge(s["kd"], 16)

            @block.gpsimd
            def _(pool):
                pool.memset(G.ident[:], 0.0).then_inc(s["zero"], 1)
                pool.memset(G.triu[:], 1.0).then_inc(s["zero"], 1)
                pool.memset(G.ones[:], 1.0).then_inc(s["zero"], 1)
                pool.memset(G.onesrow[:], 1.0).then_inc(s["zero"], 1)
                pool.wait_ge(s["zero"], 4)
                pool.affine_select(out=G.ident[:], in_=G.ident[:], compare_op=ALU.not_equal, fill=1.0,
                                   base=0, pattern=[[-1, P]], channel_multiplier=1).then_inc(s["ident"], 1)
                pool.affine_select(out=G.triu[:], in_=G.triu[:], compare_op=ALU.is_gt, fill=0.0,
                                   base=0, pattern=[[1, P]], channel_multiplier=-1).then_inc(s["ident"], 1)
                for e in range(NE):
                    pool.memset(G.iota8[:, e:e + 1], float(e - NE)).then_inc(s["ident"], 1)
                pool.memset(kpad[:, 0:T], 0.0).then_inc(s["ident"], 1)
                pool.wait_ge(s["masks"], 48)
                pool.tensor_scalar(G.pen[:], mk8[:], -MASKED, MASKED, ALU.mult, ALU.add).then_inc(s["pool"], 1)
                pool.tensor_copy(tmf[:], tm8[:]).then_inc(s["tmf"], 1)
                pool.wait_ge(s["film"], 80)
                pool.tensor_scalar(G.film[:], film0[:], G.mg[:, 0:1], None, ALU.mult).then_inc(s["pool"], 1)
                pool.tensor_scalar(G.frow[:], frow0[:], G.mg[0:1, 0:1], None, ALU.mult).then_inc(s["pool"], 1)
                pool.wait_ge(s["pool"], 3)
                for k in range(2):
                    pool.tensor_scalar(G.frow[:, 256 * k:256 * k + D], G.frow[:, 256 * k:256 * k + D],
                                       1.0, None, ALU.add).then_inc(s["pool"], 1)
                pool.wait_ge(s["pool"], 5)

            @block.tensor
            def _(pe):
                pe.wait_ge(s["ident"], 1)
                pe.wait_ge(s["vec"], 16 * len(VEC))
                pe.transpose(psv[:, 0:NVEC], vrow[:], G.ident[0:NVEC, 0:NVEC]).then_inc(s["vec_ps"], 1)
                pe.wait_ge(s["tmf"], 1)
                pe.transpose(pst[:, 0:NT], tmf[:], G.ident[0:NT, 0:NT]).then_inc(s["tm_ps"], 1)

            @block.scalar
            def _(act):
                act.preload_act_table(ACT.Exp)
                act.wait_ge(s["vec_ps"], 1)
                act.activation(G.vec[:], psv[:, 0:NVEC], ACT.Copy).then_inc(s["vec_sb"], 1)
                act.wait_ge(s["tm_ps"], 1)
                act.activation(G.tmask[:], pst[:, 0:NT], ACT.Copy, scale=1.0 / H0).then_inc(s["vec_sb"], 1)
                act.wait_ge(s["vec_sb"], 1)
                at = VEC["L0_xattn_log_dt"][0]
                act.activation(G.dt[:], G.vec[:, at:at + 1], ACT.Exp).then_inc(s["exp"], 1)
                act.wait_ge(s["args"], 1)
                act.activation(kt[:, 3, :], kt[:, 0, :], ACT.Exp).then_inc(s["exp"], 1)
                act.wait_ge(s["args"], 2)
                act.activation(kt[:, 4:6, :], kt[:, 4:6, :], ACT.Sin).then_inc(s["trig"], 1)
                act.wait_ge(s["var"], 1)
                act.activation(var[:], var[:], ACT.Sqrt).then_inc(s["rms"], 1)
                act.wait_ge(s["var"], 2)
                act.activation(var2[:], var2[:], ACT.Sqrt).then_inc(s["rms"], 1)

            @block.vector
            def _(dve):
                step = Steps(dve, s["dve"])
                step.scratch = G.scratch[:]
                TT, TS = dve.tensor_tensor, dve.tensor_scalar
                dve.wait_ge(s["kin"], 64)
                dve.wait_ge(s["exp"], 1)
                TS(kt[:, 0, :], kin[:, 0, :], G.dt[:, 0:1], None, ALU.mult).then_inc(s["args"], 1)
                step.then(TS(kt[:, 1, :], kin[:, 1, :], G.dt[:, 0:1], None, ALU.mult))
                step.did(TS(kt[:, 6, :], kt[:, 1, :], 1.0 / TWO_PI, 0.25, ALU.mult, ALU.add))
                step.then(TS(kt[:, 7, :], kt[:, 1, :], 1.0 / TWO_PI, None, ALU.mult))
                step.then(TS(kt[:, 6:8, :], kt[:, 6:8, :], ROUND, None, ALU.add))
                step.then(TS(kt[:, 6:8, :], kt[:, 6:8, :], ROUND, None, ALU.subtract))
                c1 = 6.28125
                c2 = TWO_PI - c1
                th = wide(kt[:, 1:2, :], [P, 2, NS])
                step.then(dve.scalar_tensor_tensor(kt[:, 4:6, :], kt[:, 6:8, :], -c1, th, ALU.mult, ALU.add))
                step.then(dve.scalar_tensor_tensor(kt[:, 4:6, :], kt[:, 6:8, :], -c2, kt[:, 4:6, :], ALU.mult, ALU.add))
                step.then(TS(kt[:, 4, :], kt[:, 4, :], float(np.pi / 2), None, ALU.add))
                TS(kt[:, 4:6, :], kt[:, 4:6, :], float(np.float32(3.1415925)), float(np.float32(-3.1415925)),
                   ALU.min, ALU.max).then_inc(s["args"], 1)
                dve.wait_ge(s["exp"], 2)
                dve.wait_ge(s["trig"], 1)
                V = [(zV[:, b, 0, :], zV[:, b, 1, :]) for b in range(8)]
                dve.memset(zV[:, 0, 0, :], 1.0)
                dve.memset(zV[:, 0, 1, :], 0.0)
                TT(zV[:, 1, 0, :], kt[:, 3, :], kt[:, 4, :], ALU.mult)
                step.then(TT(zV[:, 1, 1, :], kt[:, 3, :], kt[:, 5, :], ALU.mult))

                def times(out, a, b, n=1):
                    t0, t1 = (ctm[:, k, 0:n, :] if n > 1 else ctm[:, k, 0, :] for k in range(2))
                    TT(t0, a[0], b[0], ALU.mult)
                    step.then(TT(t1, a[1], b[1], ALU.mult))
                    step.then(TT(out[0], t0, t1, ALU.subtract))
                    TT(t0, a[0], b[1], ALU.mult)
                    step.then(TT(t1, a[1], b[0], ALU.mult))
                    step.then(TT(out[1], t0, t1, ALU.add))

                def powers(z, a, n):
                    return tuple(z[:, a:a + n, k, :] for k in range(2))

                def same(z, n):
                    return tuple(wide(q.unsqueeze(1), [P, n, NS]) for q in z)

                z2, z4, z8, z16, z32 = ((kt[:, 6 + 2 * k, :], kt[:, 7 + 2 * k, :]) for k in range(5))
                times(z2, V[1], V[1])
                times(powers(zV, 2, 2), powers(zV, 0, 2), same(z2, 2), 2)
                times(z4, z2, z2)
                times(powers(zV, 4, 4), powers(zV, 0, 4), same(z4, 4), 4)
                times(z8, z4, z4)
                times(z16, z8, z8)
                times(z32, z16, z16)
                zm = (kt[:, 0, :], kt[:, 1, :])
                TS(zm[0], V[1][0], -1.0, None, ALU.add)
                dve.tensor_copy(zm[1], V[1][1])
                TT(ctm[:, 0, 0, :], kin[:, 0, :], kin[:, 0, :], ALU.mult)
                TT(ctm[:, 1, 0, :], kin[:, 1, :], kin[:, 1, :], ALU.mult)
                step.then(TS(kt[:, 2, :], kin[:, 1, :], -1.0, None, ALU.mult))
                step.then(TT(kt[:, 3, :], ctm[:, 0, 0, :], ctm[:, 1, 0, :], ALU.add))
                step.then(dve.reciprocal(kt[:, 3, :], kt[:, 3, :]))
                step.then(TS(kt[:, 3, :], kt[:, 3, :], 2.0, None, ALU.mult))
                prod = (kt[:, 4, :], kt[:, 5, :])
                times(prod, zm, (kin[:, 2, :], kin[:, 3, :]))
                U0 = (zU[:, 0, 0, :], zU[:, 0, 1, :])
                times((big[:, 0, 0, :], big[:, 0, 1, :]), prod, (kin[:, 0, :], kt[:, 2, :]))
                TT(U0[0], big[:, 0, 0, :], kt[:, 3, :], ALU.mult)
                step.then(TT(U0[1], big[:, 0, 1, :], kt[:, 3, :], ALU.mult))
                times((zU[:, 1, 0, :], zU[:, 1, 1, :]), U0, z8)
                times(powers(zU, 2, 2), powers(zU, 0, 2), same(z16, 2), 2)
                times(powers(zU, 4, 4), powers(zU, 0, 4), same(z32, 4), 4)
                step.then(TS(zV[:, :, 1, :], zV[:, :, 1, :], -1.0, None, ALU.mult))
                dve.wait_ge(s["ident"], 11)
                for a in range(8):
                    u = wide(zU[:, a:a + 1, :, :], [P, 8, 2, NS])
                    step.then(TT(big[:], zV[:], u, ALU.mult))
                    step.then(dve.tensor_reduce(kpad[:, T + 8 * a:T + 8 * a + 8],
                                                big[:].rearrange("p b c n -> p b (c n)"), AX.X, ALU.add))
                dve.wait_ge(s["vec_sb"], 2)
                at = VEC["L0_xattn_D_skip"][0]
                TT(kpad[:, T:T + 1], kpad[:, T:T + 1], G.vec[:, at:at + 1], ALU.add).then_inc(s["kpad"], 1)
                dve.wait_ge(s["x"], 64)
                row_statistics(dve, step, G.X, st)
                mean_and_variance(dve, step, st, G.mean[:], var2[:], tmp[:])
                TS(var[:], var2[:], EPS, None, ALU.add).then_inc(s["var"], 1)
                dve.wait_ge(s["rms"], 1)
                step.then(dve.reciprocal(G.rstd[:], var[:]))
                step.then(TT(tmp[:], G.rstd[:], G.rstd[:], ALU.mult))
                step.then(TT(var2[:], var2[:], tmp[:], ALU.mult))
                TS(var2[:], var2[:], EPS, None, ALU.add).then_inc(s["var"], 1)
                dve.wait_ge(s["rms"], 2)
                step.then(dve.reciprocal(G.rstd2[:], var2[:]))
                step.then(TT(G.XT[:], G.X[:], wide(G.mean[:].unsqueeze(2), [P, NT, D]), ALU.subtract))
                step.then(TT(G.XT[:], G.XT[:], wide(G.rstd[:].unsqueeze(2), [P, NT, D]), ALU.mult))


def first_attention(nc, C, A, G):
    scale = 1.0 / float(np.sqrt(DH0).astype(np.float32))
    with ExitStack() as ctx:
        def two(name, shape):
            return [C.sb(f"{name}{j}", shape, ctx=ctx) for j in range(2)]

        xs, cs, cb = two("xs", [P, D]), two("cs", [P, DC]), two("cb", [P, DC])
        xf, cf = two("xf", [D, P]), two("cf", [DC, P])
        qt, kb = two("qt", [P, P]), two("kb", [P, 2, H0, T])
        sc, wk_, m8 = two("sc", [P, H0, T]), two("work", [P, H0, T]), two("m8", [P, H0, 4, 8])
        dd, ee, pr = two("dd", [P, H0, T]), two("ee", [P, H0, T]), two("pr", [P, H0, T])
        rs, at, abd = two("rs", [P, 2, H0]), two("at", [P, P]), two("abd", [P, P])
        us, ct, fi = two("us", [DC, P]), two("ct", [D, P]), two("fi", [P, 256])
        xn = C.sb("xn", [P, D], ctx=ctx)
        psa = [C.ps(f"psa{j}", [P, 512], ctx) for j in range(2)]
        pss = [C.ps(f"pss{j}", [P, 512], ctx) for j in range(2)]
        psb = [C.ps(f"psb{j}", [P, 512], ctx) for j in range(2)]
        psf = [C.ps(f"psf{j}", [P, 512], ctx) for j in range(2)]
        s = {n: C.sem("att0_" + n) for n in (
            "xs", "turned", "turned_sb", "qk", "qk_sb", "scores", "scores_sb", "max", "diff", "exp",
            "attn", "attn_turned", "attn_sb", "u", "u_sb", "c", "c_sb", "film", "film_sb", "mod",
            "ctx_kept", "zero", "dve", "pool")}
        loaded = [C.sem(f"att0_ctx_loaded{j}") for j in range(2)]
        again = [C.sem(f"att0_ctx_again{j}") for j in range(2)]
        ctx_v = A["ctx_768"].rearrange("b t d -> (b t) d")

        with nc.Block() as block:
            SWEEP = (-2, 3, 29, NT + 1)

            @block.sync
            def _(sp):
                def rows(t):
                    return ctx_v[bass.ds(t * P, P), :]

                def slot(x):
                    a, c = x.by(2), x.by(-1)
                    if a.real():
                        after(sp, s["turned"], a.t - 1)
                        sp.dma_start(cs[a.j][:], rows(a.t)).then_inc(loaded[a.j], 16)
                    if c.real():
                        after(sp, s["u"], c.t - 1)
                        sp.dma_start(cb[c.j][:], rows(c.t)).then_inc(again[c.j], 16)

                sweep(sp, slot, *SWEEP)

            @block.gpsimd
            def _(pool):
                step = Steps(pool, s["pool"])
                for j in range(2):
                    for m in (kb[j], abd[j], at[j]):
                        pool.memset(m[:], 0.0).then_inc(s["zero"], 1)

                def slot(x):
                    j, a, g, c = x.j, x.by(2), x.by(3), x.by(-1)
                    if x.real():
                        pool.wait_ge(s["max"], x.t + 1)
                        pool.tensor_tensor(dd[j][:], sc[j][:], wide(m8[j][:, :, 0, 0:1], [P, H0, T]),
                                           ALU.subtract).then_inc(s["diff"], 1)
                    if g.real():
                        after(pool, s["turned"], g.t - 1)
                        pool.tensor_copy(xs[g.j][:], G.XT[:, g.t, :]).then_inc(s["xs"], 1)
                    if a.real():
                        pool.wait_ge(s["turned_sb"], a.t + 1)
                        pool.tensor_copy(G.ctxT[:, bass.ds(a.t * P, P)], cf[a.j][:]).then_inc(s["ctx_kept"], 1)
                    if c.real():
                        step.then(pool.tensor_tensor(xn[:], G.XT[:, c.t, :], wide(G.rstd2[:, bass.ds(c.t, 1)], [P, D]), ALU.mult))
                        step.then(pool.tensor_tensor(xn[:], xn[:], G.gin[:], ALU.mult))
                        step.then(pool.tensor_tensor(xn[:], xn[:], G.bin[:], ALU.add))
                        pool.wait_ge(s["film_sb"], c.t + 1)
                        step.then(pool.tensor_tensor(xn[:], xn[:], fi[c.j][:, 0:D], ALU.mult))
                        pool.tensor_tensor(G.XM[:, c.t, :], xn[:], fi[c.j][:, D:2 * D], ALU.add).then_inc(s["mod"], 1)
                        step.clear()
                        pool.wait_ge(s["mod"], c.t + 1)

                for j in range(1):
                    pool.tensor_copy(xs[j][:], G.XT[:, j, :]).then_inc(s["xs"], 1)
                sweep(pool, slot, *SWEEP)

            @block.tensor
            def _(pe):
                pe.wait_ge(s["zero"], 6)

                def slot(x):
                    a, c = x.by(2), x.by(-1)
                    if a.real():
                        j = a.j
                        pe.wait_ge(s["xs"], a.t + 1)
                        after(pe, s["qk_sb"], a.t - 1)
                        pe.transpose(psa[j][:, 0:P], xs[j][:], G.ident[:])
                        pe.wait_ge(loaded[j], (a.k + 1) * 16)
                        pe.transpose(psa[j][0:DC, P:2 * P], cs[j][:], G.ident[:]).then_inc(s["turned"], 1)
                    if c.real():
                        pe.wait_ge(s["attn"], c.t + 1)
                        after(pe, s["c_sb"], c.t - 1)
                        pe.transpose(psb[c.j][:, 0:P], at[c.j][:], G.ident[:]).then_inc(s["attn_turned"], 1)
                    if a.real():
                        pe.wait_ge(s["turned_sb"], a.t + 1)
                        pe.matmul(psa[j][:, 256:384], G.wq[:], xf[j][:], start=True, stop=True)
                        pe.matmul(psa[j][:, 384:512], G.wk[:], cf[j][:], start=True, stop=True).then_inc(s["qk"], 1)
                    if c.real():
                        pe.wait_ge(s["attn_sb"], c.t + 1)
                        pe.wait_ge(again[c.j], (c.k + 1) * 16)
                        pe.matmul(psb[c.j][0:DC, P:2 * P], cb[c.j][:], abd[c.j][:], start=True, stop=True).then_inc(s["u"], 1)
                    if a.real():
                        pe.wait_ge(s["qk_sb"], a.t + 1)
                        after(pe, s["scores_sb"], a.t - 1)
                        for b2 in range(2):
                            mm = pe.matmul(pss[j][T * b2:T * b2 + T, 0:H0 * T], qt[j][:, T * b2:T * b2 + T],
                                           kb[j][:, b2, :, :], start=True, stop=True)
                        mm.then_inc(s["scores"], 1)
                    if c.real():
                        pe.wait_ge(s["u_sb"], c.t + 1)
                        pe.matmul(psb[c.j][:, 256:384], G.wv[:], us[c.j][:], start=True, stop=True).then_inc(s["c"], 1)
                        pe.wait_ge(s["c_sb"], c.t + 1)
                        after(pe, s["film_sb"], c.t - 1)
                        pe.matmul(psf[c.j][:], ct[c.j][:], G.film[:], start=True, stop=False)
                        pe.matmul(psf[c.j][:], G.onesrow[:], G.frow[:], start=False, stop=True).then_inc(s["film"], 1)

                sweep(pe, slot, *SWEEP)

            @block.scalar
            def _(act):
                act.preload_act_table(ACT.Exp)
                copy = lambda out, in_: act.activation(out, in_, ACT.Copy)

                def slot(x):
                    a, c = x.by(2), x.by(-1)
                    if a.real():
                        j = a.j
                        act.wait_ge(s["turned"], a.t + 1)
                        after(act, s["ctx_kept"], a.t - 1)
                        copy(xf[j][:], psa[j][:, 0:P])
                        copy(cf[j][:], psa[j][0:DC, P:2 * P]).then_inc(s["turned_sb"], 1)
                    if c.real():
                        act.wait_ge(s["attn_turned"], c.t + 1)
                        copy(abd[c.j][0:T, 0:T], psb[c.j][0:T, 0:T])
                        copy(abd[c.j][T:P, T:P], psb[c.j][0:T, T:P]).then_inc(s["attn_sb"], 1)
                    if x.real():
                        act.wait_ge(s["diff"], x.t + 1)
                        act.activation(ee[x.j][:], dd[x.j][:], ACT.Exp, scale=scale).then_inc(s["exp"], 1)
                    if a.real():
                        act.wait_ge(s["qk"], a.t + 1)
                        after(act, s["scores"], a.t - 1)
                        copy(qt[j][:], psa[j][:, 256:384])
                        for h in range(H0):
                            rows = slice(DH0 * h, DH0 * h + DH0)
                            m = copy(kb[j][rows, :, h, :], psa[j][rows, 384:512].rearrange("p (b g) -> p b g", b=2))
                        m.then_inc(s["qk_sb"], 1)
                    if c.real():
                        act.wait_ge(s["u"], c.t + 1)
                        copy(us[c.j][:], psb[c.j][0:DC, P:2 * P]).then_inc(s["u_sb"], 1)
                        act.wait_ge(s["c"], c.t + 1)
                        copy(ct[c.j][:], psb[c.j][:, 256:384]).then_inc(s["c_sb"], 1)
                        act.wait_ge(s["film"], c.t + 1)
                        after(act, s["mod"], c.t - 1)
                        copy(fi[c.j][:], psf[c.j][:, 0:256])
                        copy(G.FO[:, c.t, :], psf[c.j][:, 256:512]).then_inc(s["film_sb"], 1)

                sweep(act, slot, *SWEEP)

            @block.vector
            def _(dve):
                dve.wait_ge(s["zero"], 6)
                step = Steps(dve, s["dve"])

                def select(x):
                    t, j = x.t, x.j
                    dve.wait_ge(s["scores"], t + 1)
                    dve.tensor_tensor(sc[j][:], pss[j][:, 0:H0 * T].rearrange("p (h g) -> p h g", h=H0),
                                      wide(G.pen[:, bass.ds(t, 1), :], [P, H0, T]), ALU.add).then_inc(s["scores_sb"], 1)
                    dve.wait_ge(s["scores_sb"], t + 1)
                    step.passed()
                    src = sc[j]
                    for r in range(KTOP // 8):
                        for h in range(H0):
                            mx = dve.max(m8[j][:, h, r, :], src[:, h, :])
                            if r == 0 and h == H0 - 1:
                                mx.then_inc(s["max"], 1)
                            else:
                                step.did(mx)
                        if r == 0:
                            dve.wait_ge(s["max"], t + 1)
                            step.passed()
                        else:
                            step.wait()
                        for h in range(H0):
                            step.did(dve.match_replace(wk_[j][:, h, :], m8[j][:, h, r, :], src[:, h, :], TAKEN))
                        step.wait()
                        src = wk_[j]
                    dve.wait_ge(s["exp"], t + 1)
                    flat = lambda m: m[j][:].rearrange("p h g -> p (h g)")
                    step.then(dve.scalar_tensor_tensor(flat(pr), flat(wk_), TAKEN / 3, flat(ee), ALU.is_le, ALU.mult))
                    step.then(dve.tensor_reduce(rs[j][:, 0, :], pr[j][:], AX.X, ALU.add))
                    step.then(dve.reciprocal(rs[j][:, 1, :], rs[j][:, 0, :]))
                    step.then(dve.tensor_scalar(rs[j][:, 1, :], rs[j][:, 1, :], G.tmask[:, bass.ds(t, 1)], None, ALU.mult))
                    step.then(dve.tensor_tensor(pr[j][:], pr[j][:], wide(rs[j][:, 1, :].unsqueeze(2), [P, H0, T]), ALU.mult))
                    after(dve, s["attn_turned"], t - 1)
                    dve.tensor_reduce(at[j][:, 0:T], pr[j][:].rearrange("p h g -> p g h"), AX.X, ALU.add).then_inc(s["attn"], 1)
                    step.clear()

                sweep(dve, select, 0, 2, NT, NT)


def convolution(nc, C, A, G):
    CH = 16
    NG = D // CH
    with ExitStack() as ctx:
        toe = [C.sb(f"toe{j}", [P, CH, P], ctx=ctx) for j in range(2)]
        psy = [C.ps(f"psy{j}", [P, CH, NT], ctx) for j in range(2)]
        ym = [C.sb(f"ym{j}", [P, NT, CH], ctx=ctx) for j in range(2)]
        yn = [C.sb(f"yn{j}", [P, NT, CH], ctx=ctx) for j in range(2)]
        flip = C.sb("flip", [P, P], ctx=ctx)
        psr = [C.ps(f"psr{j}", [P, TB, D], ctx) for j in range(2)]
        s = {n: C.sem("conv_" + n) for n in ("zero", "flip", "y", "y_film", "y_sum", "step", "rev", "rev_sb")}
        loaded = [C.sem(f"conv_toeplitz_loaded{j}") for j in range(2)]
        with nc.Block() as block:

            @block.sync
            def _(sp):
                sp.wait_ge(s["zero"], 2)
                for g in range(NG):
                    j = g % 2
                    if g >= 2:
                        sp.wait_ge(s["y"], g - 1)
                    for b2 in range(2):
                        src = bass.AP(G.kd.tensor, g * (CH * P) + 1, [[1, T], [P, CH], [1, T]])
                        sp.dma_start(toe[j][T * b2:T * b2 + T, :, T * b2:T * b2 + T], src).then_inc(loaded[j], 16)

            @block.gpsimd
            def _(pool):
                pool.sem_inc(s["y_sum"], 2)
                pool.memset(flip[:], 0.0).then_inc(s["flip"], 1)
                pool.wait_ge(s["flip"], 1)
                for b2 in range(2):
                    half = flip[T * b2:T * b2 + T, T * b2:T * b2 + T]
                    pool.affine_select(out=half, in_=half, compare_op=ALU.not_equal, fill=1.0, base=1 - T,
                                       pattern=[[1, T]], channel_multiplier=1).then_inc(s["flip"], 1)
                    pool.wait_ge(s["flip"], 2 + b2)
                for j in range(2):
                    pool.memset(toe[j][:], 0.0).then_inc(s["zero"], 1)
                with pool.Fori(0, NG // 2) as i:
                    for j in range(2):
                        g = i * 2 + j
                        pool.wait_ge(s["y_film"], g + 3)
                        ch = bass.ds(g * CH, CH)
                        pool.tensor_tensor(yn[j][:], ym[j][:], G.FO[:, :, bass.ds(g * CH + D, CH)], ALU.add).then_inc(s["step"], 1)
                        pool.wait_ge(s["step"], g + 1)
                        pool.tensor_tensor(G.XT[:, :, ch], G.XT[:, :, ch], yn[j][:], ALU.add).then_inc(s["y_sum"], 1)
                pool.wait_ge(s["y_sum"], NG + 2)

            @block.tensor
            def _(pe):
                pe.wait_ge(s["flip"], 3)
                with pe.Fori(0, NBLK // 2) as i:
                    for j in range(2):
                        b = i * 2 + j
                        pe.wait_ge(s["rev_sb"], b + 1)
                        pe.matmul(psr[j][:], flip[:], G.XM[:, bass.ds(b * TB, TB), :], start=True, stop=True).then_inc(s["rev"], 1)
                pe.wait_ge(s["rev_sb"], NBLK + 2)
                with pe.Fori(0, NG // 2) as i:
                    for j in range(2):
                        g = i * 2 + j
                        pe.wait_ge(loaded[j], (i + 1) * 32)
                        pe.wait_ge(s["y_film"], g + 1)
                        for c in range(CH):
                            mm = pe.matmul(psy[j][:, c, :], toe[j][:, c, :], G.XM[:, :, bass.ds(g * CH + c, 1)],
                                           start=True, stop=True)
                        mm.then_inc(s["y"], 1)

            @block.scalar
            def _(act):
                act.sem_inc(s["rev_sb"], 2)
                act.preload_act_table(ACT.Copy)
                with act.Fori(0, NBLK // 2) as i:
                    for j in range(2):
                        b = i * 2 + j
                        act.wait_ge(s["rev"], b + 1)
                        act.activation(G.XM[:, bass.ds(b * TB, TB), :], psr[j][:], ACT.Copy).then_inc(s["rev_sb"], 1)

            @block.vector
            def _(dve):
                dve.sem_inc(s["y_film"], 2)
                with dve.Fori(0, NG // 2) as i:
                    for j in range(2):
                        g = i * 2 + j
                        dve.wait_ge(s["y"], g + 1)
                        dve.wait_ge(s["y_sum"], g + 1)
                        dve.tensor_tensor(ym[j][:], psy[j][:].rearrange("p c b -> p b c"),
                                          G.FO[:, :, bass.ds(g * CH, CH)], ALU.mult).then_inc(s["y_film"], 1)


def normalise_rows(nc, C, G, tag, src, then=None):
    with ExitStack() as ctx:
        st = C.sb(tag + "st", [P, NT, 6], ctx=ctx)
        tmp = C.sb(tag + "tmp", [P, NT], ctx=ctx)
        var = C.sb(tag + "var", [P, NT], ctx=ctx)
        root = C.sb(tag + "root", [P, NT], ctx=ctx)
        s = {n: C.sem(tag + n) for n in ("var", "root", "dve")}
        with nc.Block() as block:

            @block.scalar
            def _(act):
                act.wait_ge(s["var"], 1)
                act.activation(root[:], var[:], ACT.Sqrt).then_inc(s["root"], 1)

            @block.vector
            def _(dve):
                step = Steps(dve, s["dve"])
                step.scratch = G.scratch[:]
                row_statistics(dve, step, src, st)
                mean_and_variance(dve, step, st, G.mean[:], var[:], tmp[:])
                dve.tensor_scalar(var[:], var[:], EPS, None, ALU.add).then_inc(s["var"], 1)
                dve.wait_ge(s["root"], 1)
                step.then(dve.reciprocal(root[:], root[:]))
                newton(dve, step, G.rstd[:], root[:], var[:], tmp[:])
                if then:
                    then(dve, step)


def newton(dve, step, out, r, v, tmp):
    step.then(dve.tensor_tensor(tmp, r, r, ALU.mult))
    step.then(dve.tensor_tensor(tmp, tmp, v, ALU.mult))
    step.then(dve.tensor_scalar(tmp, tmp, -0.5, 1.5, ALU.mult, ALU.add))
    step.then(dve.tensor_tensor(out, r, tmp, ALU.mult))


def first_mlp(nc, C, A, G):
    normalise_rows(nc, C, G, "ln_ffn_", G.XT)
    C.end_phase()
    gv, bv = VEC["L0_xattn_g_ffn"][0], VEC["L0_xattn_b_ffn"][0]
    b1 = VEC["L0_xattn_b1"][0]
    with ExitStack() as ctx:
        w1 = C.sb("w1", [D, HID], ctx=ctx)
        w2 = C.sb("w2", [P, HID // P, D], ctx=ctx)
        b2 = C.sb("b2", [P, D], ctx=ctx)
        xs = [C.sb(f"mlp_xs{j}", [P, TB, D], ctx=ctx) for j in range(2)]
        xf = [C.sb(f"mlp_xf{j}", [D, TB * P], ctx=ctx) for j in range(2)]
        hs = [C.sb(f"mlp_hs{j}", [P, HID // P, TB * P], ctx=ctx) for j in range(2)]
        ys = [C.sb(f"mlp_ys{j}", [P, TB, D], ctx=ctx) for j in range(2)]
        pst = C.ps("mlp_pst", [P, TB * P], ctx)
        psh = [C.ps(f"mlp_psh{c}", [P, TB * P], ctx) for c in range(4)]
        psy = [C.ps(f"mlp_psy{j}", [P, TB, D], ctx) for j in range(2)]
        s = {n: C.sem("mlp_" + n) for n in ("weights", "xs", "turned", "turned_sb", "y", "y_b", "y_sum", "dve")}
        h_ps = [C.sem(f"mlp_h_ps{c}") for c in range(4)]
        h_sb = [C.sem(f"mlp_h_sb{c}") for c in range(4)]
        with nc.Block() as block:

            @block.sync
            def _(sp):
                sp.dma_start(w1[:], A["L0_xattn_W1"]).then_inc(s["weights"], 16)
                sp.dma_start(w2[:], A["L0_xattn_W2"].rearrange("(c p) d -> p c d", p=P)).then_inc(s["weights"], 16)
                sp.dma_start(b2[:], A["L0_xattn_b2"].partition_broadcast(P)).then_inc(s["weights"], 16)

            @block.tensor
            def _(pe):
                pe.sem_inc(s["turned"], 2)
                pe.sem_inc(s["y"], 2)
                pe.wait_ge(s["weights"], 48)
                with pe.Fori(0, NBLK // 2) as i:
                    for j in range(2):
                        b = i * 2 + j
                        pe.wait_ge(s["xs"], b + 1)
                        pe.wait_ge(s["turned_sb"], b + 1)
                        for k in range(TB):
                            mm = pe.transpose(pst[:, k * P:(k + 1) * P], xs[j][:, k, :], G.ident[:])
                        mm.then_inc(s["turned"], 1)
                        pe.wait_ge(s["turned_sb"], b + 2)
                        for c in range(4):
                            pe.wait_ge(h_sb[c], b + 1)
                            pe.matmul(psh[c][:], w1[:, c * P:(c + 1) * P], xf[j][:], start=True, stop=True).then_inc(h_ps[c], 1)
                        pe.wait_ge(s["y_b"], b + 1)
                        for c in range(4):
                            pe.wait_ge(h_sb[c], b + 2)
                            for k in range(TB):
                                mm = pe.matmul(psy[j][:, k, :], hs[j][:, c, k * P:(k + 1) * P], w2[:, c, :],
                                               start=(c == 0 and k == 0), stop=(c == 3), skip_group_check=True)
                        mm.then_inc(s["y"], 1)

            @block.scalar
            def _(act):
                act.preload_act_table(ACT.Gelu)
                act.sem_inc(s["turned_sb"], 1)
                for c in range(4):
                    act.sem_inc(h_sb[c], 1)
                with act.Fori(0, NBLK // 2) as i:
                    for j in range(2):
                        b = i * 2 + j
                        act.wait_ge(s["turned"], b + 3)
                        act.activation(xf[j][:], pst[:], ACT.Identity, scale=G.vec[:, gv:gv + 1],
                                       bias=G.vec[:, bv:bv + 1]).then_inc(s["turned_sb"], 1)
                        act.wait_ge(s["y"], b + 1)
                        for c in range(4):
                            act.wait_ge(h_ps[c], b + 1)
                            act.activation(hs[j][:, c, :], psh[c][:], ACT.Gelu,
                                           bias=G.vec[:, b1 + c:b1 + c + 1]).then_inc(h_sb[c], 1)

            @block.vector
            def _(dve):
                dve.sem_inc(s["y_b"], 2)
                step = Steps(dve, s["dve"])

                def give(b, j):
                    mean = wide(G.mean[:, bass.ds(b * TB, TB)].unsqueeze(2), [P, TB, D])
                    rstd = wide(G.rstd[:, bass.ds(b * TB, TB)].unsqueeze(2), [P, TB, D])
                    step.then(dve.tensor_tensor(xs[j][:], G.XT[:, bass.ds(b * TB, TB), :], mean, ALU.subtract))
                    dve.tensor_tensor(xs[j][:], xs[j][:], rstd, ALU.mult).then_inc(s["xs"], 1)
                    step.clear()

                def take(b, j):
                    dve.wait_ge(s["y"], b + 3)
                    dve.tensor_tensor(ys[j][:], psy[j][:], wide(b2[:].unsqueeze(1), [P, TB, D]), ALU.add).then_inc(s["y_b"], 1)
                    dve.wait_ge(s["y_b"], b + 3)
                    rows = G.XT[:, bass.ds(b * TB, TB), :]
                    dve.tensor_tensor(rows, rows, ys[j][:], ALU.add).then_inc(s["y_sum"], 1)

                dve.wait_ge(s["weights"], 48)
                give(0, 0)
                give(1, 1)
                with dve.Fori(0, NBLK // 2 - 1) as i:
                    for j in range(2):
                        take(i * 2 + j, j)
                        give(i * 2 + 2 + j, j)
                take(NBLK - 2, 0)
                take(NBLK - 1, 1)
                dve.wait_ge(s["y_sum"], NBLK)


def close_first_attention(nc, C, A, G):
    with ExitStack() as ctx:
        g = C.sb("gout", [P, D], ctx=ctx)
        b = C.sb("bout", [P, D], ctx=ctx)
        loaded = C.sem("close_loaded")
        with nc.Block() as block:

            @block.sync
            def _(sp):
                sp.dma_start(g[:], A["L0_xattn_g_norm_out"].partition_broadcast(P)).then_inc(loaded, 16)
                sp.dma_start(b[:], A["L0_xattn_b_norm_out"].partition_broadcast(P)).then_inc(loaded, 16)

        def then(dve, step):
            dve.wait_ge(loaded, 32)
            full = [P, NT, D]
            XT = G.XT[:]
            step.then(dve.tensor_tensor(XT, XT, wide(G.mean[:].unsqueeze(2), full), ALU.subtract))
            step.then(dve.tensor_tensor(XT, XT, wide(G.rstd[:].unsqueeze(2), full), ALU.mult))
            step.then(dve.tensor_tensor(XT, XT, wide(g[:].unsqueeze(1), full), ALU.mult))
            step.then(dve.tensor_tensor(XT, XT, wide(b[:].unsqueeze(1), full), ALU.add))
            step.then(dve.tensor_tensor(G.X[:], G.X[:], XT, ALU.add))

        normalise_rows(nc, C, G, "ln_out_", G.XT, then)


def turn_rows(nc, C, G, tag):
    with ExitStack() as ctx:
        xs = [C.sb(f"{tag}xs{j}", [P, TB, D], ctx=ctx) for j in range(2)]
        pst = [C.ps(f"{tag}pst{j}", [P, TB * P], ctx) for j in range(2)]
        s = {n: C.sem(tag + n) for n in ("xs", "turned", "turned_sb", "dve")}
        with nc.Block() as block:

            @block.vector
            def _(dve):
                step = Steps(dve, s["dve"])
                with dve.Fori(0, NBLK // 2) as i:
                    for j in range(2):
                        b = i * 2 + j
                        dve.wait_ge(s["turned"], b + 1)
                        mean = wide(G.mean[:, bass.ds(b * TB, TB)].unsqueeze(2), [P, TB, D])
                        rstd = wide(G.rstd[:, bass.ds(b * TB, TB)].unsqueeze(2), [P, TB, D])
                        step.then(dve.tensor_tensor(xs[j][:], G.X[:, bass.ds(b * TB, TB), :], mean, ALU.subtract))
                        dve.tensor_tensor(xs[j][:], xs[j][:], rstd, ALU.mult).then_inc(s["xs"], 1)
                        step.clear()

            @block.tensor
            def _(pe):
                pe.sem_inc(s["turned"], 2)
                with pe.Fori(0, NBLK // 2) as i:
                    for j in range(2):
                        b = i * 2 + j
                        pe.wait_ge(s["xs"], b + 1)
                        pe.wait_ge(s["turned_sb"], b + 1)
                        for k in range(TB):
                            mm = pe.transpose(pst[j][:, k * P:(k + 1) * P], xs[j][:, k, :], G.ident[:])
                        mm.then_inc(s["turned"], 1)

            @block.scalar
            def _(act):
                act.preload_act_table(ACT.Copy)
                act.sem_inc(s["turned_sb"], 2)
                with act.Fori(0, NBLK // 2) as i:
                    for j in range(2):
                        b = i * 2 + j
                        act.wait_ge(s["turned"], b + 3)
                        act.activation(G.XF[:, bass.ds(b * TB * P, TB * P)], pst[j][:], ACT.Copy).then_inc(s["turned_sb"], 1)


def two_largest(dve, step, C, G, lg, w, iota):
    full = [P, NT, NE]
    e, idx = w["e"], w["idx"]
    for k in range(2):
        oh = w["oh"][k]
        step.then(dve.tensor_reduce(w["m"][:, k, :], lg, AX.X, ALU.max))
        step.then(dve.tensor_tensor(e[:], lg, wide(w["m"][:, k, :].unsqueeze(2), full), ALU.is_equal))
        step.then(dve.tensor_tensor(e[:], e[:], wide(iota[:].unsqueeze(1), full), ALU.mult))
        step.then(dve.tensor_reduce(idx[:], e[:], AX.X, ALU.min))
        step.then(dve.tensor_tensor(oh[:], wide(iota[:].unsqueeze(1), full), wide(idx[:].unsqueeze(2), full), ALU.is_equal))
        if k == 0:
            step.then(dve.scalar_tensor_tensor(lg, oh[:].rearrange("p n e -> p (n e)").rearrange("p (n e) -> p n e", e=NE), TAKEN, lg, ALU.mult, ALU.add))
    step.then(dve.tensor_tensor(w["d"][:], w["m"][:, 1, :], w["m"][:, 0, :], ALU.subtract))


def weigh(dve, step, w):
    step.then(dve.tensor_scalar(w["p"][:, 0, :], w["d"][:], 1.0, None, ALU.add))
    step.then(dve.reciprocal(w["p"][:, 0, :], w["p"][:, 0, :]))
    step.then(dve.tensor_tensor(w["p"][:, 1, :], w["d"][:], w["p"][:, 0, :], ALU.mult))
    full = [P, NT, NE]
    a, b = w["oh"]
    step.then(dve.tensor_tensor(w["e"][:], b[:], wide(w["p"][:, 1, :].unsqueeze(2), full), ALU.mult))
    step.then(dve.tensor_tensor(w["gate"], a[:], wide(w["p"][:, 0, :].unsqueeze(2), full), ALU.mult))
    step.then(dve.tensor_tensor(w["gate"], w["gate"], w["e"][:], ALU.add))


def routing_memory(C, ctx, tag, G):
    w = {"m": C.sb(tag + "m", [P, 2, NT], ctx=ctx), "e": C.sb(tag + "e", [P, NT, NE], ctx=ctx),
         "idx": C.sb(tag + "idx", [P, NT], ctx=ctx), "d": C.sb(tag + "d", [P, NT], ctx=ctx),
         "oh": [C.sb(tag + f"oh{k}", [P, NT, NE], ctx=ctx) for k in range(2)],
         "p": C.sb(tag + "p", [P, 2, NT], ctx=ctx), "gate": G.gate[:]}
    return w


def first_router(nc, C, A, G):
    rb1 = VEC["L0_ffn_rb1"][0]
    with ExitStack() as ctx:
        w1 = C.sb("rw1", [D, HID], ctx=ctx)
        w2 = C.sb("rw2", [P, 4, NE], ctx=ctx)
        b2 = C.sb("rb2", [P, NE], ctx=ctx)
        hs = [C.sb(f"rt_hs{j}", [P, 4, TB * P], ctx=ctx) for j in range(2)]
        lg = C.sb("rt_lg", [P, NT, NE], ctx=ctx)
        sel = C.sb("rt_sel", [P, NT, NE], ctx=ctx)
        run = [C.sb(f"rt_run{k}", [P, NT, NE], ctx=ctx) for k in range(2)]
        w = routing_memory(C, ctx, "rt_", G)
        psh = [C.ps(f"rt_psh{c}", [P, TB * P], ctx) for c in range(4)]
        psl = [C.ps(f"rt_psl{j}", [P, TB, NE], ctx) for j in range(2)]
        psp = C.ps("rt_psp", [P, NT, NE], ctx)
        s = {n: C.sem("rt_" + n) for n in ("weights", "logits", "logits_sb", "d", "exp", "sel", "pos", "dve")}
        h_ps = [C.sem(f"rt_h_ps{c}") for c in range(4)]
        h_sb = [C.sem(f"rt_h_sb{c}") for c in range(4)]
        with nc.Block() as block:

            @block.sync
            def _(sp):
                sp.dma_start(w1[:], A["L0_ffn_rw1"]).then_inc(s["weights"], 16)
                sp.dma_start(w2[:], A["L0_ffn_rw2"].rearrange("(c p) e -> p c e", p=P)).then_inc(s["weights"], 16)
                sp.dma_start(b2[:], A["L0_ffn_rb2"].partition_broadcast(P)).then_inc(s["weights"], 16)

            @block.tensor
            def _(pe):
                pe.sem_inc(s["logits"], 2)
                pe.wait_ge(s["weights"], 48)
                with pe.Fori(0, NBLK // 2) as i:
                    for j in range(2):
                        b = i * 2 + j
                        for c in range(4):
                            pe.wait_ge(h_sb[c], b + 1)
                            pe.matmul(psh[c][:], w1[:, c * P:(c + 1) * P], G.XF[:, bass.ds(b * TB * P, TB * P)],
                                      start=True, stop=True).then_inc(h_ps[c], 1)
                        pe.wait_ge(s["logits_sb"], b + 1)
                        for c in range(4):
                            pe.wait_ge(h_sb[c], b + 2)
                            for k in range(TB):
                                mm = pe.matmul(psl[j][:, k, :], hs[j][:, c, k * P:(k + 1) * P], w2[:, c, :],
                                               start=(c == 0 and k == 0), stop=(c == 3), skip_group_check=True)
                        mm.then_inc(s["logits"], 1)
                pe.wait_ge(s["sel"], 1)
                pe.matmul(psp[:], G.triu[:], sel[:], start=True, stop=False)
                pe.matmul(psp[:], G.ones[:], run[1][:], start=False, stop=True).then_inc(s["pos"], 1)

            @block.scalar
            def _(act):
                act.preload_act_table(ACT.Exp)
                for c in range(4):
                    act.sem_inc(h_sb[c], 1)
                with act.Fori(0, NBLK // 2) as i:
                    for j in range(2):
                        b = i * 2 + j
                        act.wait_ge(s["logits"], b + 1)
                        for c in range(4):
                            act.wait_ge(h_ps[c], b + 1)
                            act.activation(hs[j][:, c, :], psh[c][:], ACT.Relu,
                                           bias=G.vec[:, rb1 + c:rb1 + c + 1]).then_inc(h_sb[c], 1)
                act.wait_ge(s["d"], 1)
                act.activation(w["d"][:], w["d"][:], ACT.Exp).then_inc(s["exp"], 1)

            @block.vector
            def _(dve):
                dve.sem_inc(s["logits_sb"], 2)
                step = Steps(dve, s["dve"])
                dve.wait_ge(s["weights"], 48)
                with dve.Fori(0, NBLK // 2) as i:
                    for j in range(2):
                        b = i * 2 + j
                        dve.wait_ge(s["logits"], b + 3)
                        dve.tensor_tensor(lg[:, bass.ds(b * TB, TB), :], psl[j][:], wide(b2[:].unsqueeze(1), [P, TB, NE]),
                                          ALU.add).then_inc(s["logits_sb"], 1)
                dve.wait_ge(s["logits_sb"], NBLK + 2)
                two_largest(dve, step, C, G, lg[:], w, G.iota8)
                dve.sem_inc(s["d"], 1)
                step.then(dve.tensor_tensor(sel[:], w["oh"][0][:], w["oh"][1][:], ALU.add))
                dve.memset(run[0][:, 0, :], 0.0)
                step.then(dve.tensor_copy(run[0][:, 1:NT, :], sel[:, 0:NT - 1, :]))
                src, k = 0, 1
                while k < NT:
                    dve.tensor_copy(run[1 - src][:, 0:k, :], run[src][:, 0:k, :])
                    step.then(dve.tensor_tensor(run[1 - src][:, k:NT, :], run[src][:, k:NT, :], run[src][:, 0:NT - k, :], ALU.add))
                    src, k = 1 - src, 2 * k
                assert src == 1
                dve.sem_inc(s["sel"], 1)
                dve.wait_ge(s["exp"], 1)
                weigh(dve, step, w)
                dve.wait_ge(s["pos"], 1)
                step.then(dve.tensor_scalar(w["e"][:], psp[:], float(CAP), None, ALU.is_lt))
                step.then(dve.tensor_tensor(G.gate[:], G.gate[:], w["e"][:], ALU.mult))


def add_gated_biases(nc, C, A, G, tag, name):
    with ExitStack() as ctx:
        gs = [C.sb(f"{tag}gs{j}", [P, TB, 32], ctx=ctx) for j in range(2)]
        gt = [C.sb(f"{tag}gt{j}", [P, P], ctx=ctx) for j in range(2)]
        bd = C.sb(tag + "bd", [P, TB, D], ctx=ctx)
        pst = [C.ps(f"{tag}pst{j}", [P, P], ctx) for j in range(2)]
        psy = [C.ps(f"{tag}psy{j}", [P, TB, D], ctx) for j in range(2)]
        s = {n: C.sem(tag + n) for n in ("zero", "loaded", "gs", "turned", "turned_sb", "y", "x")}
        with nc.Block() as block:

            @block.gpsimd
            def _(pool):
                pool.memset(bd[:], 0.0).then_inc(s["zero"], 1)
                for j in range(2):
                    pool.memset(gs[j][:], 0.0).then_inc(s["zero"], 1)

            @block.sync
            def _(sp):
                sp.wait_ge(s["zero"], 1)
                for k in range(TB):
                    sp.dma_start(bd[32 * k:32 * k + NE, k, :], A[name]).then_inc(s["loaded"], 16)

            @block.tensor
            def _(pe):
                pe.sem_inc(s["turned"], 2)
                pe.wait_ge(s["loaded"], 64)
                with pe.Fori(0, NBLK // 2) as i:
                    for j in range(2):
                        b = i * 2 + j
                        pe.wait_ge(s["gs"], b + 1)
                        pe.transpose(pst[j][:], gs[j][:].rearrange("p k e -> p (k e)"), G.ident[:]).then_inc(s["turned"], 1)
                        pe.wait_ge(s["turned_sb"], b + 1)
                        pe.wait_ge(s["x"], b + 1)
                        pe.matmul(psy[j][:], gt[j][:], bd[:], start=True, stop=True).then_inc(s["y"], 1)

            @block.scalar
            def _(act):
                with act.Fori(0, NBLK // 2) as i:
                    for j in range(2):
                        b = i * 2 + j
                        act.wait_ge(s["turned"], b + 3)
                        act.activation(gt[j][:], pst[j][:], ACT.Copy).then_inc(s["turned_sb"], 1)

            @block.vector
            def _(dve):
                dve.sem_inc(s["x"], 2)
                dve.wait_ge(s["zero"], 3)
                with dve.Fori(0, NBLK // 2) as i:
                    for j in range(2):
                        b = i * 2 + j
                        dve.wait_ge(s["turned"], b + 1)
                        dve.tensor_copy(gs[j][:, :, 0:NE], G.gate[:, bass.ds(b * TB, TB), :]).then_inc(s["gs"], 1)
                        dve.wait_ge(s["y"], b + 1)
                        rows = G.X[:, bass.ds(b * TB, TB), :]
                        dve.tensor_tensor(rows, rows, psy[j][:], ALU.add).then_inc(s["x"], 1)


def first_experts(nc, C, A, G):
    eb1 = VEC["L0_ffn_eb1"][0]
    with ExitStack() as ctx:
        w1 = [C.sb(f"ew1{j}", [D, HID], ctx=ctx) for j in range(2)]
        w2 = [C.sb(f"ew2{j}", [P, 4, D], ctx=ctx) for j in range(2)]
        hs = [C.sb(f"ex_hs{j}", [P, 4, TB * P], ctx=ctx) for j in range(2)]
        psh = [C.ps(f"ex_psh{c}", [P, TB * P], ctx) for c in range(4)]
        psy = [C.ps(f"ex_psy{j}", [P, TB, D], ctx) for j in range(2)]
        s = {n: C.sem("ex_" + n) for n in ("y", "y_sum")}
        h_ps = [C.sem(f"ex_h_ps{c}") for c in range(4)]
        h_sb = [C.sem(f"ex_h_sb{c}") for c in range(4)]
        loaded = [C.sem(f"ex_weights{j}") for j in range(2)]
        with nc.Block() as block:

            @block.sync
            def _(sp):
                for e in range(NE):
                    j = e % 2
                    if e >= 2:
                        sp.wait_ge(s["y"], 2 + NBLK * (e - 1))
                    sp.dma_start(w1[j][:], A["L0_ffn_ew1"][e]).then_inc(loaded[j], 16)
                    sp.dma_start(w2[j][:], A["L0_ffn_ew2"][e].rearrange("(c p) d -> p c d", p=P)).then_inc(loaded[j], 16)

            @block.tensor
            def _(pe):
                pe.sem_inc(s["y"], 2)
                for e in range(NE):
                        ej = e % 2
                        pe.wait_ge(loaded[ej], (e // 2 + 1) * 32)
                        with pe.Fori(0, NBLK // 2) as i:
                            for j in range(2):
                                b = i * 2 + j
                                n = i * 2 + (e * NBLK + j)
                                for c in range(4):
                                    pe.wait_ge(h_sb[c], n + 1)
                                    pe.matmul(psh[c][:], w1[ej][:, c * P:(c + 1) * P], G.XF[:, bass.ds(b * TB * P, TB * P)],
                                              start=True, stop=True).then_inc(h_ps[c], 1)
                                pe.wait_ge(s["y_sum"], n + 1)
                                for c in range(4):
                                    pe.wait_ge(h_sb[c], n + 2)
                                    for k in range(TB):
                                        mm = pe.matmul(psy[j][:, k, :], hs[j][:, c, k * P:(k + 1) * P], w2[ej][:, c, :],
                                                       start=(c == 0 and k == 0), stop=(c == 3), skip_group_check=True)
                                mm.then_inc(s["y"], 1)

            @block.scalar
            def _(act):
                act.preload_act_table(ACT.Relu)
                for c in range(4):
                    act.sem_inc(h_sb[c], 1)
                for e in range(NE):
                    with act.Fori(0, NBLK // 2) as i:
                        for j in range(2):
                            n = i * 2 + (e * NBLK + j)
                            act.wait_ge(s["y"], n + 1)
                            for c in range(4):
                                act.wait_ge(h_ps[c], n + 1)
                                k = eb1 + 4 * e + c
                                act.activation(hs[j][:, c, :], psh[c][:], ACT.Relu, bias=G.vec[:, k:k + 1]).then_inc(h_sb[c], 1)

            @block.vector
            def _(dve):
                dve.sem_inc(s["y_sum"], 2)
                for e in range(NE):
                    with dve.Fori(0, NBLK // 2) as i:
                        for j in range(2):
                            b = i * 2 + j
                            n = i * 2 + (e * NBLK + j)
                            dve.wait_ge(s["y"], n + 3)
                            if e > 0:
                                dve.wait_ge(s["y_sum"], n + 2 - NBLK + 1)
                            for k in range(TB):
                                row = G.X[:, bass.ds(b * TB + k, 1), :].rearrange("p a d -> p (a d)")
                                gate = G.gate[:, bass.ds(b * TB + k, 1), e:e + 1].rearrange("p a e -> p (a e)")
                                st = dve.scalar_tensor_tensor(row, psy[j][:, k, :], gate, row, ALU.mult, ALU.add)
                            st.then_inc(s["y_sum"], 1)


def second_attention(nc, C, A, G):
    bqi, bki, bvi = (VEC["L1_xattn_" + n][0] for n in ("bq", "bk", "bv"))
    HG = 4
    with ExitStack() as ctx:
        def two(name, shape):
            return [C.sb(f"a1_{name}{j}", shape, ctx=ctx) for j in range(2)]

        wq, wk, wv, wo = (C.sb("a1_w" + n, [k, D], ctx=ctx) for n, k in (("q", D), ("k", DC), ("v", DC), ("o", D)))
        bo = C.sb("a1_bo", [P, D], ctx=ctx)
        sca = C.sb("a1_scale", [P, 1], ctx=ctx)
        bqs = C.sb("a1_bqs", [P, 1], ctx=ctx)
        m4 = C.sb("a1_m4", [P, HG], ctx=ctx)
        bk4 = C.sb("a1_bk4", [P, HG], ctx=ctx)
        c2, vb = two("c2", [DC, 2, 2, T]), two("vb", [P, 2, H1 // 2, 2, DH1 + 1])
        qt, kb = two("qt", [P, P]), two("kb", [P, 2, HG, T])
        mx, dd, pp = two("mx", [P, H1]), two("dd", [P, H1, T]), two("pp", [P, H1, T])
        pt = two("pt", [P, H1 // 2, P])
        rc, oo, of = two("rc", [P, H1]), two("oo", [P, H1, DH1]), two("of", [P, P])
        psx = C.ps("a1_psx", [P, 512], ctx)
        psv = C.ps("a1_psv", [P, 2, D], ctx)
        pss = C.ps("a1_pss", [P, 2, 512], ctx)
        psp = [C.ps(f"a1_psp{k}", [P, 4, P], ctx) for k in range(2)]
        pso = C.ps("a1_pso", [P, H1 // 2, 2, DH1 + 1], ctx)
        psz = C.ps("a1_psz", [P, 512], ctx)
        s = {n: C.sem("a1_" + n) for n in (
            "weights", "ready", "zero", "c2", "qkv", "qkv_sb", "scores", "scores_sb", "diff", "exp", "turned", "turned_sb",
            "o", "o_sb", "o_turned", "of", "y", "x", "dve", "pool")}
        with nc.Block() as block:

            @block.sync
            def _(sp):
                for dst, name in ((wq, "Wq"), (wk, "Wk"), (wv, "Wv"), (wo, "Wo")):
                    sp.dma_start(dst[:], A["L1_xattn_" + name]).then_inc(s["weights"], 16)
                sp.dma_start(bo[:], A["L1_xattn_bo"].partition_broadcast(P)).then_inc(s["weights"], 16)
                sp.dma_start(sca[:], A["L1_xattn_scale"].partition_broadcast(P)).then_inc(s["weights"], 16)

            @block.gpsimd
            def _(pool):
                step = Steps(pool, s["pool"])
                step.then(pool.memset(m4[:], 1.0))
                for g in range(4):
                    rows = m4[32 * g:32 * g + 32, :]
                    step.then(pool.affine_select(out=rows, in_=rows, compare_op=ALU.is_ge, fill=0.0,
                                                 base=0, pattern=[[-DH1, HG]], channel_multiplier=1))
                    step.then(pool.affine_select(out=rows, in_=rows, compare_op=ALU.is_ge, fill=0.0,
                                                 base=DH1 - 1, pattern=[[DH1, HG]], channel_multiplier=-1))
                for j in range(2):
                    step.did(pool.memset(vb[j][:], 0.0))
                step.wait()
                for j in range(2):
                    step.did(pool.memset(vb[j][0:T, :, :, 0, DH1:DH1 + 1], 1.0))
                    step.did(pool.memset(vb[j][T:P, :, :, 1, DH1:DH1 + 1], 1.0))
                step.wait()
                pool.sem_inc(s["zero"], 1)
                with pool.Fori(0, NT // 2) as i:
                    for j in range(2):
                        t = i * 2 + j
                        pool.wait_ge(s["qkv"], t + 1)
                        src = G.ctxT[:, bass.ds(t * P, P)].rearrange("p (b k) -> p b k", b=2)
                        pool.tensor_copy(c2[j][:, :, 0, :], src)
                        pool.tensor_copy(c2[j][:, :, 1, :], src).then_inc(s["c2"], 1)

            @block.tensor
            def _(pe):
                pe.sem_inc(s["qkv"], 2)
                pe.wait_ge(s["weights"], 96)

                def a(t, j):
                    tok = bass.ds(t * P, P)
                    pe.wait_ge(s["qkv_sb"], t + 1)
                    pe.wait_ge(s["c2"], t + 1)
                    pe.matmul(psx[:, 0:P], wq[:], G.XF[:, tok], start=True, stop=True)
                    pe.matmul(psx[:, P:2 * P], wk[:], G.ctxT[:, tok], start=True, stop=True)
                    for b in range(2):
                        mm = pe.matmul(psv[:, b, :], c2[j][:, b, :, :], wv[:], start=True, stop=True)
                    mm.then_inc(s["qkv"], 1)
                    pe.wait_ge(s["qkv_sb"], t + 2)
                    for half in range(2):
                        pe.wait_ge(s["scores_sb"], t * 2 + half + 1)
                        for b in range(2):
                            for g in range(2):
                                rows = slice(64 * half + 32 * g, 64 * half + 32 * g + 32)
                                mm = pe.matmul(pss[T * b:T * b + T, g, 0:HG * T], qt[j][rows, T * b:T * b + T],
                                               kb[j][rows, b, :, :], start=True, stop=True)
                        mm.then_inc(s["scores"], 1)

                def b(t, j):
                    pe.wait_ge(s["exp"], t + 1)
                    for half in range(2):
                        pe.wait_ge(s["turned_sb"], t * 2 + half + 1)
                        for k in range(4):
                            h = 8 * half + 2 * k
                            mm = pe.transpose(psp[half][:, k, :], pp[j][:, h:h + 2, :].rearrange("p h k -> p (h k)"), G.ident[:])
                        mm.then_inc(s["turned"], 1)
                    pe.wait_ge(s["turned_sb"], t * 2 + 4)
                    pe.wait_ge(s["o_sb"], t + 1)
                    for bb in range(2):
                        for k in range(H1 // 2):
                            mm = pe.matmul(pso[T * bb:T * bb + T, k, :, :], pt[j][:, k, T * bb:T * bb + T],
                                           vb[j][:, bb, k, :, :], start=True, stop=True)
                    mm.then_inc(s["o"], 1)
                    pe.wait_ge(s["o_sb"], t + 2)
                    pe.wait_ge(s["x"], t + 1)
                    pe.transpose(psz[:, 0:P], oo[j][:].rearrange("p h d -> p (h d)"), G.ident[:]).then_inc(s["o_turned"], 1)
                    pe.wait_ge(s["of"], t + 1)
                    pe.matmul(psz[:, P:2 * P], of[j][:], wo[:], start=True, stop=True).then_inc(s["y"], 1)

                a(0, 0)
                with pe.Fori(0, NT // 2 - 1) as i:
                    a(i * 2 + 1, 1)
                    b(i * 2, 0)
                    a(i * 2 + 2, 0)
                    b(i * 2 + 1, 1)
                a(NT - 1, 1)
                b(NT - 2, 0)
                b(NT - 1, 1)

            @block.scalar
            def _(act):
                act.preload_act_table(ACT.Exp)
                act.sem_inc(s["qkv_sb"], 1)
                act.sem_inc(s["turned_sb"], 2)
                act.wait_ge(s["ready"], 1)
                act.wait_ge(s["zero"], 1)
                ident = ACT.Identity

                def a(t, j):
                    act.wait_ge(s["qkv"], t + 3)
                    act.activation(qt[j][:], psx[:, 0:P], ident, scale=sca[:, 0:1], bias=bqs[:, 0:1])
                    k = psx[:, P:2 * P].rearrange("p (b k) -> p b k", b=2)
                    for h in range(HG):
                        act.activation(kb[j][:, :, h, :], k, ident, scale=m4[:, h:h + 1], bias=bk4[:, h:h + 1])
                    v = psv[:].rearrange("p b (k c d) -> p b k c d", c=2, d=DH1)
                    for b in range(2):
                        act.activation(vb[j][0:T, b, :, 0, 0:DH1], v[0:T, b, :, 0, :], ACT.Copy)
                        c = act.activation(vb[j][T:P, b, :, 1, 0:DH1], v[T:P, b, :, 1, :], ACT.Copy)
                    c.then_inc(s["qkv_sb"], 1)
                    act.wait_ge(s["diff"], t + 1)
                    act.activation(pp[j][:], dd[j][:], ACT.Exp).then_inc(s["exp"], 1)

                def b(t, j):
                    for half in range(2):
                        act.wait_ge(s["turned"], t * 2 + half + 1)
                        act.activation(pt[j][:, 4 * half:4 * half + 4, :], psp[half][:], ACT.Copy).then_inc(s["turned_sb"], 1)
                    act.wait_ge(s["o_turned"], t + 1)
                    act.activation(of[j][:], psz[:, 0:P], ident, bias=G.vec[:, bvi:bvi + 1]).then_inc(s["of"], 1)

                a(0, 0)
                with act.Fori(0, NT // 2 - 1) as i:
                    a(i * 2 + 1, 1)
                    b(i * 2, 0)
                    a(i * 2 + 2, 0)
                    b(i * 2 + 1, 1)
                a(NT - 1, 1)
                b(NT - 2, 0)
                b(NT - 1, 1)

            @block.vector
            def _(dve):
                dve.sem_inc(s["scores_sb"], 1)
                dve.sem_inc(s["o_sb"], 1)
                dve.sem_inc(s["x"], 1)
                step = Steps(dve, s["dve"])
                dve.wait_ge(s["weights"], 96)
                dve.wait_ge(s["zero"], 1)
                dve.tensor_scalar(bqs[:], G.vec[:, bqi:bqi + 1], sca[:, 0:1], None, ALU.mult)
                dve.tensor_scalar(bk4[:], m4[:], G.vec[:, bki:bki + 1], None, ALU.mult)
                step.then(dve.tensor_tensor(G.X[:], G.X[:], wide(bo[:].unsqueeze(1), [P, NT, D]), ALU.add))
                dve.sem_inc(s["ready"], 1)
                step.clear()

                def a(t, j):
                    for half in range(2):
                        dve.wait_ge(s["scores"], t * 2 + half + 1)
                        heads = slice(8 * half, 8 * half + 8)
                        src = pss[:, :, 0:HG * T].rearrange("p g (h k) -> p g h k", h=HG)
                        step.then(dve.tensor_reduce(mx[j][:, heads].rearrange("p (g h) -> p g h", g=2), src, AX.X, ALU.max))
                        m = wide(mx[j][:, heads].rearrange("p (g h) -> p g h", g=2).unsqueeze(3), [P, 2, HG, T])
                        out = dd[j][:, heads, :].rearrange("p (g h) k -> p g h k", g=2)
                        dve.tensor_tensor(out, src, m, ALU.subtract).then_inc(s["scores_sb"], 1)
                        dve.wait_ge(s["scores_sb"], t * 2 + half + 2)
                        step.passed()
                    step.clear()
                    dve.sem_inc(s["diff"], 1)

                def b(t, j):
                    dve.wait_ge(s["o"], t + 1)
                    o = pso[:].rearrange("p k c d -> p (k c) d")
                    step.then(dve.reciprocal(rc[j][:], o[:, :, DH1]))
                    dve.tensor_tensor(oo[j][:], o[:, :, 0:DH1], wide(rc[j][:].unsqueeze(2), [P, H1, DH1]), ALU.mult).then_inc(s["o_sb"], 1)
                    dve.wait_ge(s["y"], t + 1)
                    row = G.X[:, t, :]
                    dve.tensor_tensor(row, row, psz[:, P:2 * P], ALU.add).then_inc(s["x"], 1)
                    step.clear()

                a(0, 0)
                with dve.Fori(0, NT // 2 - 1) as i:
                    a(i * 2 + 1, 1)
                    b(i * 2, 0)
                    a(i * 2 + 2, 0)
                    b(i * 2 + 1, 1)
                a(NT - 1, 1)
                b(NT - 2, 0)
                b(NT - 1, 1)


def second_router(nc, C, A, G):
    with ExitStack() as ctx:
        wg = C.sb("g1_wg", [NE, D], ctx=ctx)
        wgt = C.sb("g1_wgt", [D, NE], ctx=ctx)
        xl = [C.sb(f"g1_xl{j}", [D, TB * P], ctx=ctx) for j in range(2)]
        lg = C.sb("g1_lg", [P, NT, NE], ctx=ctx)
        w = routing_memory(C, ctx, "g1_", G)
        psw = C.ps("g1_psw", [P, NE], ctx)
        psl = [C.ps(f"g1_psl{j}", [P, TB, NE], ctx) for j in range(2)]
        s = {n: C.sem("g1_" + n) for n in ("wg", "wg_ps", "wg_sb", "xl", "logits", "logits_sb", "d", "exp", "dve")}
        with nc.Block() as block:

            @block.sync
            def _(sp):
                sp.dma_start(wg[:], A["L1_ffn_Wg"]).then_inc(s["wg"], 16)

            @block.tensor
            def _(pe):
                pe.sem_inc(s["logits"], 2)
                pe.wait_ge(s["wg"], 16)
                pe.transpose(psw[:], wg[:], G.ident[0:NE, 0:NE]).then_inc(s["wg_ps"], 1)
                pe.wait_ge(s["wg_sb"], 1)
                with pe.Fori(0, NBLK // 2) as i:
                    for j in range(2):
                        b = i * 2 + j
                        pe.wait_ge(s["xl"], b + 1)
                        pe.wait_ge(s["logits_sb"], b + 1)
                        for k in range(TB):
                            mm = pe.matmul(psl[j][:, k, :], xl[j][:, k * P:(k + 1) * P], wgt[:], start=True, stop=True)
                        mm.then_inc(s["logits"], 1)

            @block.scalar
            def _(act):
                act.preload_act_table(ACT.Exp)
                act.wait_ge(s["wg_ps"], 1)
                act.activation(wgt[:], psw[:], ACT.Copy).then_inc(s["wg_sb"], 1)
                with act.Fori(0, NBLK // 2) as i:
                    for j in range(2):
                        b = i * 2 + j
                        act.wait_ge(s["logits"], b + 1)
                        act.activation(xl[j][:], G.XF[:, bass.ds(b * TB * P, TB * P)], ACT.Copy).then_inc(s["xl"], 1)
                act.wait_ge(s["d"], 1)
                act.activation(w["d"][:], w["d"][:], ACT.Exp).then_inc(s["exp"], 1)

            @block.vector
            def _(dve):
                dve.sem_inc(s["logits_sb"], 2)
                step = Steps(dve, s["dve"])
                with dve.Fori(0, NBLK // 2) as i:
                    for j in range(2):
                        b = i * 2 + j
                        dve.wait_ge(s["logits"], b + 3)
                        dve.tensor_copy(lg[:, bass.ds(b * TB, TB), :], psl[j][:]).then_inc(s["logits_sb"], 1)
                dve.wait_ge(s["logits_sb"], NBLK + 2)
                two_largest(dve, step, C, G, lg[:], w, G.iota8)
                dve.sem_inc(s["d"], 1)
                dve.wait_ge(s["exp"], 1)
                weigh(dve, step, w)


def second_experts(nc, C, A, G):
    b1i, b3i = VEC["L1_ffn_b1"][0], VEC["L1_ffn_b3"][0]
    NC = HE // P
    with ExitStack() as ctx:
        def two(name, shape):
            return [C.sb(f"e1_{name}{j}", shape, ctx=ctx) for j in range(2)]

        wr = two("wr", [P, 2, NC, D])
        w2r = two("w2r", [D, HE])
        br = two("br", [P, 2, NC, R])
        b2r = two("b2r", [D, R])
        ar = two("ar", [R, 2, D])
        a2 = two("a2", [R, HE])
        bt = two("bt", [R, 2 * NC + 1, P])
        w13 = two("w13", [D, 2, NC, P])
        w2 = two("w2", [P, NC, D])
        sg = two("sg", [P, NC, TB * P])
        hh = two("hh", [P, NC, TB * P])
        h3 = two("h3", [P, NC, TB * P])
        psb = C.ps("e1_psb", [P, 512], ctx)
        psb2 = C.ps("e1_psb2", [P, 512], ctx)
        psh = [[C.ps(f"e1_ps{m}{c}", [P, TB * P], ctx) for c in range(NC)] for m in (1, 3)]
        psy = [C.ps(f"e1_psy{j}", [P, TB, D], ctx) for j in range(2)]
        s = {n: C.sem("e1_" + n) for n in ("bt", "bt_sb", "w13", "w13_sb", "w2", "w2_sb", "hh", "y", "y_sum")}
        loaded = [C.sem(f"e1_weights{j}") for j in range(2)]
        h_ps = [[C.sem(f"e1_h{m}_ps{c}") for c in range(NC)] for m in (1, 3)]
        silu = [C.sem(f"e1_silu{c}") for c in range(NC)]
        h3_sb = [C.sem(f"e1_h3_sb{c}") for c in range(NC)]
        hh_sb = [C.sem(f"e1_hh{c}") for c in range(NC)]
        with nc.Block() as block:

            @block.sync
            def _(sp):
                for e in range(NE):
                    j = e % 2
                    if e >= 2:
                        sp.wait_ge(s["w2"], e - 1)
                    for m, (W, Bn, An) in enumerate((("W1", "B1", "A1"), ("W3", "B3", "A3"))):
                        sp.dma_start(wr[j][:, m, :, :], A["L1_ffn_" + W][e].rearrange("(c p) d -> p c d", p=P)).then_inc(loaded[j], 16)
                        sp.dma_start(br[j][:, m, :, :], A["L1_ffn_" + Bn][e].rearrange("(c p) r -> p c r", p=P)).then_inc(loaded[j], 16)
                        sp.dma_start(ar[j][:, m, :], A["L1_ffn_" + An][e]).then_inc(loaded[j], 16)
                    sp.dma_start(w2r[j][:], A["L1_ffn_W2"][e]).then_inc(loaded[j], 16)
                    sp.dma_start(b2r[j][:], A["L1_ffn_B2"][e]).then_inc(loaded[j], 16)
                    sp.dma_start(a2[j][:], A["L1_ffn_A2"][e]).then_inc(loaded[j], 16)

            @block.tensor
            def _(pe):
                pe.sem_inc(s["y"], 2)

                def fold(e, j):
                    pe.wait_ge(loaded[j], 144 * (e // 2 + 1))
                    if e:
                        pe.wait_ge(s["w2_sb"], e)
                    for m in range(2):
                        for c in range(NC):
                            k = m * NC + c
                            pe.transpose(psb[0:R, k * P:(k + 1) * P], br[j][:, m, c, :], G.ident[:])
                    pe.transpose(psb2[0:R, 0:P], b2r[j][:], G.ident[:]).then_inc(s["bt"], 1)
                    pe.wait_ge(s["bt_sb"], e + 1)
                    for m in range(2):
                        for c in range(NC):
                            k = m * NC + c
                            o = psb[:, k * P:(k + 1) * P]
                            pe.matmul(o, wr[j][:, m, c, :], G.ident[:], start=True, stop=False)
                            mm = pe.matmul(o, ar[j][:, m, :], bt[j][:, k, :], start=False, stop=True)
                    mm.then_inc(s["w13"], 1)
                    pe.wait_ge(s["w13_sb"], e + 1)
                    for c in range(NC):
                        o = psb[:, c * D:(c + 1) * D]
                        pe.matmul(o, w2r[j][:, c * P:(c + 1) * P], G.ident[:], start=True, stop=False)
                        mm = pe.matmul(o, a2[j][:, c * P:(c + 1) * P], bt[j][:, 2 * NC, :], start=False, stop=True)
                    mm.then_inc(s["w2"], 1)

                for e in range(NE):
                    ej = e % 2
                    fold(e, ej)
                    pe.wait_ge(s["w2_sb"], e + 1)
                    with pe.Fori(0, NBLK // 2) as i:
                        for j in range(2):
                            b = i * 2 + j
                            n = i * 2 + (e * NBLK + j)
                            x = G.XF[:, bass.ds(b * TB * P, TB * P)]
                            for c in range(NC):
                                for m in range(2):
                                    pe.wait_ge(hh_sb[c], n + 1)
                                    pe.matmul(psh[m][c][:], w13[ej][:, m, c, :], x, start=True, stop=True).then_inc(h_ps[m][c], 1)
                            pe.wait_ge(s["y_sum"], n + 1)
                            for c in range(NC):
                                pe.wait_ge(hh_sb[c], n + 2)
                                for k in range(TB):
                                    mm = pe.matmul(psy[j][:, k, :], hh[j][:, c, k * P:(k + 1) * P], w2[ej][:, c, :],
                                                   start=(c == 0 and k == 0), stop=(c == NC - 1), skip_group_check=True)
                            mm.then_inc(s["y"], 1)

            @block.scalar
            def _(act):
                act.preload_act_table(ACT.Silu)
                for e in range(NE):
                    ej = e % 2
                    act.wait_ge(s["bt"], e + 1)
                    act.activation(bt[ej][:, 0:2 * NC, :], psb[0:R, :].rearrange("r (k p) -> r k p", p=P), ACT.Copy)
                    act.activation(bt[ej][:, 2 * NC, :], psb2[0:R, 0:P], ACT.Copy).then_inc(s["bt_sb"], 1)
                    act.wait_ge(s["w13"], e + 1)
                    act.activation(w13[ej][:].rearrange("d m c p -> d (m c p)"), psb[:], ACT.Copy).then_inc(s["w13_sb"], 1)
                    act.wait_ge(s["w2"], e + 1)
                    act.activation(w2[ej][:].rearrange("p c d -> p (c d)"), psb[:, 0:NC * D], ACT.Copy).then_inc(s["w2_sb"], 1)
                    with act.Fori(0, NBLK // 2) as i:
                        for j in range(2):
                            n = i * 2 + (e * NBLK + j)
                            for c in range(NC):
                                k = b1i + NC * e + c
                                act.wait_ge(h_ps[0][c], n + 1)
                                act.activation(sg[j][:, c, :], psh[0][c][:], ACT.Silu, bias=G.vec[:, k:k + 1]).then_inc(silu[c], 1)

            @block.vector
            def _(dve):
                for c in range(NC):
                    dve.sem_inc(hh_sb[c], 1)
                dve.sem_inc(s["y_sum"], 2)

                def take(b, n, e, j):
                    dve.wait_ge(s["y"], n + 3)
                    if e > 0:
                        dve.wait_ge(s["y_sum"], n + 3 - NBLK)
                    for k in range(TB):
                        row = G.X[:, bass.ds(b * TB + k, 1), :].rearrange("p a d -> p (a d)")
                        gate = G.gate[:, bass.ds(b * TB + k, 1), e:e + 1].rearrange("p a e -> p (a e)")
                        st = dve.scalar_tensor_tensor(row, psy[j][:, k, :], gate, row, ALU.mult, ALU.add)
                    st.then_inc(s["y_sum"], 1)

                for e in range(NE):
                    with dve.Fori(0, NBLK // 2) as i:
                        for j in range(2):
                            b = i * 2 + j
                            n = i * 2 + (e * NBLK + j)
                            dve.wait_ge(s["y"], n + 1)
                            for c in range(NC):
                                k = b3i + NC * e + c
                                dve.wait_ge(h_ps[1][c], n + 1)
                                dve.wait_ge(silu[c], n + 1)
                                dve.scalar_tensor_tensor(hh[j][:, c, :], psh[1][c][:], G.vec[:, k:k + 1], sg[j][:, c, :],
                                                         ALU.add, ALU.mult).then_inc(hh_sb[c], 1)
                            take(b, n, e, j)


def store(nc, C, G):
    done = C.sem("stored")
    ov = G.out.rearrange("(n b) t d -> (b t) n d", b=2)
    with nc.Block() as block:

        @block.sync
        def _(sp):
            for k in range(4):
                sp.dma_start(ov[:, 8 * k:8 * k + 8, :], G.X[:, 8 * k:8 * k + 8, :]).then_inc(done, 16)
            sp.wait_ge(done, 64)


class Globals:
    pass


def program(nc, A, out, last=99):
    with ExitStack() as ctx:
        C, G = Chip(nc, ctx), Globals()
        G.kd = nc.dram_tensor("s4d_kernel", (D, P), F32, kind="Internal").ap()
        G.out = out
        G.X = C.sb("X", [P, NT, D])
        G.XT = C.sb("XT", [P, NT, D])
        G.ctxT = C.sb("ctxT", [DC, B * T])
        G.ident = C.sb("ident", [P, P])
        G.triu = C.sb("triu", [P, P])
        G.ones = C.sb("ones", [P, P])
        G.onesrow = C.sb("onesrow", [1, P])
        G.iota8 = C.sb("iota8", [P, NE])
        G.vec = C.sb("vec", [P, NVEC])
        G.tmask = C.sb("tmask", [P, NT])
        G.mg = C.sb("mg", [P, 1])
        G.dt = C.sb("dt", [P, 1])
        G.mean = C.sb("mean", [P, NT])
        G.rstd = C.sb("rstd", [P, NT])
        G.rstd2 = C.sb("rstd2", [P, NT])
        G.scratch = C.sb("scratch", [P, 8])
        with ExitStack() as early:
            G.XM = C.sb("XM", [P, NT, D], ctx=early)
            G.FO = C.sb("FO", [P, NT, 256], ctx=early)
            G.pen = C.sb("pen", [P, NT, T], ctx=early)
            G.gin = C.sb("gin", [P, D], ctx=early)
            G.bin = C.sb("bin", [P, D], ctx=early)
            G.wq = C.sb("wq", [P, P], ctx=early)
            G.wk = C.sb("wk", [DC, P], ctx=early)
            G.wv = C.sb("wv", [DC, D], ctx=early)
            G.film = C.sb("film", [P, 512], ctx=early)
            G.frow = C.sb("frow", [1, 512], ctx=early)
            setup(nc, C, A, G)
            C.end_phase()
            if last >= 1:
                first_attention(nc, C, A, G)
                C.end_phase()
            if last >= 2:
                convolution(nc, C, A, G)
                C.end_phase()
        with ExitStack() as late:
            G.XF = C.sb("XF", [D, B * T], ctx=late)
            G.gate = C.sb("gate", [P, NT, NE], ctx=late)
            if last >= 3:
                first_mlp(nc, C, A, G)
                C.end_phase()
            if last >= 4:
                close_first_attention(nc, C, A, G)
                C.end_phase()
                normalise_rows(nc, C, G, "ln1_", G.X)
                C.end_phase()
                turn_rows(nc, C, G, "turn1_")
                C.end_phase()
            if last >= 5:
                first_router(nc, C, A, G)
                C.end_phase()
            if last >= 6:
                add_gated_biases(nc, C, A, G, "gb0_", "L0_ffn_eb2")
                C.end_phase()
                first_experts(nc, C, A, G)
                C.end_phase()
            if last >= 7:
                normalise_rows(nc, C, G, "ln2_", G.X)
                C.end_phase()
                turn_rows(nc, C, G, "turn2_")
                C.end_phase()
                second_attention(nc, C, A, G)
                C.end_phase()
            if last >= 8:
                normalise_rows(nc, C, G, "ln3_", G.X)
                C.end_phase()
                turn_rows(nc, C, G, "turn3_")
                C.end_phase()
                second_router(nc, C, A, G)
                C.end_phase()
            if last >= 9:
                add_gated_biases(nc, C, A, G, "gb1_", "L1_ffn_b2")
                C.end_phase()
                second_experts(nc, C, A, G)
                C.end_phase()
                store(nc, C, G)
                C.end_phase()


_OUT = ((B, T, D), "float32")


def kernel(**inputs):
    import concourse.bacc as bacc
    from concourse.bass_utils import run_bass_kernel_spmd

    nc = bacc.Bacc("TRN2", target_bir_lowering=False, num_devices=1)
    arrays, args = {}, {}
    for name, a in inputs.items():
        a = np.ascontiguousarray(a)
        arrays[f"in_{name}"] = a
        args[name] = nc.dram_tensor(f"in_{name}", a.shape, mybir.dt.from_np(a.dtype), kind="ExternalInput").ap()
    out = nc.dram_tensor("out_0_dram", _OUT[0], mybir.dt.from_np(np.dtype(_OUT[1])), kind="ExternalOutput").ap()
    program(nc, args, out)
    r = run_bass_kernel_spmd(nc, [arrays], core_ids=[0])
    return r.results[0]["out_0_dram"]
```

```python
from contextlib import ExitStack

import numpy as np
import concourse.bass as bass
from concourse import mybir

F32 = mybir.dt.float32
U8 = mybir.dt.uint8
I32 = mybir.dt.int32
U32 = mybir.dt.uint32
F32R = mybir.dt.float32r
ALU = mybir.AluOpType
ACT = mybir.ActivationFunctionType
AX = mybir.AxisListType

P = 128
B, T, D = 64, 64, 128
DC = 96
NT = B * T // P
TB = 4
NBLK = NT // TB
H0, DH0 = 4, 32
H1, DH1 = 16, 8
KTOP = 32
NS = 64
HID = 512
NE = 8
CAP = 512
HE = 256
R = 16
EPS = 1e-5
MASKED = -1e30
TAKEN = -3e38
TWO_PI = 2.0 * np.pi
ROUND = float(1.5 * 2 ** 23)

VEC = {}
for _name, _n in (("L0_xattn_b1", 4), ("L0_ffn_rb1", 4), ("L1_xattn_bq", 1), ("L1_xattn_bk", 1),
                  ("L1_xattn_bv", 1), ("L0_xattn_g_ffn", 1), ("L0_xattn_b_ffn", 1),
                  ("L0_xattn_log_dt", 1), ("L0_xattn_D_skip", 1), ("L0_ffn_eb1", 32),
                  ("L1_ffn_b1", 16), ("L1_ffn_b3", 16)):
    VEC[_name] = (sum(n for _, n in VEC.values()), _n)
NVEC = sum(n for _, n in VEC.values())


class Steps:

    def __init__(self, eng, sem):
        self.eng, self.sem, self.n = eng, sem, 0

    def did(self, ins):
        ins.then_inc(self.sem, 1)
        self.n += 1

    def wait(self):
        self.eng.wait_ge(self.sem, self.n)

    def then(self, ins):
        self.did(ins)
        self.wait()

    def passed(self):
        self.eng.sem_inc(self.sem, 1)
        self.n += 1
        self.wait()

    def clear(self):
        self.wait()
        self.eng.sem_clear(self.sem)
        self.n = 0


class Chip:

    def __init__(self, nc, ctx):
        self.nc, self.ctx = nc, ctx
        self.own, self.before = [], []

    def sb(self, name, shape, dt=F32, ctx=None):
        return (ctx or self.ctx).enter_context(self.nc.sbuf_tensor(name, shape, dt))

    def ps(self, name, shape, ctx, dt=F32):
        return ctx.enter_context(self.nc.psum_tensor(name, shape, dt))

    def sem(self, name):
        self.own.append(self.nc.alloc_semaphore(name=name))
        return self.own[-1]

    def end_phase(self):
        for h in self.own:
            self.nc.sync.sem_clear(h)
        for h in self.before:
            self.nc.release_semaphore(h)
        self.own, self.before = [], self.own


class Tile:

    def __init__(self, t, k, j, fixed):
        self.t, self.k, self.j, self.fixed = t, k, j, fixed

    def by(self, d):
        q = self.j + d
        return Tile(self.t + d, self.k + q // 2, q % 2, self.fixed)

    def real(self):
        return not self.fixed or 0 <= self.t < NT


def sweep(eng, slot, first, lo, hi, last):
    for t in range(first, lo):
        slot(Tile(t, t // 2, t % 2, True))
    with eng.Fori(0, (hi - lo) // 2) as i:
        for q in range(2):
            slot(Tile(i * 2 + (lo + q), i + (lo + q) // 2, (lo + q) % 2, False))
    for t in range(hi, last):
        slot(Tile(t, t // 2, t % 2, True))


def after(eng, sem, n):
    if not isinstance(n, int) or n > 0:
        eng.wait_ge(sem, n)


def wide(ap, shape):
    return ap.to_broadcast(shape)


def row_statistics(dve, step, src, stats):
    with dve.Fori(0, NT // 2) as i:
        for j in range(2):
            t = i * 2 + j
            dve.bn_stats(stats[:, t, :], src[:, t, :])
    step.then(dve.memset(step.scratch, 0.0))


def mean_and_variance(dve, step, stats, mean, var, tmp):
    me, m2e, mo, m2o = (stats[:, :, k] for k in (1, 2, 4, 5))
    dve.tensor_tensor(mean, me, mo, ALU.add)
    dve.tensor_tensor(tmp, me, mo, ALU.subtract)
    step.then(dve.tensor_tensor(var, m2e, m2o, ALU.add))
    dve.tensor_scalar(mean, mean, 0.5, None, ALU.mult)
    dve.tensor_scalar(var, var, 1.0 / D, None, ALU.mult)
    step.then(dve.tensor_tensor(tmp, tmp, tmp, ALU.mult))
    step.then(dve.scalar_tensor_tensor(var, tmp, 0.25, var, ALU.mult, ALU.add))


def setup(nc, C, A, G):
    with ExitStack() as ctx:
        vrow = C.sb("vrow", [NVEC, D], ctx=ctx)
        mk8 = C.sb("mk8", [P, NT, T], U8, ctx)
        tm8 = C.sb("tm8", [NT, P], U8, ctx)
        tmf = C.sb("tmf", [NT, P], ctx=ctx)
        kin = C.sb("kin", [P, 4, NS], ctx=ctx)
        film0 = C.sb("film0", [P, 512], ctx=ctx)
        frow0 = C.sb("frow0", [1, 512], ctx=ctx)
        kt = C.sb("kt", [P, 16, NS], ctx=ctx)
        zV = C.sb("zV", [P, 8, 2, NS], ctx=ctx)
        zU = C.sb("zU", [P, 8, 2, NS], ctx=ctx)
        big = C.sb("big", [P, 8, 2, NS], ctx=ctx)
        ctm = C.sb("ctm", [P, 2, 8, NS], ctx=ctx)
        kpad = C.sb("kpad", [P, P], ctx=ctx)
        st = C.sb("st", [P, NT, 6], ctx=ctx)
        tmp = C.sb("tmp", [P, NT], ctx=ctx)
        var = C.sb("var", [P, NT], ctx=ctx)
        var2 = C.sb("var2", [P, NT], ctx=ctx)
        psv = C.ps("psv", [P, 512], ctx)
        pst = C.ps("pst", [P, 512], ctx)
        s = {n: C.sem("setup_" + n) for n in (
            "x", "kin", "vec", "masks", "film", "rest", "zero", "ident", "vec_ps", "vec_sb",
            "exp", "args", "trig", "var", "rms", "kpad", "kd", "dve", "act", "pool", "tmf", "tm_ps")}

        with nc.Block() as block:

            @block.sync
            def _(sp):
                sp.dma_start(kin[:, 0, :], A["L0_xattn_A_re"]).then_inc(s["kin"], 16)
                sp.dma_start(kin[:, 1, :], A["L0_xattn_A_im"]).then_inc(s["kin"], 16)
                sp.dma_start(kin[:, 2, :], A["L0_xattn_C_re"]).then_inc(s["kin"], 16)
                sp.dma_start(kin[:, 3, :], A["L0_xattn_C_im"]).then_inc(s["kin"], 16)
                for name, (at, n) in VEC.items():
                    src = A[name]
                    if len(src.shape) == 1:
                        src = src.rearrange("(c p) -> c p", p=D)
                    else:
                        src = src.rearrange("e (c p) -> (e c) p", p=D)
                    sp.dma_start(vrow[at:at + n, :], src).then_inc(s["vec"], 16)
                xv = A["x"].rearrange("(n b) t d -> (b t) n d", b=2)
                for k in range(4):
                    sp.dma_start(G.X[:, 8 * k:8 * k + 8, :], xv[:, 8 * k:8 * k + 8, :]).then_inc(s["x"], 16)
                for k, name in enumerate(("L0_xattn_W_film_in", "L0_xattn_W_film_out")):
                    sp.dma_start(film0[:, 256 * k:256 * k + 256], A[name]).then_inc(s["film"], 16)
                for k, name in enumerate(("L0_xattn_b_film_in", "L0_xattn_b_film_out")):
                    sp.dma_start(frow0[:, 256 * k:256 * k + 256],
                                 A[name].rearrange("(a n) -> a n", a=1)).then_inc(s["film"], 16)
                sp.dma_start(G.mg[:], A["L0_xattn_mod_gate"].partition_broadcast(P)).then_inc(s["film"], 16)
                m = A["mask_BxS2_bf1"]
                for b2 in range(2):
                    src = bass.AP(m.tensor, b2 * T, [[0, T], [2 * T, NT], [1, T]])
                    sp.dma_start(mk8[T * b2:T * b2 + T, :, :], src).then_inc(s["masks"], 16)
                sp.dma_start(tm8[:], A["mask_BxS_bf1"].rearrange("(n b) t -> n (b t)", b=2)).then_inc(s["masks"], 16)
                loads = [(G.gin[:], A["L0_xattn_g_norm_in"].partition_broadcast(P)),
                         (G.bin[:], A["L0_xattn_b_norm_in"].partition_broadcast(P)),
                         (G.wq[:], A["L0_xattn_Wq"]), (G.wk[:], A["L0_xattn_Wk"]), (G.wv[:], A["L0_xattn_Wv"])]
                for dst, src in loads:
                    sp.dma_start(dst, src).then_inc(s["rest"], 16)
                sp.wait_ge(s["rest"], 16 * len(loads))
                sp.wait_ge(s["kpad"], 1)
                sp.dma_start(G.kd, kpad[:]).then_inc(s["kd"], 16)
                sp.wait_ge(s["kd"], 16)

            @block.gpsimd
            def _(pool):
                pool.memset(G.ident[:], 0.0).then_inc(s["zero"], 1)
                pool.memset(G.triu[:], 1.0).then_inc(s["zero"], 1)
                pool.memset(G.ones[:], 1.0).then_inc(s["zero"], 1)
                pool.memset(G.onesrow[:], 1.0).then_inc(s["zero"], 1)
                pool.wait_ge(s["zero"], 4)
                pool.affine_select(out=G.ident[:], in_=G.ident[:], compare_op=ALU.not_equal, fill=1.0,
                                   base=0, pattern=[[-1, P]], channel_multiplier=1).then_inc(s["ident"], 1)
                pool.affine_select(out=G.triu[:], in_=G.triu[:], compare_op=ALU.is_gt, fill=0.0,
                                   base=0, pattern=[[1, P]], channel_multiplier=-1).then_inc(s["ident"], 1)
                for e in range(NE):
                    pool.memset(G.iota8[:, e:e + 1], float(e - NE)).then_inc(s["ident"], 1)
                pool.memset(kpad[:, 0:T], 0.0).then_inc(s["ident"], 1)
                pool.wait_ge(s["masks"], 48)
                pool.tensor_scalar(G.pen[:], mk8[:], -MASKED, MASKED, ALU.mult, ALU.add).then_inc(s["pool"], 1)
                pool.tensor_copy(tmf[:], tm8[:]).then_inc(s["tmf"], 1)
                pool.wait_ge(s["film"], 80)
                pool.tensor_scalar(G.film[:], film0[:], G.mg[:, 0:1], None, ALU.mult).then_inc(s["pool"], 1)
                pool.tensor_scalar(G.frow[:], frow0[:], G.mg[0:1, 0:1], None, ALU.mult).then_inc(s["pool"], 1)
                pool.wait_ge(s["pool"], 3)
                for k in range(2):
                    pool.tensor_scalar(G.frow[:, 256 * k:256 * k + D], G.frow[:, 256 * k:256 * k + D],
                                       1.0, None, ALU.add).then_inc(s["pool"], 1)
                pool.wait_ge(s["pool"], 5)

            @block.tensor
            def _(pe):
                pe.wait_ge(s["ident"], 1)
                pe.wait_ge(s["vec"], 16 * len(VEC))
                pe.transpose(psv[:, 0:NVEC], vrow[:], G.ident[0:NVEC, 0:NVEC]).then_inc(s["vec_ps"], 1)
                pe.wait_ge(s["tmf"], 1)
                pe.transpose(pst[:, 0:NT], tmf[:], G.ident[0:NT, 0:NT]).then_inc(s["tm_ps"], 1)

            @block.scalar
            def _(act):
                act.preload_act_table(ACT.Exp)
                act.wait_ge(s["vec_ps"], 1)
                act.activation(G.vec[:], psv[:, 0:NVEC], ACT.Copy).then_inc(s["vec_sb"], 1)
                act.wait_ge(s["tm_ps"], 1)
                act.activation(G.tmask[:], pst[:, 0:NT], ACT.Copy, scale=1.0 / H0).then_inc(s["vec_sb"], 1)
                act.wait_ge(s["vec_sb"], 1)
                at = VEC["L0_xattn_log_dt"][0]
                act.activation(G.dt[:], G.vec[:, at:at + 1], ACT.Exp).then_inc(s["exp"], 1)
                act.wait_ge(s["args"], 1)
                act.activation(kt[:, 3, :], kt[:, 0, :], ACT.Exp).then_inc(s["exp"], 1)
                act.wait_ge(s["args"], 2)
                act.activation(kt[:, 4:6, :], kt[:, 4:6, :], ACT.Sin).then_inc(s["trig"], 1)
                act.wait_ge(s["var"], 1)
                act.activation(var[:], var[:], ACT.Sqrt).then_inc(s["rms"], 1)
                act.wait_ge(s["var"], 2)
                act.activation(var2[:], var2[:], ACT.Sqrt).then_inc(s["rms"], 1)

            @block.vector
            def _(dve):
                step = Steps(dve, s["dve"])
                step.scratch = G.scratch[:]
                TT, TS = dve.tensor_tensor, dve.tensor_scalar
                dve.wait_ge(s["kin"], 64)
                dve.wait_ge(s["exp"], 1)
                TS(kt[:, 0, :], kin[:, 0, :], G.dt[:, 0:1], None, ALU.mult).then_inc(s["args"], 1)
                step.then(TS(kt[:, 1, :], kin[:, 1, :], G.dt[:, 0:1], None, ALU.mult))
                step.did(TS(kt[:, 6, :], kt[:, 1, :], 1.0 / TWO_PI, 0.25, ALU.mult, ALU.add))
                step.then(TS(kt[:, 7, :], kt[:, 1, :], 1.0 / TWO_PI, None, ALU.mult))
                step.then(TS(kt[:, 6:8, :], kt[:, 6:8, :], ROUND, None, ALU.add))
                step.then(TS(kt[:, 6:8, :], kt[:, 6:8, :], ROUND, None, ALU.subtract))
                c1 = 6.28125
                c2 = TWO_PI - c1
                th = wide(kt[:, 1:2, :], [P, 2, NS])
                step.then(dve.scalar_tensor_tensor(kt[:, 4:6, :], kt[:, 6:8, :], -c1, th, ALU.mult, ALU.add))
                step.then(dve.scalar_tensor_tensor(kt[:, 4:6, :], kt[:, 6:8, :], -c2, kt[:, 4:6, :], ALU.mult, ALU.add))
                step.then(TS(kt[:, 4, :], kt[:, 4, :], float(np.pi / 2), None, ALU.add))
                TS(kt[:, 4:6, :], kt[:, 4:6, :], float(np.float32(3.1415925)), float(np.float32(-3.1415925)),
                   ALU.min, ALU.max).then_inc(s["args"], 1)
                dve.wait_ge(s["exp"], 2)
                dve.wait_ge(s["trig"], 1)
                V = [(zV[:, b, 0, :], zV[:, b, 1, :]) for b in range(8)]
                dve.memset(zV[:, 0, 0, :], 1.0)
                dve.memset(zV[:, 0, 1, :], 0.0)
                TT(zV[:, 1, 0, :], kt[:, 3, :], kt[:, 4, :], ALU.mult)
                step.then(TT(zV[:, 1, 1, :], kt[:, 3, :], kt[:, 5, :], ALU.mult))

                def times(out, a, b, n=1):
                    t0, t1 = (ctm[:, k, 0:n, :] if n > 1 else ctm[:, k, 0, :] for k in range(2))
                    TT(t0, a[0], b[0], ALU.mult)
                    step.then(TT(t1, a[1], b[1], ALU.mult))
                    step.then(TT(out[0], t0, t1, ALU.subtract))
                    TT(t0, a[0], b[1], ALU.mult)
                    step.then(TT(t1, a[1], b[0], ALU.mult))
                    step.then(TT(out[1], t0, t1, ALU.add))

                def powers(z, a, n):
                    return tuple(z[:, a:a + n, k, :] for k in range(2))

                def same(z, n):
                    return tuple(wide(q.unsqueeze(1), [P, n, NS]) for q in z)

                z2, z4, z8, z16, z32 = ((kt[:, 6 + 2 * k, :], kt[:, 7 + 2 * k, :]) for k in range(5))
                times(z2, V[1], V[1])
                times(powers(zV, 2, 2), powers(zV, 0, 2), same(z2, 2), 2)
                times(z4, z2, z2)
                times(powers(zV, 4, 4), powers(zV, 0, 4), same(z4, 4), 4)
                times(z8, z4, z4)
                times(z16, z8, z8)
                times(z32, z16, z16)
                zm = (kt[:, 0, :], kt[:, 1, :])
                TS(zm[0], V[1][0], -1.0, None, ALU.add)
                dve.tensor_copy(zm[1], V[1][1])
                TT(ctm[:, 0, 0, :], kin[:, 0, :], kin[:, 0, :], ALU.mult)
                TT(ctm[:, 1, 0, :], kin[:, 1, :], kin[:, 1, :], ALU.mult)
                step.then(TS(kt[:, 2, :], kin[:, 1, :], -1.0, None, ALU.mult))
                step.then(TT(kt[:, 3, :], ctm[:, 0, 0, :], ctm[:, 1, 0, :], ALU.add))
                step.then(dve.reciprocal(kt[:, 3, :], kt[:, 3, :]))
                step.then(TS(kt[:, 3, :], kt[:, 3, :], 2.0, None, ALU.mult))
                prod = (kt[:, 4, :], kt[:, 5, :])
                times(prod, zm, (kin[:, 2, :], kin[:, 3, :]))
                U0 = (zU[:, 0, 0, :], zU[:, 0, 1, :])
                times((big[:, 0, 0, :], big[:, 0, 1, :]), prod, (kin[:, 0, :], kt[:, 2, :]))
                TT(U0[0], big[:, 0, 0, :], kt[:, 3, :], ALU.mult)
                step.then(TT(U0[1], big[:, 0, 1, :], kt[:, 3, :], ALU.mult))
                times((zU[:, 1, 0, :], zU[:, 1, 1, :]), U0, z8)
                times(powers(zU, 2, 2), powers(zU, 0, 2), same(z16, 2), 2)
                times(powers(zU, 4, 4), powers(zU, 0, 4), same(z32, 4), 4)
                step.then(TS(zV[:, :, 1, :], zV[:, :, 1, :], -1.0, None, ALU.mult))
                dve.wait_ge(s["ident"], 11)
                for a in range(8):
                    u = wide(zU[:, a:a + 1, :, :], [P, 8, 2, NS])
                    step.then(TT(big[:], zV[:], u, ALU.mult))
                    step.then(dve.tensor_reduce(kpad[:, T + 8 * a:T + 8 * a + 8],
                                                big[:].rearrange("p b c n -> p b (c n)"), AX.X, ALU.add))
                dve.wait_ge(s["vec_sb"], 2)
                at = VEC["L0_xattn_D_skip"][0]
                TT(kpad[:, T:T + 1], kpad[:, T:T + 1], G.vec[:, at:at + 1], ALU.add).then_inc(s["kpad"], 1)
                dve.wait_ge(s["x"], 64)
                row_statistics(dve, step, G.X, st)
                mean_and_variance(dve, step, st, G.mean[:], var2[:], tmp[:])
                TS(var[:], var2[:], EPS, None, ALU.add).then_inc(s["var"], 1)
                dve.wait_ge(s["rms"], 1)
                step.then(dve.reciprocal(G.rstd[:], var[:]))
                step.then(TT(tmp[:], G.rstd[:], G.rstd[:], ALU.mult))
                step.then(TT(var2[:], var2[:], tmp[:], ALU.mult))
                TS(var2[:], var2[:], EPS, None, ALU.add).then_inc(s["var"], 1)
                dve.wait_ge(s["rms"], 2)
                step.then(dve.reciprocal(G.rstd2[:], var2[:]))
                step.then(TT(G.XT[:], G.X[:], wide(G.mean[:].unsqueeze(2), [P, NT, D]), ALU.subtract))
                step.then(TT(G.XT[:], G.XT[:], wide(G.rstd[:].unsqueeze(2), [P, NT, D]), ALU.mult))


def first_attention(nc, C, A, G):
    scale = 1.0 / float(np.sqrt(DH0).astype(np.float32))
    with ExitStack() as ctx:
        def two(name, shape):
            return [C.sb(f"{name}{j}", shape, ctx=ctx) for j in range(2)]

        xs, cs, cb = two("xs", [P, D]), two("cs", [P, DC]), two("cb", [P, DC])
        xf, cf = two("xf", [D, P]), two("cf", [DC, P])
        qt, kb = two("qt", [P, P]), two("kb", [P, 2, H0, T])
        sc, wk_, m8 = two("sc", [P, H0, T]), two("work", [P, H0, T]), two("m8", [P, H0, 4, 8])
        dd, ee, pr = two("dd", [P, H0, T]), two("ee", [P, H0, T]), two("pr", [P, H0, T])
        rs, at, abd = two("rs", [P, 2, H0]), two("at", [P, P]), two("abd", [P, P])
        us, ct, fi = two("us", [DC, P]), two("ct", [D, P]), two("fi", [P, 256])
        xn = C.sb("xn", [P, D], ctx=ctx)
        psa = [C.ps(f"psa{j}", [P, 512], ctx) for j in range(2)]
        pss = [C.ps(f"pss{j}", [P, 512], ctx) for j in range(2)]
        psb = [C.ps(f"psb{j}", [P, 512], ctx) for j in range(2)]
        psf = [C.ps(f"psf{j}", [P, 512], ctx) for j in range(2)]
        s = {n: C.sem("att0_" + n) for n in (
            "xs", "turned", "turned_sb", "qk", "qk_sb", "scores", "scores_sb", "max", "diff", "exp",
            "attn", "attn_turned", "attn_sb", "u", "u_sb", "c", "c_sb", "film", "film_sb", "mod",
            "ctx_kept", "zero", "dve", "pool")}
        loaded = [C.sem(f"att0_ctx_loaded{j}") for j in range(2)]
        again = [C.sem(f"att0_ctx_again{j}") for j in range(2)]
        ctx_v = A["ctx_768"].rearrange("b t d -> (b t) d")

        with nc.Block() as block:
            SWEEP = (-2, 3, 29, NT + 1)

            @block.sync
            def _(sp):
                def rows(t):
                    return ctx_v[bass.ds(t * P, P), :]

                def slot(x):
                    a, c = x.by(2), x.by(-1)
                    if a.real():
                        after(sp, s["turned"], a.t - 1)
                        sp.dma_start(cs[a.j][:], rows(a.t)).then_inc(loaded[a.j], 16)
                    if c.real():
                        after(sp, s["u"], c.t - 1)
                        sp.dma_start(cb[c.j][:], rows(c.t)).then_inc(again[c.j], 16)

                sweep(sp, slot, *SWEEP)

            @block.gpsimd
            def _(pool):
                step = Steps(pool, s["pool"])
                for j in range(2):
                    for m in (kb[j], abd[j], at[j]):
                        pool.memset(m[:], 0.0).then_inc(s["zero"], 1)

                def slot(x):
                    j, a, g, c = x.j, x.by(2), x.by(3), x.by(-1)
                    if x.real():
                        pool.wait_ge(s["max"], x.t + 1)
                        pool.tensor_tensor(dd[j][:], sc[j][:], wide(m8[j][:, :, 0, 0:1], [P, H0, T]),
                                           ALU.subtract).then_inc(s["diff"], 1)
                    if g.real():
                        after(pool, s["turned"], g.t - 1)
                        pool.tensor_copy(xs[g.j][:], G.XT[:, g.t, :]).then_inc(s["xs"], 1)
                    if a.real():
                        pool.wait_ge(s["turned_sb"], a.t + 1)
                        pool.tensor_copy(G.ctxT[:, bass.ds(a.t * P, P)], cf[a.j][:]).then_inc(s["ctx_kept"], 1)
                    if c.real():
                        step.then(pool.tensor_tensor(xn[:], G.XT[:, c.t, :], wide(G.rstd2[:, bass.ds(c.t, 1)], [P, D]), ALU.mult))
                        step.then(pool.tensor_tensor(xn[:], xn[:], G.gin[:], ALU.mult))
                        step.then(pool.tensor_tensor(xn[:], xn[:], G.bin[:], ALU.add))
                        pool.wait_ge(s["film_sb"], c.t + 1)
                        step.then(pool.tensor_tensor(xn[:], xn[:], fi[c.j][:, 0:D], ALU.mult))
                        pool.tensor_tensor(G.XM[:, c.t, :], xn[:], fi[c.j][:, D:2 * D], ALU.add).then_inc(s["mod"], 1)
                        step.clear()
                        pool.wait_ge(s["mod"], c.t + 1)

                for j in range(1):
                    pool.tensor_copy(xs[j][:], G.XT[:, j, :]).then_inc(s["xs"], 1)
                sweep(pool, slot, *SWEEP)

            @block.tensor
            def _(pe):
                pe.wait_ge(s["zero"], 6)

                def slot(x):
                    a, c = x.by(2), x.by(-1)
                    if a.real():
                        j = a.j
                        pe.wait_ge(s["xs"], a.t + 1)
                        after(pe, s["qk_sb"], a.t - 1)
                        pe.transpose(psa[j][:, 0:P], xs[j][:], G.ident[:])
                        pe.wait_ge(loaded[j], (a.k + 1) * 16)
                        pe.transpose(psa[j][0:DC, P:2 * P], cs[j][:], G.ident[:]).then_inc(s["turned"], 1)
                    if c.real():
                        pe.wait_ge(s["attn"], c.t + 1)
                        after(pe, s["c_sb"], c.t - 1)
                        pe.transpose(psb[c.j][:, 0:P], at[c.j][:], G.ident[:]).then_inc(s["attn_turned"], 1)
                    if a.real():
                        pe.wait_ge(s["turned_sb"], a.t + 1)
                        pe.matmul(psa[j][:, 256:384], G.wq[:], xf[j][:], start=True, stop=True)
                        pe.matmul(psa[j][:, 384:512], G.wk[:], cf[j][:], start=True, stop=True).then_inc(s["qk"], 1)
                    if c.real():
                        pe.wait_ge(s["attn_sb"], c.t + 1)
                        pe.wait_ge(again[c.j], (c.k + 1) * 16)
                        pe.matmul(psb[c.j][0:DC, P:2 * P], cb[c.j][:], abd[c.j][:], start=True, stop=True).then_inc(s["u"], 1)
                    if a.real():
                        pe.wait_ge(s["qk_sb"], a.t + 1)
                        after(pe, s["scores_sb"], a.t - 1)
                        for b2 in range(2):
                            mm = pe.matmul(pss[j][T * b2:T * b2 + T, 0:H0 * T], qt[j][:, T * b2:T * b2 + T],
                                           kb[j][:, b2, :, :], start=True, stop=True)
                        mm.then_inc(s["scores"], 1)
                    if c.real():
                        pe.wait_ge(s["u_sb"], c.t + 1)
                        pe.matmul(psb[c.j][:, 256:384], G.wv[:], us[c.j][:], start=True, stop=True).then_inc(s["c"], 1)
                        pe.wait_ge(s["c_sb"], c.t + 1)
                        after(pe, s["film_sb"], c.t - 1)
                        pe.matmul(psf[c.j][:], ct[c.j][:], G.film[:], start=True, stop=False)
                        pe.matmul(psf[c.j][:], G.onesrow[:], G.frow[:], start=False, stop=True).then_inc(s["film"], 1)

                sweep(pe, slot, *SWEEP)

            @block.scalar
            def _(act):
                act.preload_act_table(ACT.Exp)
                copy = lambda out, in_: act.activation(out, in_, ACT.Copy)

                def slot(x):
                    a, c = x.by(2), x.by(-1)
                    if a.real():
                        j = a.j
                        act.wait_ge(s["turned"], a.t + 1)
                        after(act, s["ctx_kept"], a.t - 1)
                        copy(xf[j][:], psa[j][:, 0:P])
                        copy(cf[j][:], psa[j][0:DC, P:2 * P]).then_inc(s["turned_sb"], 1)
                    if c.real():
                        act.wait_ge(s["attn_turned"], c.t + 1)
                        copy(abd[c.j][0:T, 0:T], psb[c.j][0:T, 0:T])
                        copy(abd[c.j][T:P, T:P], psb[c.j][0:T, T:P]).then_inc(s["attn_sb"], 1)
                    if x.real():
                        act.wait_ge(s["diff"], x.t + 1)
                        act.activation(ee[x.j][:], dd[x.j][:], ACT.Exp, scale=scale).then_inc(s["exp"], 1)
                    if a.real():
                        act.wait_ge(s["qk"], a.t + 1)
                        after(act, s["scores"], a.t - 1)
                        copy(qt[j][:], psa[j][:, 256:384])
                        for h in range(H0):
                            rows = slice(DH0 * h, DH0 * h + DH0)
                            m = copy(kb[j][rows, :, h, :], psa[j][rows, 384:512].rearrange("p (b g) -> p b g", b=2))
                        m.then_inc(s["qk_sb"], 1)
                    if c.real():
                        act.wait_ge(s["u"], c.t + 1)
                        copy(us[c.j][:], psb[c.j][0:DC, P:2 * P]).then_inc(s["u_sb"], 1)
                        act.wait_ge(s["c"], c.t + 1)
                        copy(ct[c.j][:], psb[c.j][:, 256:384]).then_inc(s["c_sb"], 1)
                        act.wait_ge(s["film"], c.t + 1)
                        after(act, s["mod"], c.t - 1)
                        copy(fi[c.j][:], psf[c.j][:, 0:256])
                        copy(G.FO[:, c.t, :], psf[c.j][:, 256:512]).then_inc(s["film_sb"], 1)

                sweep(act, slot, *SWEEP)

            @block.vector
            def _(dve):
                dve.wait_ge(s["zero"], 6)
                step = Steps(dve, s["dve"])

                def select(x):
                    t, j = x.t, x.j
                    dve.wait_ge(s["scores"], t + 1)
                    dve.tensor_tensor(sc[j][:], pss[j][:, 0:H0 * T].rearrange("p (h g) -> p h g", h=H0),
                                      wide(G.pen[:, bass.ds(t, 1), :], [P, H0, T]), ALU.add).then_inc(s["scores_sb"], 1)
                    dve.wait_ge(s["scores_sb"], t + 1)
                    step.passed()
                    src = sc[j]
                    for r in range(KTOP // 8):
                        for h in range(H0):
                            mx = dve.max(m8[j][:, h, r, :], src[:, h, :])
                            if r == 0 and h == H0 - 1:
                                mx.then_inc(s["max"], 1)
                            else:
                                step.did(mx)
                        if r == 0:
                            dve.wait_ge(s["max"], t + 1)
                            step.passed()
                        else:
                            step.wait()
                        for h in range(H0):
                            step.did(dve.match_replace(wk_[j][:, h, :], m8[j][:, h, r, :], src[:, h, :], TAKEN))
                        step.wait()
                        src = wk_[j]
                    dve.wait_ge(s["exp"], t + 1)
                    flat = lambda m: m[j][:].rearrange("p h g -> p (h g)")
                    step.then(dve.scalar_tensor_tensor(flat(pr), flat(wk_), TAKEN / 3, flat(ee), ALU.is_le, ALU.mult))
                    step.then(dve.tensor_reduce(rs[j][:, 0, :], pr[j][:], AX.X, ALU.add))
                    step.then(dve.reciprocal(rs[j][:, 1, :], rs[j][:, 0, :]))
                    step.then(dve.tensor_scalar(rs[j][:, 1, :], rs[j][:, 1, :], G.tmask[:, bass.ds(t, 1)], None, ALU.mult))
                    step.then(dve.tensor_tensor(pr[j][:], pr[j][:], wide(rs[j][:, 1, :].unsqueeze(2), [P, H0, T]), ALU.mult))
                    after(dve, s["attn_turned"], t - 1)
                    dve.tensor_reduce(at[j][:, 0:T], pr[j][:].rearrange("p h g -> p g h"), AX.X, ALU.add).then_inc(s["attn"], 1)
                    step.clear()

                sweep(dve, select, 0, 2, NT, NT)


def convolution(nc, C, A, G):
    CH = 16
    NG = D // CH
    with ExitStack() as ctx:
        toe = [C.sb(f"toe{j}", [P, CH, P], ctx=ctx) for j in range(2)]
        psy = [C.ps(f"psy{j}", [P, CH, NT], ctx) for j in range(2)]
        ym = [C.sb(f"ym{j}", [P, NT, CH], ctx=ctx) for j in range(2)]
        yn = [C.sb(f"yn{j}", [P, NT, CH], ctx=ctx) for j in range(2)]
        flip = C.sb("flip", [P, P], ctx=ctx)
        psr = [C.ps(f"psr{j}", [P, TB, D], ctx) for j in range(2)]
        s = {n: C.sem("conv_" + n) for n in ("zero", "flip", "y", "y_film", "y_sum", "step", "rev", "rev_sb")}
        loaded = [C.sem(f"conv_toeplitz_loaded{j}") for j in range(2)]
        with nc.Block() as block:

            @block.sync
            def _(sp):
                sp.wait_ge(s["zero"], 2)
                for g in range(NG):
                    j = g % 2
                    if g >= 2:
                        sp.wait_ge(s["y"], g - 1)
                    for b2 in range(2):
                        src = bass.AP(G.kd.tensor, g * (CH * P) + 1, [[1, T], [P, CH], [1, T]])
                        sp.dma_start(toe[j][T * b2:T * b2 + T, :, T * b2:T * b2 + T], src).then_inc(loaded[j], 16)

            @block.gpsimd
            def _(pool):
                pool.sem_inc(s["y_sum"], 2)
                pool.memset(flip[:], 0.0).then_inc(s["flip"], 1)
                pool.wait_ge(s["flip"], 1)
                for b2 in range(2):
                    half = flip[T * b2:T * b2 + T, T * b2:T * b2 + T]
                    pool.affine_select(out=half, in_=half, compare_op=ALU.not_equal, fill=1.0, base=1 - T,
                                       pattern=[[1, T]], channel_multiplier=1).then_inc(s["flip"], 1)
                    pool.wait_ge(s["flip"], 2 + b2)
                for j in range(2):
                    pool.memset(toe[j][:], 0.0).then_inc(s["zero"], 1)
                with pool.Fori(0, NG // 2) as i:
                    for j in range(2):
                        g = i * 2 + j
                        pool.wait_ge(s["y_film"], g + 3)
                        ch = bass.ds(g * CH, CH)
                        pool.tensor_tensor(yn[j][:], ym[j][:], G.FO[:, :, bass.ds(g * CH + D, CH)], ALU.add).then_inc(s["step"], 1)
                        pool.wait_ge(s["step"], g + 1)
                        pool.tensor_tensor(G.XT[:, :, ch], G.XT[:, :, ch], yn[j][:], ALU.add).then_inc(s["y_sum"], 1)
                pool.wait_ge(s["y_sum"], NG + 2)

            @block.tensor
            def _(pe):
                pe.wait_ge(s["flip"], 3)
                with pe.Fori(0, NBLK // 2) as i:
                    for j in range(2):
                        b = i * 2 + j
                        pe.wait_ge(s["rev_sb"], b + 1)
                        pe.matmul(psr[j][:], flip[:], G.XM[:, bass.ds(b * TB, TB), :], start=True, stop=True).then_inc(s["rev"], 1)
                pe.wait_ge(s["rev_sb"], NBLK + 2)
                with pe.Fori(0, NG // 2) as i:
                    for j in range(2):
                        g = i * 2 + j
                        pe.wait_ge(loaded[j], (i + 1) * 32)
                        pe.wait_ge(s["y_film"], g + 1)
                        for c in range(CH):
                            mm = pe.matmul(psy[j][:, c, :], toe[j][:, c, :], G.XM[:, :, bass.ds(g * CH + c, 1)],
                                           start=True, stop=True)
                        mm.then_inc(s["y"], 1)

            @block.scalar
            def _(act):
                act.sem_inc(s["rev_sb"], 2)
                act.preload_act_table(ACT.Copy)
                with act.Fori(0, NBLK // 2) as i:
                    for j in range(2):
                        b = i * 2 + j
                        act.wait_ge(s["rev"], b + 1)
                        act.activation(G.XM[:, bass.ds(b * TB, TB), :], psr[j][:], ACT.Copy).then_inc(s["rev_sb"], 1)

            @block.vector
            def _(dve):
                dve.sem_inc(s["y_film"], 2)
                with dve.Fori(0, NG // 2) as i:
                    for j in range(2):
                        g = i * 2 + j
                        dve.wait_ge(s["y"], g + 1)
                        dve.wait_ge(s["y_sum"], g + 1)
                        dve.tensor_tensor(ym[j][:], psy[j][:].rearrange("p c b -> p b c"),
                                          G.FO[:, :, bass.ds(g * CH, CH)], ALU.mult).then_inc(s["y_film"], 1)


def normalise_rows(nc, C, G, tag, src, then=None):
    with ExitStack() as ctx:
        st = C.sb(tag + "st", [P, NT, 6], ctx=ctx)
        tmp = C.sb(tag + "tmp", [P, NT], ctx=ctx)
        var = C.sb(tag + "var", [P, NT], ctx=ctx)
        root = C.sb(tag + "root", [P, NT], ctx=ctx)
        s = {n: C.sem(tag + n) for n in ("var", "root", "dve")}
        with nc.Block() as block:

            @block.scalar
            def _(act):
                act.wait_ge(s["var"], 1)
                act.activation(root[:], var[:], ACT.Sqrt).then_inc(s["root"], 1)

            @block.vector
            def _(dve):
                step = Steps(dve, s["dve"])
                step.scratch = G.scratch[:]
                row_statistics(dve, step, src, st)
                mean_and_variance(dve, step, st, G.mean[:], var[:], tmp[:])
                dve.tensor_scalar(var[:], var[:], EPS, None, ALU.add).then_inc(s["var"], 1)
                dve.wait_ge(s["root"], 1)
                step.then(dve.reciprocal(root[:], root[:]))
                newton(dve, step, G.rstd[:], root[:], var[:], tmp[:])
                if then:
                    then(dve, step)


def newton(dve, step, out, r, v, tmp):
    step.then(dve.tensor_tensor(tmp, r, r, ALU.mult))
    step.then(dve.tensor_tensor(tmp, tmp, v, ALU.mult))
    step.then(dve.tensor_scalar(tmp, tmp, -0.5, 1.5, ALU.mult, ALU.add))
    step.then(dve.tensor_tensor(out, r, tmp, ALU.mult))


def first_mlp(nc, C, A, G):
    normalise_rows(nc, C, G, "ln_ffn_", G.XT)
    C.end_phase()
    gv, bv = VEC["L0_xattn_g_ffn"][0], VEC["L0_xattn_b_ffn"][0]
    b1 = VEC["L0_xattn_b1"][0]
    with ExitStack() as ctx:
        w1 = C.sb("w1", [D, HID], ctx=ctx)
        w2 = C.sb("w2", [P, HID // P, D], ctx=ctx)
        b2 = C.sb("b2", [P, D], ctx=ctx)
        xs = [C.sb(f"mlp_xs{j}", [P, TB, D], ctx=ctx) for j in range(2)]
        xf = [C.sb(f"mlp_xf{j}", [D, TB * P], ctx=ctx) for j in range(2)]
        hs = [C.sb(f"mlp_hs{j}", [P, HID // P, TB * P], ctx=ctx) for j in range(2)]
        ys = [C.sb(f"mlp_ys{j}", [P, TB, D], ctx=ctx) for j in range(2)]
        pst = C.ps("mlp_pst", [P, TB * P], ctx)
        psh = [C.ps(f"mlp_psh{c}", [P, TB * P], ctx) for c in range(4)]
        psy = [C.ps(f"mlp_psy{j}", [P, TB, D], ctx) for j in range(2)]
        s = {n: C.sem("mlp_" + n) for n in ("weights", "xs", "turned", "turned_sb", "y", "y_b", "y_sum", "dve")}
        h_ps = [C.sem(f"mlp_h_ps{c}") for c in range(4)]
        h_sb = [C.sem(f"mlp_h_sb{c}") for c in range(4)]
        with nc.Block() as block:

            @block.sync
            def _(sp):
                sp.dma_start(w1[:], A["L0_xattn_W1"]).then_inc(s["weights"], 16)
                sp.dma_start(w2[:], A["L0_xattn_W2"].rearrange("(c p) d -> p c d", p=P)).then_inc(s["weights"], 16)
                sp.dma_start(b2[:], A["L0_xattn_b2"].partition_broadcast(P)).then_inc(s["weights"], 16)

            @block.tensor
            def _(pe):
                pe.sem_inc(s["turned"], 2)
                pe.sem_inc(s["y"], 2)
                pe.wait_ge(s["weights"], 48)
                with pe.Fori(0, NBLK // 2) as i:
                    for j in range(2):
                        b = i * 2 + j
                        pe.wait_ge(s["xs"], b + 1)
                        pe.wait_ge(s["turned_sb"], b + 1)
                        for k in range(TB):
                            mm = pe.transpose(pst[:, k * P:(k + 1) * P], xs[j][:, k, :], G.ident[:])
                        mm.then_inc(s["turned"], 1)
                        pe.wait_ge(s["turned_sb"], b + 2)
                        for c in range(4):
                            pe.wait_ge(h_sb[c], b + 1)
                            pe.matmul(psh[c][:], w1[:, c * P:(c + 1) * P], xf[j][:], start=True, stop=True).then_inc(h_ps[c], 1)
                        pe.wait_ge(s["y_b"], b + 1)
                        for c in range(4):
                            pe.wait_ge(h_sb[c], b + 2)
                            for k in range(TB):
                                mm = pe.matmul(psy[j][:, k, :], hs[j][:, c, k * P:(k + 1) * P], w2[:, c, :],
                                               start=(c == 0 and k == 0), stop=(c == 3), skip_group_check=True)
                        mm.then_inc(s["y"], 1)

            @block.scalar
            def _(act):
                act.preload_act_table(ACT.Gelu)
                act.sem_inc(s["turned_sb"], 1)
                for c in range(4):
                    act.sem_inc(h_sb[c], 1)
                with act.Fori(0, NBLK // 2) as i:
                    for j in range(2):
                        b = i * 2 + j
                        act.wait_ge(s["turned"], b + 3)
                        act.activation(xf[j][:], pst[:], ACT.Identity, scale=G.vec[:, gv:gv + 1],
                                       bias=G.vec[:, bv:bv + 1]).then_inc(s["turned_sb"], 1)
                        act.wait_ge(s["y"], b + 1)
                        for c in range(4):
                            act.wait_ge(h_ps[c], b + 1)
                            act.activation(hs[j][:, c, :], psh[c][:], ACT.Gelu,
                                           bias=G.vec[:, b1 + c:b1 + c + 1]).then_inc(h_sb[c], 1)

            @block.vector
            def _(dve):
                dve.sem_inc(s["y_b"], 2)
                step = Steps(dve, s["dve"])

                def give(b, j):
                    mean = wide(G.mean[:, bass.ds(b * TB, TB)].unsqueeze(2), [P, TB, D])
                    rstd = wide(G.rstd[:, bass.ds(b * TB, TB)].unsqueeze(2), [P, TB, D])
                    step.then(dve.tensor_tensor(xs[j][:], G.XT[:, bass.ds(b * TB, TB), :], mean, ALU.subtract))
                    dve.tensor_tensor(xs[j][:], xs[j][:], rstd, ALU.mult).then_inc(s["xs"], 1)
                    step.clear()

                def take(b, j):
                    dve.wait_ge(s["y"], b + 3)
                    dve.tensor_tensor(ys[j][:], psy[j][:], wide(b2[:].unsqueeze(1), [P, TB, D]), ALU.add).then_inc(s["y_b"], 1)
                    dve.wait_ge(s["y_b"], b + 3)
                    rows = G.XT[:, bass.ds(b * TB, TB), :]
                    dve.tensor_tensor(rows, rows, ys[j][:], ALU.add).then_inc(s["y_sum"], 1)

                dve.wait_ge(s["weights"], 48)
                give(0, 0)
                give(1, 1)
                with dve.Fori(0, NBLK // 2 - 1) as i:
                    for j in range(2):
                        take(i * 2 + j, j)
                        give(i * 2 + 2 + j, j)
                take(NBLK - 2, 0)
                take(NBLK - 1, 1)
                dve.wait_ge(s["y_sum"], NBLK)


def close_first_attention(nc, C, A, G):
    with ExitStack() as ctx:
        g = C.sb("gout", [P, D], ctx=ctx)
        b = C.sb("bout", [P, D], ctx=ctx)
        loaded = C.sem("close_loaded")
        with nc.Block() as block:

            @block.sync
            def _(sp):
                sp.dma_start(g[:], A["L0_xattn_g_norm_out"].partition_broadcast(P)).then_inc(loaded, 16)
                sp.dma_start(b[:], A["L0_xattn_b_norm_out"].partition_broadcast(P)).then_inc(loaded, 16)

        def then(dve, step):
            dve.wait_ge(loaded, 32)
            full = [P, NT, D]
            XT = G.XT[:]
            step.then(dve.tensor_tensor(XT, XT, wide(G.mean[:].unsqueeze(2), full), ALU.subtract))
            step.then(dve.tensor_tensor(XT, XT, wide(G.rstd[:].unsqueeze(2), full), ALU.mult))
            step.then(dve.tensor_tensor(XT, XT, wide(g[:].unsqueeze(1), full), ALU.mult))
            step.then(dve.tensor_tensor(XT, XT, wide(b[:].unsqueeze(1), full), ALU.add))
            step.then(dve.tensor_tensor(G.X[:], G.X[:], XT, ALU.add))

        normalise_rows(nc, C, G, "ln_out_", G.XT, then)


def turn_rows(nc, C, G, tag, keep=False):
    with ExitStack() as ctx:
        xs = [C.sb(f"{tag}xs{j}", [P, TB, D], ctx=ctx) for j in range(2)]
        pst = [C.ps(f"{tag}pst{j}", [P, TB * P], ctx) for j in range(2)]
        s = {n: C.sem(tag + n) for n in ("xs", "kept", "turned", "turned_sb", "dve")}
        with nc.Block() as block:

            @block.vector
            def _(dve):
                step = Steps(dve, s["dve"])
                with dve.Fori(0, NBLK // 2) as i:
                    for j in range(2):
                        b = i * 2 + j
                        dve.wait_ge(s["turned"], b + 1)
                        if keep:
                            dve.wait_ge(s["kept"], b + 1)
                        mean = wide(G.mean[:, bass.ds(b * TB, TB)].unsqueeze(2), [P, TB, D])
                        rstd = wide(G.rstd[:, bass.ds(b * TB, TB)].unsqueeze(2), [P, TB, D])
                        step.then(dve.tensor_tensor(xs[j][:], G.X[:, bass.ds(b * TB, TB), :], mean, ALU.subtract))
                        dve.tensor_tensor(xs[j][:], xs[j][:], rstd, ALU.mult).then_inc(s["xs"], 1)
                        step.clear()

            if keep:
                @block.gpsimd
                def _(pool):
                    pool.sem_inc(s["kept"], 2)
                    with pool.Fori(0, NBLK // 2) as i:
                        for j in range(2):
                            b = i * 2 + j
                            pool.wait_ge(s["xs"], b + 1)
                            pool.tensor_copy(G.XT[:, bass.ds(b * TB, TB), :], xs[j][:]).then_inc(s["kept"], 1)

            @block.tensor
            def _(pe):
                pe.sem_inc(s["turned"], 2)
                with pe.Fori(0, NBLK // 2) as i:
                    for j in range(2):
                        b = i * 2 + j
                        pe.wait_ge(s["xs"], b + 1)
                        pe.wait_ge(s["turned_sb"], b + 1)
                        for k in range(TB):
                            mm = pe.transpose(pst[j][:, k * P:(k + 1) * P], xs[j][:, k, :], G.ident[:])
                        mm.then_inc(s["turned"], 1)

            @block.scalar
            def _(act):
                act.preload_act_table(ACT.Copy)
                act.sem_inc(s["turned_sb"], 2)
                with act.Fori(0, NBLK // 2) as i:
                    for j in range(2):
                        b = i * 2 + j
                        act.wait_ge(s["turned"], b + 3)
                        act.activation(G.XF[:, bass.ds(b * TB * P, TB * P)], pst[j][:], ACT.Copy).then_inc(s["turned_sb"], 1)


def two_largest(dve, step, C, G, lg, w, iota):
    full = [P, NT, NE]
    e, idx = w["e"], w["idx"]
    for k in range(2):
        oh = w["oh"][k]
        step.then(dve.tensor_reduce(w["m"][:, k, :], lg, AX.X, ALU.max))
        step.then(dve.tensor_tensor(e[:], lg, wide(w["m"][:, k, :].unsqueeze(2), full), ALU.is_equal))
        step.then(dve.tensor_tensor(e[:], e[:], wide(iota[:].unsqueeze(1), full), ALU.mult))
        step.then(dve.tensor_reduce(idx[:], e[:], AX.X, ALU.min))
        step.then(dve.tensor_tensor(oh[:], wide(iota[:].unsqueeze(1), full), wide(idx[:].unsqueeze(2), full), ALU.is_equal))
        if k == 0:
            step.then(dve.scalar_tensor_tensor(lg, oh[:].rearrange("p n e -> p (n e)").rearrange("p (n e) -> p n e", e=NE), TAKEN, lg, ALU.mult, ALU.add))
    step.then(dve.tensor_tensor(w["d"][:], w["m"][:, 1, :], w["m"][:, 0, :], ALU.subtract))


def weigh(dve, step, w):
    step.then(dve.tensor_scalar(w["p"][:, 0, :], w["d"][:], 1.0, None, ALU.add))
    step.then(dve.reciprocal(w["p"][:, 0, :], w["p"][:, 0, :]))
    step.then(dve.tensor_tensor(w["p"][:, 1, :], w["d"][:], w["p"][:, 0, :], ALU.mult))
    full = [P, NT, NE]
    a, b = w["oh"]
    step.then(dve.tensor_tensor(w["e"][:], b[:], wide(w["p"][:, 1, :].unsqueeze(2), full), ALU.mult))
    step.then(dve.tensor_tensor(w["gate"], a[:], wide(w["p"][:, 0, :].unsqueeze(2), full), ALU.mult))
    step.then(dve.tensor_tensor(w["gate"], w["gate"], w["e"][:], ALU.add))


def routing_memory(C, ctx, tag, G):
    w = {"m": C.sb(tag + "m", [P, 2, NT], ctx=ctx), "e": C.sb(tag + "e", [P, NT, NE], ctx=ctx),
         "idx": C.sb(tag + "idx", [P, NT], ctx=ctx), "d": C.sb(tag + "d", [P, NT], ctx=ctx),
         "oh": [C.sb(tag + f"oh{k}", [P, NT, NE], ctx=ctx) for k in range(2)],
         "p": C.sb(tag + "p", [P, 2, NT], ctx=ctx), "gate": G.gate[:]}
    return w


def first_router(nc, C, A, G):
    rb1 = VEC["L0_ffn_rb1"][0]
    with ExitStack() as ctx:
        w1 = C.sb("rw1", [D, HID], ctx=ctx)
        w2 = C.sb("rw2", [P, 4, NE], ctx=ctx)
        b2 = C.sb("rb2", [P, NE], ctx=ctx)
        hs = [C.sb(f"rt_hs{j}", [P, 4, TB * P], ctx=ctx) for j in range(2)]
        lg = C.sb("rt_lg", [P, NT, NE], ctx=ctx)
        sel = C.sb("rt_sel", [P, NT, NE], ctx=ctx)
        run = [C.sb(f"rt_run{k}", [P, NT, NE], ctx=ctx) for k in range(2)]
        base = C.sb("rt_base", [P, NE], ctx=ctx)
        spare_i = C.sb("rt_spare_i", [P, 2, NT], dt=I32, ctx=ctx)
        spare = C.sb("rt_spare", [P, 2, NT], ctx=ctx)
        zeros = C.sb("rt_zeros", [P, 4, 2 * D], ctx=ctx)
        w = routing_memory(C, ctx, "rt_", G)
        psh = [C.ps(f"rt_psh{c}", [P, TB * P], ctx) for c in range(4)]
        psl = [C.ps(f"rt_psl{j}", [P, TB, NE], ctx) for j in range(2)]
        psp = C.ps("rt_psp", [P, NT, NE], ctx)
        s = {n: C.sem("rt_" + n) for n in ("weights", "logits", "logits_sb", "d", "exp", "sel", "pos", "dve", "spare", "zeros", "cleared")}
        h_ps = [C.sem(f"rt_h_ps{c}") for c in range(4)]
        h_sb = [C.sem(f"rt_h_sb{c}") for c in range(4)]
        with nc.Block() as block:

            @block.sync
            def _(sp):
                sp.dma_start(w1[:], A["L0_ffn_rw1"]).then_inc(s["weights"], 16)
                sp.dma_start(w2[:], A["L0_ffn_rw2"].rearrange("(c p) e -> p c e", p=P)).then_inc(s["weights"], 16)
                sp.dma_start(b2[:], A["L0_ffn_rb2"].partition_broadcast(P)).then_inc(s["weights"], 16)
                sp.wait_ge(s["zeros"], 1)
                z = zeros[:].rearrange("p a d -> p (a d)")
                for k in range(NE * CAP // P // 8):
                    sp.dma_start(G.slots_in[k * 8 * P:(k + 1) * 8 * P, :].rearrange("(p r) d -> p (r d)", p=P), z).then_inc(s["cleared"], 16)
                sp.wait_ge(s["cleared"], NE * CAP // P // 8 * 16)

            @block.gpsimd
            def _(pool):
                pool.memset(zeros[:], 0.0).then_inc(s["zeros"], 1)
                pool.iota(spare_i[:], pattern=[[P * NT, 2], [P, NT]], base=NE * CAP, channel_multiplier=1).then_inc(s["spare"], 1)

            @block.tensor
            def _(pe):
                pe.sem_inc(s["logits"], 2)
                pe.wait_ge(s["weights"], 48)
                with pe.Fori(0, NBLK // 2) as i:
                    for j in range(2):
                        b = i * 2 + j
                        for c in range(4):
                            pe.wait_ge(h_sb[c], b + 1)
                            pe.matmul(psh[c][:], w1[:, c * P:(c + 1) * P], G.XF[:, bass.ds(b * TB * P, TB * P)],
                                      start=True, stop=True).then_inc(h_ps[c], 1)
                        pe.wait_ge(s["logits_sb"], b + 1)
                        for c in range(4):
                            pe.wait_ge(h_sb[c], b + 2)
                            for k in range(TB):
                                mm = pe.matmul(psl[j][:, k, :], hs[j][:, c, k * P:(k + 1) * P], w2[:, c, :],
                                               start=(c == 0 and k == 0), stop=(c == 3), skip_group_check=True)
                        mm.then_inc(s["logits"], 1)
                pe.wait_ge(s["sel"], 1)
                pe.matmul(psp[:], G.triu[:], sel[:], start=True, stop=False)
                pe.matmul(psp[:], G.ones[:], run[1][:], start=False, stop=True).then_inc(s["pos"], 1)

            @block.scalar
            def _(act):
                act.preload_act_table(ACT.Exp)
                for c in range(4):
                    act.sem_inc(h_sb[c], 1)
                with act.Fori(0, NBLK // 2) as i:
                    for j in range(2):
                        b = i * 2 + j
                        act.wait_ge(s["logits"], b + 1)
                        for c in range(4):
                            act.wait_ge(h_ps[c], b + 1)
                            act.activation(hs[j][:, c, :], psh[c][:], ACT.Relu,
                                           bias=G.vec[:, rb1 + c:rb1 + c + 1]).then_inc(h_sb[c], 1)
                act.wait_ge(s["d"], 1)
                act.activation(w["d"][:], w["d"][:], ACT.Exp).then_inc(s["exp"], 1)

            @block.vector
            def _(dve):
                dve.sem_inc(s["logits_sb"], 2)
                step = Steps(dve, s["dve"])
                dve.wait_ge(s["weights"], 48)
                with dve.Fori(0, NBLK // 2) as i:
                    for j in range(2):
                        b = i * 2 + j
                        dve.wait_ge(s["logits"], b + 3)
                        dve.tensor_tensor(lg[:, bass.ds(b * TB, TB), :], psl[j][:], wide(b2[:].unsqueeze(1), [P, TB, NE]),
                                          ALU.add).then_inc(s["logits_sb"], 1)
                dve.wait_ge(s["logits_sb"], NBLK + 2)
                two_largest(dve, step, C, G, lg[:], w, G.iota8)
                dve.sem_inc(s["d"], 1)
                step.then(dve.tensor_tensor(sel[:], w["oh"][0][:], w["oh"][1][:], ALU.add))
                dve.memset(run[0][:, 0, :], 0.0)
                step.then(dve.tensor_copy(run[0][:, 1:NT, :], sel[:, 0:NT - 1, :]))
                src, k = 0, 1
                while k < NT:
                    dve.tensor_copy(run[1 - src][:, 0:k, :], run[src][:, 0:k, :])
                    step.then(dve.tensor_tensor(run[1 - src][:, k:NT, :], run[src][:, k:NT, :], run[src][:, 0:NT - k, :], ALU.add))
                    src, k = 1 - src, 2 * k
                assert src == 1
                dve.sem_inc(s["sel"], 1)
                dve.wait_ge(s["exp"], 1)
                weigh(dve, step, w)
                dve.wait_ge(s["pos"], 1)
                step.then(dve.tensor_scalar(w["e"][:], psp[:], float(CAP), None, ALU.is_lt))
                step.then(dve.tensor_tensor(G.gate[:], G.gate[:], w["e"][:], ALU.mult))
                dve.wait_ge(s["spare"], 1)
                step.did(dve.tensor_copy(spare[:], spare_i[:]))
                step.then(dve.tensor_scalar(base[:], G.iota8[:], float(CAP), float(NE * CAP), ALU.mult, ALU.add))
                step.then(dve.tensor_tensor(sel[:], psp[:], wide(base[:].unsqueeze(1), [P, NT, NE]), ALU.add))
                slot, keep = w["m"][:, 0, :], w["m"][:, 1, :]
                for k in range(2):
                    oh = w["oh"][k]
                    step.then(dve.tensor_tensor(lg[:], oh[:], sel[:], ALU.mult))
                    step.then(dve.tensor_reduce(slot, lg[:], AX.X, ALU.add))
                    step.then(dve.tensor_tensor(lg[:], oh[:], w["e"][:], ALU.mult))
                    step.then(dve.tensor_reduce(keep, lg[:], AX.X, ALU.add))
                    step.did(dve.tensor_tensor(G.prob[:, k, :], w["p"][:, k, :], keep, ALU.mult))
                    step.then(dve.tensor_tensor(slot, slot, keep, ALU.mult))
                    step.did(dve.tensor_copy(G.slot_out[:, k, :], slot))
                    step.then(dve.tensor_tensor(keep, spare[:, k, :], keep, ALU.mult))
                    step.then(dve.tensor_tensor(keep, spare[:, k, :], keep, ALU.subtract))
                    step.then(dve.tensor_tensor(slot, slot, keep, ALU.add))
                    step.then(dve.tensor_copy(G.slot_in[:, k, :], slot))


def add_gated_biases(nc, C, A, G, tag, name, beside=None):
    with ExitStack() as ctx:
        gs = C.sb(tag + "gs", [P, NBLK, TB, 32], ctx=ctx)
        gt = C.sb(tag + "gt", [P, NBLK, P], ctx=ctx)
        bd = C.sb(tag + "bd", [P, TB, D], ctx=ctx)
        pst = [C.ps(f"{tag}pst{j}", [P, NBLK // 2, P], ctx) for j in range(2)]
        psy = [C.ps(f"{tag}psy{j}", [P, TB, D], ctx) for j in range(6)]
        s = {n: C.sem(tag + n) for n in ("zero", "loaded", "gs", "turned", "turned_sb", "y", "x")}
        with nc.Block() as block:

            @block.gpsimd
            def _(pool):
                pool.memset(gs[:], 0.0).then_inc(s["zero"], 1)
                pool.memset(bd[:], 0.0).then_inc(s["zero"], 1)
                if beside:
                    beside(pool)

            @block.sync
            def _(sp):
                sp.wait_ge(s["zero"], 2)
                for k in range(TB):
                    sp.dma_start(bd[32 * k:32 * k + NE, k, :], A[name]).then_inc(s["loaded"], 16)

            @block.tensor
            def _(pe):
                pe.wait_ge(s["gs"], 1)
                for half in range(2):
                    for k in range(NBLK // 2):
                        b = half * (NBLK // 2) + k
                        mm = pe.transpose(pst[half][:, k, :], gs[:, b, :, :].rearrange("p k e -> p (k e)"), G.ident[:])
                    mm.then_inc(s["turned"], 1)
                pe.wait_ge(s["loaded"], 64)
                for b in range(NBLK):
                    pe.wait_ge(s["turned_sb"], b // (NBLK // 2) + 1)
                    after(pe, s["x"], b - len(psy) + 1)
                    pe.matmul(psy[b % len(psy)][:], gt[:, b, :], bd[:], start=True, stop=True).then_inc(s["y"], 1)

            @block.scalar
            def _(act):
                for half in range(2):
                    act.wait_ge(s["turned"], half + 1)
                    act.activation(gt[:, half * NBLK // 2:(half + 1) * NBLK // 2, :], pst[half][:], ACT.Copy).then_inc(s["turned_sb"], 1)

            @block.vector
            def _(dve):
                dve.wait_ge(s["zero"], 1)
                dve.tensor_copy(gs[:, :, :, 0:NE], G.gate[:].rearrange("p (b k) e -> p b k e", k=TB)).then_inc(s["gs"], 1)
                for b in range(NBLK):
                    dve.wait_ge(s["y"], b + 1)
                    rows = G.X[:, b * TB:(b + 1) * TB, :]
                    dve.tensor_tensor(rows, rows, psy[b % len(psy)][:], ALU.add).then_inc(s["x"], 1)


def send_rows(C, G):
    sent = C.sem("rows_sent")

    def send(pool):
        for t in range(NT):
            for k in range(2):
                pool.indirect_dma_start(G.slots_in, bass.IndirectOffsetOnAxis(ap=G.slot_in[:, k, t:t + 1], axis=0),
                                        G.XT[:, t, :], None).then_inc(sent, 16)
        pool.wait_ge(sent, 2 * NT * 16)

    return send


def first_experts(nc, C, A, G):
    eb1 = VEC["L0_ffn_eb1"][0]
    S = CAP // P
    Q = 4
    with ExitStack() as ctx:
        w1 = [C.sb(f"ew1{j}", [D, HID], ctx=ctx) for j in range(2)]
        w2 = [C.sb(f"ew2{j}", [P, 4, D], ctx=ctx) for j in range(2)]
        xr = [C.sb(f"ex_rows{j}", [P, S, D], ctx=ctx) for j in range(2)]
        xt = [C.sb(f"ex_turned{j}", [D, CAP], ctx=ctx) for j in range(2)]
        hs = [C.sb(f"ex_hs{j}", [P, 4, CAP], ctx=ctx) for j in range(2)]
        ys = [C.sb(f"ex_ys{j}", [P, S, D], ctx=ctx) for j in range(2)]
        gathered = [G.XT[:], G.XF[:].rearrange("p (n d) -> p n d", d=D)]
        psh = [C.ps(f"ex_psh{c}", [P, CAP], ctx) for c in range(4)]
        pst = C.ps("ex_pst", [P, CAP], ctx)
        psy = [C.ps(f"ex_psy{j}", [P, S, D], ctx) for j in range(2)]
        s = {n: C.sem("ex_" + n) for n in ("turned", "turned_sb", "y", "y_sb", "summed")}
        h_ps = [C.sem(f"ex_h_ps{c}") for c in range(4)]
        h_sb = [C.sem(f"ex_h_sb{c}") for c in range(4)]
        loaded = [C.sem(f"ex_weights{j}") for j in range(2)]
        rows = [C.sem(f"ex_rows_loaded{j}") for j in range(2)]
        kept = [C.sem(f"ex_kept{j}") for j in range(2)]
        fetched = [C.sem(f"ex_fetched{q}") for q in range(Q)]
        slots_in = G.slots_in[0:NE * CAP, :].rearrange("(e k p) d -> e p k d", p=P, k=S)
        slots_out = G.slots_out.rearrange("(e k p) d -> e p k d", p=P, k=S)
        with nc.Block() as block:

            @block.sync
            def _(sp):
                for e in range(NE):
                    j = e % 2
                    if e >= 2:
                        sp.wait_ge(s["y"], e - 1)
                    sp.dma_start(xr[j][:], slots_in[e]).then_inc(rows[j], 16)
                    sp.dma_start(w1[j][:], A["L0_ffn_ew1"][e]).then_inc(loaded[j], 16)
                    sp.dma_start(w2[j][:], A["L0_ffn_ew2"][e].rearrange("(c p) d -> p c d", p=P)).then_inc(loaded[j], 16)
                    if e >= 2:
                        sp.wait_ge(s["y_sb"], e - 1)
                        sp.dma_start(slots_out[e - 2], ys[j][:]).then_inc(kept[j], 16)
                for e in (NE - 2, NE - 1):
                    sp.wait_ge(s["y_sb"], e + 1)
                    sp.dma_start(slots_out[e], ys[e % 2][:]).then_inc(kept[e % 2], 16)

            @block.gpsimd
            def _(pool):
                for j in range(2):
                    pool.wait_ge(kept[j], NE // 2 * 16)
                for t in range(NT):
                    for k in range(2):
                        pool.indirect_dma_start(gathered[k][:, t, :], None, G.slots_out,
                                                bass.IndirectOffsetOnAxis(ap=G.slot_out[:, k, t:t + 1], axis=0)
                                                ).then_inc(fetched[t // (NT // Q)], 16)

            @block.tensor
            def _(pe):
                def turn(e):
                    pe.wait_ge(rows[e % 2], (e // 2 + 1) * 16)
                    after(pe, s["turned_sb"], e)
                    for k in range(S):
                        mm = pe.transpose(pst[:, k * P:(k + 1) * P], xr[e % 2][:, k, :], G.ident[:])
                    mm.then_inc(s["turned"], 1)

                turn(0)
                for e in range(NE):
                    j = e % 2
                    pe.wait_ge(loaded[j], (e // 2 + 1) * 32)
                    pe.wait_ge(s["turned_sb"], e + 1)
                    for c in range(4):
                        after(pe, h_sb[c], e)
                        pe.matmul(psh[c][:], w1[j][:, c * P:(c + 1) * P], xt[j][:], start=True, stop=True).then_inc(h_ps[c], 1)
                    if e + 1 < NE:
                        turn(e + 1)
                    after(pe, s["y_sb"], e - 1)
                    for c in range(4):
                        pe.wait_ge(h_sb[c], e + 1)
                        for k in range(S):
                            mm = pe.matmul(psy[j][:, k, :], hs[j][:, c, k * P:(k + 1) * P], w2[j][:, c, :],
                                           start=(c == 0 and k == 0), stop=(c == 3), skip_group_check=True)
                    mm.then_inc(s["y"], 1)

            @block.scalar
            def _(act):
                act.preload_act_table(ACT.Relu)
                for e in range(NE):
                    after(act, s["y"], e - 1)
                    for c in range(4):
                        act.wait_ge(h_ps[c], e + 1)
                        v = eb1 + 4 * e + c
                        act.activation(hs[e % 2][:, c, :], psh[c][:], ACT.Relu, bias=G.vec[:, v:v + 1]).then_inc(h_sb[c], 1)

            @block.vector
            def _(dve):
                def keep_rows(e):
                    dve.wait_ge(s["y"], e + 1)
                    after(dve, kept[e % 2], e // 2 * 16)
                    dve.tensor_copy(ys[e % 2][:], psy[e % 2][:]).then_inc(s["y_sb"], 1)

                for e in range(NE):
                    dve.wait_ge(s["turned"], e + 1)
                    dve.tensor_copy(xt[e % 2][:], pst[:]).then_inc(s["turned_sb"], 1)
                    if e > 0:
                        keep_rows(e - 1)
                keep_rows(NE - 1)
                for q in range(Q):
                    dve.wait_ge(fetched[q], NT // Q * 2 * 16)
                    for k in range(2):
                        for t in range(q * NT // Q, (q + 1) * NT // Q):
                            row = G.X[:, t, :]
                            m = dve.scalar_tensor_tensor(row, gathered[k][:, t, :], G.prob[:, k, t:t + 1], row, ALU.mult, ALU.add)
                        m.then_inc(s["summed"], 1)
                        dve.wait_ge(s["summed"], 2 * q + k + 1)


def second_attention(nc, C, A, G):
    bqi, bki, bvi = (VEC["L1_xattn_" + n][0] for n in ("bq", "bk", "bv"))
    HG = 4
    W = 2 * (DH1 + 1)
    with ExitStack() as ctx:
        def two(name, shape):
            return [C.sb(f"a1_{name}{j}", shape, ctx=ctx) for j in range(2)]

        wq, wk, wv, wo = (C.sb("a1_w" + n, [k, D], ctx=ctx) for n, k in (("q", D), ("k", DC), ("v", DC), ("o", D)))
        bo = C.sb("a1_bo", [P, D], ctx=ctx)
        sca = C.sb("a1_scale", [P, 1], ctx=ctx)
        bqs = C.sb("a1_bqs", [P, 1], ctx=ctx)
        m4 = C.sb("a1_m4", [P, HG], ctx=ctx)
        bk4 = C.sb("a1_bk4", [P, HG], ctx=ctx)
        c2, vb = two("c2", [DC, 2, 2, T]), two("vb", [P, 2, H1 // 2, 2, DH1 + 1])
        qt, kb = two("qt", [P, P]), two("kb", [P, 2, HG, T])
        mx, dd, pp = two("mx", [P, H1]), two("dd", [P, H1, T]), two("pp", [P, H1, T])
        pt = two("pt", [P, H1 // 2, P])
        rc, oo, of = two("rc", [P, H1]), two("oo", [P, H1, DH1]), two("of", [P, P])
        psx = C.ps("a1_psx", [P, 512], ctx)
        pss = [C.ps(f"a1_pss{h}", [P, 2, 512], ctx) for h in range(2)]
        psp = [C.ps(f"a1_psp{h}", [P, 4, P], ctx) for h in range(2)]
        pso = C.ps("a1_pso", [P, 512], ctx)
        s = {n: C.sem("a1_" + n) for n in (
            "weights", "ready", "zero", "c2", "qk", "qk_sb", "v", "v_sb", "scores", "scores_sb", "exp",
            "turned", "turned_sb", "o", "o_sb", "o_turned", "of", "y", "x", "dve", "pool")}
        with nc.Block() as block:
            SWEEP = (-2, 3, 29, NT + 1)

            @block.sync
            def _(sp):
                for dst, name in ((wq, "Wq"), (wk, "Wk"), (wv, "Wv"), (wo, "Wo")):
                    sp.dma_start(dst[:], A["L1_xattn_" + name]).then_inc(s["weights"], 16)
                sp.dma_start(bo[:], A["L1_xattn_bo"].partition_broadcast(P)).then_inc(s["weights"], 16)
                sp.dma_start(sca[:], A["L1_xattn_scale"].partition_broadcast(P)).then_inc(s["weights"], 16)

            @block.gpsimd
            def _(pool):
                step = Steps(pool, s["pool"])
                step.then(pool.memset(m4[:], 1.0))
                for g in range(4):
                    rows = m4[32 * g:32 * g + 32, :]
                    step.then(pool.affine_select(out=rows, in_=rows, compare_op=ALU.is_ge, fill=0.0,
                                                 base=0, pattern=[[-DH1, HG]], channel_multiplier=1))
                    step.then(pool.affine_select(out=rows, in_=rows, compare_op=ALU.is_ge, fill=0.0,
                                                 base=DH1 - 1, pattern=[[DH1, HG]], channel_multiplier=-1))
                for j in range(2):
                    step.did(pool.memset(vb[j][:], 0.0))
                step.wait()
                for j in range(2):
                    step.did(pool.memset(vb[j][0:T, :, :, 0, DH1:DH1 + 1], 1.0))
                    step.did(pool.memset(vb[j][T:P, :, :, 1, DH1:DH1 + 1], 1.0))
                step.wait()
                pool.sem_inc(s["zero"], 1)

                def slot(x):
                    g = x.by(1)
                    if g.real():
                        after(pool, s["v"], g.t - 1)
                        src = G.ctxT[:, bass.ds(g.t * P, P)].rearrange("p (b k) -> p b k", b=2)
                        pool.tensor_copy(c2[g.j][:, :, 0, :], src)
                        pool.tensor_copy(c2[g.j][:, :, 1, :], src).then_inc(s["c2"], 1)

                sweep(pool, slot, *SWEEP)

            @block.tensor
            def _(pe):
                pe.wait_ge(s["weights"], 96)

                def scores(g, half):
                    if not g.real():
                        return
                    j = g.j
                    if half == 0:
                        pe.wait_ge(s["qk_sb"], g.t + 1)
                    after(pe, s["scores_sb"], g.t * 2 + half - 1)
                    for b in range(2):
                        for h in range(2):
                            rows = slice(64 * half + 32 * h, 64 * half + 32 * h + 32)
                            mm = pe.matmul(pss[half][T * b:T * b + T, h, 0:HG * T], qt[j][rows, T * b:T * b + T],
                                           kb[j][rows, b, :, :], start=True, stop=True)
                    mm.then_inc(s["scores"], 1)

                def slot(x):
                    a, g, c = x.by(2), x.by(1), x.by(-1)
                    scores(g, 0)
                    if c.real():
                        pe.wait_ge(s["o_sb"], c.t + 1)
                        pe.transpose(pso[:, 384:512], oo[c.j][:].rearrange("p h d -> p (h d)"), G.ident[:]).then_inc(s["o_turned"], 1)
                    if a.real():
                        tok = bass.ds(a.t * P, P)
                        after(pe, s["v_sb"], a.t - 1)
                        after(pe, s["qk_sb"], a.t)
                        pe.matmul(psx[:, 0:P], wq[:], G.XF[:, tok], start=True, stop=True)
                        pe.matmul(psx[:, P:2 * P], wk[:], G.ctxT[:, tok], start=True, stop=True).then_inc(s["qk"], 1)
                    if g.real():
                        pe.wait_ge(s["c2"], g.t + 1)
                        after(pe, s["v_sb"], g.t)
                        for b in range(2):
                            mm = pe.matmul(psx[:, 256 + P * b:256 + P * b + P], c2[g.j][:, b, :, :], wv[:], start=True, stop=True)
                        mm.then_inc(s["v"], 1)
                    if c.real():
                        pe.wait_ge(s["of"], c.t + 1)
                        pe.matmul(pso[:, 384:512], of[c.j][:], wo[:], start=True, stop=True).then_inc(s["y"], 1)
                    if x.real():
                        for half in range(2):
                            pe.wait_ge(s["exp"], x.t * 2 + half + 1)
                            after(pe, s["turned_sb"], x.t * 2 + half - 1)
                            for k in range(4):
                                h = 8 * half + 2 * k
                                mm = pe.transpose(psp[half][:, k, :], pp[x.j][:, h:h + 2, :].rearrange("p h k -> p (h k)"), G.ident[:])
                            mm.then_inc(s["turned"], 1)
                    scores(g, 1)
                    if x.real():
                        pe.wait_ge(s["turned_sb"], x.t * 2 + 2)
                        pe.wait_ge(s["v_sb"], x.t + 1)
                        after(pe, s["x"], x.t)
                        for k in range(H1 // 2):
                            mm = pe.matmul(pso[:, 2 * W * k:2 * W * k + 2 * W], pt[x.j][:, k, :], vb[x.j][:, :, k, :, :],
                                           start=True, stop=True)
                        mm.then_inc(s["o"], 1)

                sweep(pe, slot, *SWEEP)

            @block.scalar
            def _(act):
                act.preload_act_table(ACT.Exp)
                act.wait_ge(s["ready"], 1)
                act.wait_ge(s["zero"], 1)
                ident = ACT.Identity

                def exp(x, half):
                    if x.real():
                        act.wait_ge(s["scores_sb"], x.t * 2 + half + 1)
                        h = slice(8 * half, 8 * half + 8)
                        act.activation(pp[x.j][:, h, :], dd[x.j][:, h, :], ACT.Exp).then_inc(s["exp"], 1)

                def slot(x):
                    a, g, c = x.by(2), x.by(1), x.by(-1)
                    exp(x, 1)
                    if c.real():
                        act.wait_ge(s["o_turned"], c.t + 1)
                        act.activation(of[c.j][:], pso[:, 384:512], ident, bias=G.vec[:, bvi:bvi + 1]).then_inc(s["of"], 1)
                    if g.real():
                        act.wait_ge(s["v"], g.t + 1)
                    if a.real():
                        act.wait_ge(s["qk"], a.t + 1)
                        act.activation(qt[a.j][:], psx[:, 0:P], ident, scale=sca[:, 0:1], bias=bqs[:, 0:1])
                        k = psx[:, P:2 * P].rearrange("p (b k) -> p b k", b=2)
                        for h in range(HG):
                            m = act.activation(kb[a.j][:, :, h, :], k, ident, scale=m4[:, h:h + 1], bias=bk4[:, h:h + 1])
                        m.then_inc(s["qk_sb"], 1)
                    if g.real():
                        v = psx[:, 256:512].rearrange("p (b k c d) -> p b k c d", b=2, c=2, d=DH1)
                        act.activation(vb[g.j][0:T, :, :, 0, 0:DH1], v[0:T, :, :, 0, :], ACT.Copy)
                        act.activation(vb[g.j][T:P, :, :, 1, 0:DH1], v[T:P, :, :, 1, :], ACT.Copy).then_inc(s["v_sb"], 1)
                    if x.real():
                        for half in range(2):
                            act.wait_ge(s["turned"], x.t * 2 + half + 1)
                            act.activation(pt[x.j][:, 4 * half:4 * half + 4, :], psp[half][:], ACT.Copy).then_inc(s["turned_sb"], 1)
                    exp(g, 0)

                sweep(act, slot, *SWEEP)

            @block.vector
            def _(dve):
                step = Steps(dve, s["dve"])
                dve.wait_ge(s["weights"], 96)
                dve.wait_ge(s["zero"], 1)
                dve.tensor_scalar(bqs[:], G.vec[:, bqi:bqi + 1], sca[:, 0:1], None, ALU.mult)
                step.then(dve.tensor_scalar(bk4[:], m4[:], G.vec[:, bki:bki + 1], None, ALU.mult))
                dve.sem_inc(s["ready"], 1)
                step.then(dve.tensor_tensor(G.X[:], G.X[:], wide(bo[:].unsqueeze(1), [P, NT, D]), ALU.add))
                step.clear()

                def centre(g, half):
                    if not g.real():
                        return
                    heads = slice(8 * half, 8 * half + 8)
                    dve.wait_ge(s["scores"], g.t * 2 + half + 1)
                    src = pss[half][:, :, 0:HG * T].rearrange("p g (h k) -> p g h k", h=HG)
                    m = mx[g.j][:, heads].rearrange("p (g h) -> p g h", g=2)
                    step.then(dve.tensor_reduce(m, src, AX.X, ALU.max))
                    after(dve, s["exp"], g.t * 2 + half - 3)
                    out = dd[g.j][:, heads, :].rearrange("p (g h) k -> p g h k", g=2)
                    dve.tensor_tensor(out, src, wide(m.unsqueeze(3), [P, 2, HG, T]), ALU.subtract).then_inc(s["scores_sb"], 1)

                def slot(x):
                    g, c = x.by(1), x.by(-1)
                    if c.real():
                        dve.wait_ge(s["o"], c.t + 1)
                        o = pso[:, 0:2 * W * (H1 // 2)].rearrange("p (k b c d) -> p b k c d", b=2, c=2, d=DH1 + 1)
                        r = rc[c.j][:].rearrange("p (k c) -> p k c", c=2)
                        y = oo[c.j][:].rearrange("p (k c) d -> p k c d", c=2)
                        for b in range(2):
                            rows = slice(T * b, T * b + T)
                            step.did(dve.reciprocal(r[rows], o[rows, b, :, :, DH1]))
                        step.wait()
                        for b in range(2):
                            rows = slice(T * b, T * b + T)
                            m = dve.tensor_tensor(y[rows], o[rows, b, :, :, 0:DH1], wide(r[rows].unsqueeze(3), [T, H1 // 2, 2, DH1]), ALU.mult)
                        m.then_inc(s["o_sb"], 1)
                    centre(g, 0)
                    if c.real():
                        dve.wait_ge(s["y"], c.t + 1)
                        row = G.X[:, c.t, :]
                        dve.tensor_tensor(row, row, pso[:, 384:512], ALU.add).then_inc(s["x"], 1)
                    centre(g, 1)
                    if g.real() or c.real():
                        step.clear()

                sweep(dve, slot, *SWEEP)


def second_router(nc, C, A, G):
    with ExitStack() as ctx:
        wg = C.sb("g1_wg", [NE, D], ctx=ctx)
        wgt = C.sb("g1_wgt", [D, NE], ctx=ctx)
        xl = [C.sb(f"g1_xl{j}", [D, TB * P], ctx=ctx) for j in range(2)]
        lg = C.sb("g1_lg", [P, NT, NE], ctx=ctx)
        w = routing_memory(C, ctx, "g1_", G)
        psw = C.ps("g1_psw", [P, NE], ctx)
        psl = [C.ps(f"g1_psl{j}", [P, TB, NE], ctx) for j in range(2)]
        s = {n: C.sem("g1_" + n) for n in ("wg", "wg_ps", "wg_sb", "xl", "logits", "logits_sb", "d", "exp", "dve")}
        with nc.Block() as block:

            @block.sync
            def _(sp):
                sp.dma_start(wg[:], A["L1_ffn_Wg"]).then_inc(s["wg"], 16)

            @block.tensor
            def _(pe):
                pe.sem_inc(s["logits"], 2)
                pe.wait_ge(s["wg"], 16)
                pe.transpose(psw[:], wg[:], G.ident[0:NE, 0:NE]).then_inc(s["wg_ps"], 1)
                pe.wait_ge(s["wg_sb"], 1)
                with pe.Fori(0, NBLK // 2) as i:
                    for j in range(2):
                        b = i * 2 + j
                        pe.wait_ge(s["xl"], b + 1)
                        pe.wait_ge(s["logits_sb"], b + 1)
                        for k in range(TB):
                            mm = pe.matmul(psl[j][:, k, :], xl[j][:, k * P:(k + 1) * P], wgt[:], start=True, stop=True)
                        mm.then_inc(s["logits"], 1)

            @block.scalar
            def _(act):
                act.preload_act_table(ACT.Exp)
                act.wait_ge(s["wg_ps"], 1)
                act.activation(wgt[:], psw[:], ACT.Copy).then_inc(s["wg_sb"], 1)
                with act.Fori(0, NBLK // 2) as i:
                    for j in range(2):
                        b = i * 2 + j
                        act.wait_ge(s["logits"], b + 1)
                        act.activation(xl[j][:], G.XF[:, bass.ds(b * TB * P, TB * P)], ACT.Copy).then_inc(s["xl"], 1)
                act.wait_ge(s["d"], 1)
                act.activation(w["d"][:], w["d"][:], ACT.Exp).then_inc(s["exp"], 1)

            @block.vector
            def _(dve):
                dve.sem_inc(s["logits_sb"], 2)
                step = Steps(dve, s["dve"])
                with dve.Fori(0, NBLK // 2) as i:
                    for j in range(2):
                        b = i * 2 + j
                        dve.wait_ge(s["logits"], b + 3)
                        dve.tensor_copy(lg[:, bass.ds(b * TB, TB), :], psl[j][:]).then_inc(s["logits_sb"], 1)
                dve.wait_ge(s["logits_sb"], NBLK + 2)
                two_largest(dve, step, C, G, lg[:], w, G.iota8)
                dve.sem_inc(s["d"], 1)
                dve.wait_ge(s["exp"], 1)
                weigh(dve, step, w)


def second_experts(nc, C, A, G):
    b1i, b3i = VEC["L1_ffn_b1"][0], VEC["L1_ffn_b3"][0]
    NC = HE // P
    with ExitStack() as ctx:
        def two(name, shape, dt=F32):
            return [C.sb(f"e1_{name}{j}", shape, dt, ctx=ctx) for j in range(2)]

        wr = two("wr", [P, 2, NC, D])
        w2r = two("w2r", [D, HE])
        br = two("br", [P, 2, NC, R])
        b2r = two("b2r", [D, R])
        ar = two("ar", [R, 2, D])
        a2 = two("a2", [R, HE])
        bt = two("bt", [R, 2 * NC + 1, P])
        wf, wh, wl = (two(n, [D, 2, NC, P], dt) for n, dt in (("wf", F32), ("wh", F32R), ("wl", F32R)))
        w2 = two("w2", [P, NC, D])
        XH, XL = C.sb("e1_XH", [D, B * T], F32R, ctx=ctx), C.sb("e1_XL", [D, B * T], F32R, ctx=ctx)
        sg = two("sg", [P, NC, TB * P])
        hh = two("hh", [P, NC, TB * P])
        psb = C.ps("e1_psb", [P, 512], ctx)
        psb2 = C.ps("e1_psb2", [P, 512], ctx)
        psh = [[C.ps(f"e1_ps{m}{c}", [P, TB * P], ctx) for c in range(NC)] for m in (1, 3)]
        psy = [C.ps(f"e1_psy{j}", [P, TB, D], ctx) for j in range(2)]
        s = {n: C.sem("e1_" + n) for n in ("bt", "bt_sb", "w", "w_sb", "w_high", "w_low", "x_high", "x_low", "y", "y_sum")}
        loaded = [C.sem(f"e1_weights{j}") for j in range(2)]
        h_ps = [[C.sem(f"e1_h{m}_ps{c}") for c in range(NC)] for m in (1, 3)]
        silu = [C.sem(f"e1_silu{c}") for c in range(NC)]
        hh_sb = [C.sem(f"e1_hh{c}") for c in range(NC)]
        with nc.Block() as block:
            def experts(eng, slot, fold):
                fold(0, 0)
                fold(0, 1)
                for e in range(NE):
                    for b in range(2):
                        slot(e, b, e * NBLK + b, b % 2)
                    if e + 1 < NE:
                        fold(e + 1, 0)
                    with eng.Fori(0, (NBLK - 4) // 2) as i:
                        for j in range(2):
                            slot(e, i * 2 + (2 + j), i * 2 + (e * NBLK + 2 + j), j)
                    if e + 1 < NE:
                        fold(e + 1, 1)
                    for b in range(NBLK - 2, NBLK):
                        slot(e, b, e * NBLK + b, b % 2)

            @block.sync
            def _(sp):
                for e in range(NE):
                    j = e % 2
                    if e >= 2:
                        sp.wait_ge(s["w"], e - 1)
                    for m, (W, Bn, An) in enumerate((("W1", "B1", "A1"), ("W3", "B3", "A3"))):
                        sp.dma_start(wr[j][:, m, :, :], A["L1_ffn_" + W][e].rearrange("(c p) d -> p c d", p=P)).then_inc(loaded[j], 16)
                        sp.dma_start(br[j][:, m, :, :], A["L1_ffn_" + Bn][e].rearrange("(c p) r -> p c r", p=P)).then_inc(loaded[j], 16)
                        sp.dma_start(ar[j][:, m, :], A["L1_ffn_" + An][e]).then_inc(loaded[j], 16)
                    sp.dma_start(w2r[j][:], A["L1_ffn_W2"][e]).then_inc(loaded[j], 16)
                    sp.dma_start(b2r[j][:], A["L1_ffn_B2"][e]).then_inc(loaded[j], 16)
                    sp.dma_start(a2[j][:], A["L1_ffn_A2"][e]).then_inc(loaded[j], 16)

            @block.tensor
            def _(pe):
                def fold(e, step):
                    j = e % 2
                    if step == 0:
                        pe.wait_ge(loaded[j], (e // 2 + 1) * 9 * 16)
                        after(pe, s["w_sb"], e)
                        for m in range(2):
                            for c in range(NC):
                                k = m * NC + c
                                pe.transpose(psb[0:R, k * P:(k + 1) * P], br[j][:, m, c, :], G.ident[:])
                        pe.transpose(psb2[0:R, 0:P], b2r[j][:], G.ident[:]).then_inc(s["bt"], 1)
                        return
                    pe.wait_ge(s["bt_sb"], e + 1)
                    for m in range(2):
                        for c in range(NC):
                            k = m * NC + c
                            o = psb[:, k * P:(k + 1) * P]
                            pe.matmul(o, wr[j][:, m, c, :], G.ident[:], start=True, stop=False)
                            pe.matmul(o, ar[j][:, m, :], bt[j][:, k, :], start=False, stop=True)
                    for c in range(NC):
                        o = psb2[:, c * D:(c + 1) * D]
                        pe.matmul(o, w2r[j][:, c * P:(c + 1) * P], G.ident[:], start=True, stop=False)
                        mm = pe.matmul(o, a2[j][:, c * P:(c + 1) * P], bt[j][:, 2 * NC, :], start=False, stop=True)
                    mm.then_inc(s["w"], 1)

                def product(e, n, j):
                    after(pe, s["y_sum"], n - 1)
                    for c in range(NC):
                        pe.wait_ge(hh_sb[c], n + 1)
                        for k in range(TB):
                            mm = pe.matmul(psy[j][:, k, :], hh[j][:, c, k * P:(k + 1) * P], w2[e % 2][:, c, :],
                                           start=(c == 0 and k == 0), stop=(c == NC - 1), skip_group_check=True)
                    mm.then_inc(s["y"], 1)

                def slot(e, b, n, j):
                    if isinstance(b, int) and b == 0:
                        pe.wait_ge(s["w_low"], e + 1)
                    if e == 0:
                        pe.wait_ge(s["x_low"], b + 1)
                    x, xl = (m[:, bass.ds(b * TB * P, TB * P)] for m in (XH, XL))
                    for c in range(NC):
                        for m in range(2):
                            after(pe, hh_sb[c], n)
                            pe.matmul(psh[m][c][:], wh[e % 2][:, m, c, :], x, start=True, stop=False)
                            pe.matmul(psh[m][c][:], wh[e % 2][:, m, c, :], xl, start=False, stop=False)
                            pe.matmul(psh[m][c][:], wl[e % 2][:, m, c, :], x, start=False, stop=True).then_inc(h_ps[m][c], 1)
                    if isinstance(b, int) and b == 0:
                        if e > 0:
                            product(e - 1, n - 1, 1 - j)
                    else:
                        product(e, n - 1, 1 - j)

                experts(pe, slot, fold)
                product(NE - 1, NE * NBLK - 1, 1)

            @block.scalar
            def _(act):
                act.preload_act_table(ACT.Silu)

                def fold(e, step):
                    j = e % 2
                    if step == 0:
                        act.wait_ge(s["bt"], e + 1)
                        act.activation(bt[j][:, 0:2 * NC, :], psb[0:R, :].rearrange("r (k p) -> r k p", p=P), ACT.Copy)
                        act.activation(bt[j][:, 2 * NC, :], psb2[0:R, 0:P], ACT.Copy).then_inc(s["bt_sb"], 1)
                        return
                    act.wait_ge(s["w"], e + 1)
                    after(act, s["w_low"], e - 1)
                    act.activation(wf[j][:].rearrange("d m c p -> d (m c p)"), psb[:], ACT.Copy)
                    act.activation(w2[j][:].rearrange("p c d -> p (c d)"), psb2[:, 0:NC * D], ACT.Copy).then_inc(s["w_sb"], 1)

                def slot(e, b, n, j):
                    for c in range(NC):
                        k = b1i + NC * e + c
                        act.wait_ge(h_ps[0][c], n + 1)
                        act.activation(sg[j][:, c, :], psh[0][c][:], ACT.Silu, bias=G.vec[:, k:k + 1]).then_inc(silu[c], 1)

                experts(act, slot, fold)

            @block.gpsimd
            def _(pool):
                def fold(e, step):
                    if step == 1:
                        pool.wait_ge(s["w_high"], e + 1)
                        pool.tensor_tensor(wl[e % 2][:], wf[e % 2][:], wh[e % 2][:].bitcast(F32), ALU.subtract).then_inc(s["w_low"], 1)

                for b in range(NBLK):
                    t = slice(b * TB * P, (b + 1) * TB * P)
                    pool.wait_ge(s["x_high"], b + 1)
                    pool.tensor_tensor(XL[:, t], G.XF[:, t], XH[:, t].bitcast(F32), ALU.subtract).then_inc(s["x_low"], 1)
                for e in range(NE):
                    fold(e, 1)

            @block.vector
            def _(dve):
                def fold(e, step):
                    if step == 1:
                        dve.wait_ge(s["w_sb"], e + 1)
                        dve.tensor_copy(wh[e % 2][:], wf[e % 2][:]).then_inc(s["w_high"], 1)

                def take(e, b, n, j):
                    dve.wait_ge(s["y"], n + 1)
                    if e > 0:
                        after(dve, s["y_sum"], n + 1 - NBLK)
                    for k in range(TB):
                        row = G.X[:, bass.ds(b * TB + k, 1), :].rearrange("p a d -> p (a d)")
                        gate = G.gate[:, bass.ds(b * TB + k, 1), e:e + 1].rearrange("p a e -> p (a e)")
                        st = dve.scalar_tensor_tensor(row, psy[j][:, k, :], gate, row, ALU.mult, ALU.add)
                    st.then_inc(s["y_sum"], 1)

                def slot(e, b, n, j):
                    for c in range(NC):
                        k = b3i + NC * e + c
                        dve.wait_ge(h_ps[1][c], n + 1)
                        dve.wait_ge(silu[c], n + 1)
                        dve.scalar_tensor_tensor(hh[j][:, c, :], psh[1][c][:], G.vec[:, k:k + 1], sg[j][:, c, :],
                                                 ALU.add, ALU.mult).then_inc(hh_sb[c], 1)
                    if isinstance(b, int) and b == 0:
                        if e > 0:
                            take(e - 1, NBLK - 1, n - 1, 1 - j)
                    else:
                        take(e, b - 1, n - 1, 1 - j)

                for b in range(NBLK):
                    t = slice(b * TB * P, (b + 1) * TB * P)
                    dve.tensor_copy(XH[:, t], G.XF[:, t]).then_inc(s["x_high"], 1)
                experts(dve, slot, fold)
                take(NE - 1, NBLK - 1, NE * NBLK - 1, 1)


def store(nc, C, G):
    done = C.sem("stored")
    ov = G.out.rearrange("(n b) t d -> (b t) n d", b=2)
    with nc.Block() as block:

        @block.sync
        def _(sp):
            for k in range(4):
                sp.dma_start(ov[:, 8 * k:8 * k + 8, :], G.X[:, 8 * k:8 * k + 8, :]).then_inc(done, 16)
            sp.wait_ge(done, 64)


class Globals:
    pass


def program(nc, A, out, last=99):
    with ExitStack() as ctx:
        C, G = Chip(nc, ctx), Globals()
        G.kd = nc.dram_tensor("s4d_kernel", (D, P), F32, kind="Internal").ap()
        G.slots_in = nc.dram_tensor("slots_in", (NE * CAP + 2 * B * T, D), F32, kind="Internal").ap()
        G.slots_out = nc.dram_tensor("slots_out", (NE * CAP, D), F32, kind="Internal").ap()
        G.out = out
        G.X = C.sb("X", [P, NT, D])
        G.XT = C.sb("XT", [P, NT, D])
        G.ctxT = C.sb("ctxT", [DC, B * T])
        G.ident = C.sb("ident", [P, P])
        G.triu = C.sb("triu", [P, P])
        G.ones = C.sb("ones", [P, P])
        G.onesrow = C.sb("onesrow", [1, P])
        G.iota8 = C.sb("iota8", [P, NE])
        G.vec = C.sb("vec", [P, NVEC])
        G.tmask = C.sb("tmask", [P, NT])
        G.mg = C.sb("mg", [P, 1])
        G.dt = C.sb("dt", [P, 1])
        G.mean = C.sb("mean", [P, NT])
        G.rstd = C.sb("rstd", [P, NT])
        G.rstd2 = C.sb("rstd2", [P, NT])
        G.scratch = C.sb("scratch", [P, 8])
        with ExitStack() as early:
            G.XM = C.sb("XM", [P, NT, D], ctx=early)
            G.FO = C.sb("FO", [P, NT, 256], ctx=early)
            G.pen = C.sb("pen", [P, NT, T], ctx=early)
            G.gin = C.sb("gin", [P, D], ctx=early)
            G.bin = C.sb("bin", [P, D], ctx=early)
            G.wq = C.sb("wq", [P, P], ctx=early)
            G.wk = C.sb("wk", [DC, P], ctx=early)
            G.wv = C.sb("wv", [DC, D], ctx=early)
            G.film = C.sb("film", [P, 512], ctx=early)
            G.frow = C.sb("frow", [1, 512], ctx=early)
            setup(nc, C, A, G)
            C.end_phase()
            if last >= 1:
                first_attention(nc, C, A, G)
                C.end_phase()
            if last >= 2:
                convolution(nc, C, A, G)
                C.end_phase()
        with ExitStack() as late:
            G.XF = C.sb("XF", [D, B * T], ctx=late)
            G.gate = C.sb("gate", [P, NT, NE], ctx=late)
            G.slot_in = C.sb("slot_in", [P, 2, NT], dt=U32, ctx=late)
            G.slot_out = C.sb("slot_out", [P, 2, NT], dt=U32, ctx=late)
            G.prob = C.sb("prob", [P, 2, NT], ctx=late)
            if last >= 3:
                first_mlp(nc, C, A, G)
                C.end_phase()
            if last >= 4:
                close_first_attention(nc, C, A, G)
                C.end_phase()
                normalise_rows(nc, C, G, "ln1_", G.X)
                C.end_phase()
                turn_rows(nc, C, G, "turn1_", keep=True)
                C.end_phase()
            if last >= 5:
                first_router(nc, C, A, G)
                C.end_phase()
            if last >= 6:
                add_gated_biases(nc, C, A, G, "gb0_", "L0_ffn_eb2", send_rows(C, G))
                C.end_phase()
                first_experts(nc, C, A, G)
                C.end_phase()
            if last >= 7:
                normalise_rows(nc, C, G, "ln2_", G.X)
                C.end_phase()
                turn_rows(nc, C, G, "turn2_")
                C.end_phase()
                second_attention(nc, C, A, G)
                C.end_phase()
            if last >= 8:
                normalise_rows(nc, C, G, "ln3_", G.X)
                C.end_phase()
                turn_rows(nc, C, G, "turn3_")
                C.end_phase()
                second_router(nc, C, A, G)
                C.end_phase()
            if last >= 9:
                add_gated_biases(nc, C, A, G, "gb1_", "L1_ffn_b2")
                C.end_phase()
                second_experts(nc, C, A, G)
                C.end_phase()
                store(nc, C, G)
                C.end_phase()


_OUT = ((B, T, D), "float32")


def kernel(**inputs):
    import concourse.bacc as bacc
    from concourse.bass_utils import run_bass_kernel_spmd

    nc = bacc.Bacc("TRN2", target_bir_lowering=False, num_devices=1)
    arrays, args = {}, {}
    for name, a in inputs.items():
        a = np.ascontiguousarray(a)
        arrays[f"in_{name}"] = a
        args[name] = nc.dram_tensor(f"in_{name}", a.shape, mybir.dt.from_np(a.dtype), kind="ExternalInput").ap()
    out = nc.dram_tensor("out_0_dram", _OUT[0], mybir.dt.from_np(np.dtype(_OUT[1])), kind="ExternalOutput").ap()
    program(nc, args, out)
    r = run_bass_kernel_spmd(nc, [arrays], core_ids=[0])
    return r.results[0]["out_0_dram"]
```

```python
from contextlib import ExitStack

import numpy as np
import concourse.bass as bass
from concourse import mybir

F32 = mybir.dt.float32
U8 = mybir.dt.uint8
I32 = mybir.dt.int32
U32 = mybir.dt.uint32
F32R = mybir.dt.float32r
ALU = mybir.AluOpType
ACT = mybir.ActivationFunctionType
AX = mybir.AxisListType

P = 128
B, T, D = 64, 64, 128
DC = 96
NT = B * T // P
TB = 4
NBLK = NT // TB
H0, DH0 = 4, 32
H1, DH1 = 16, 8
KTOP = 32
NS = 64
HID = 512
NE = 8
CAP = 512
HE = 256
R = 16
EPS = 1e-5
MASKED = -1e30
TAKEN = -3e38
TWO_PI = 2.0 * np.pi
ROOT_SEED = float(0x5F3759DF)
ROUND = float(1.5 * 2 ** 23)

VEC = {}
for _name, _n in (("L0_xattn_b1", 4), ("L0_ffn_rb1", 4), ("L1_xattn_bq", 1), ("L1_xattn_bk", 1),
                  ("L1_xattn_bv", 1), ("L0_xattn_g_ffn", 1), ("L0_xattn_b_ffn", 1),
                  ("L0_xattn_log_dt", 1), ("L0_xattn_D_skip", 1), ("L0_ffn_eb1", 32),
                  ("L1_ffn_b1", 16), ("L1_ffn_b3", 16)):
    VEC[_name] = (sum(n for _, n in VEC.values()), _n)
NVEC = sum(n for _, n in VEC.values())


class Steps:

    def __init__(self, eng, sem):
        self.eng, self.sem, self.n = eng, sem, 0

    def did(self, ins):
        ins.then_inc(self.sem, 1)
        self.n += 1

    def wait(self):
        self.eng.wait_ge(self.sem, self.n)

    def then(self, ins):
        self.did(ins)
        self.wait()

    def passed(self):
        self.eng.sem_inc(self.sem, 1)
        self.n += 1
        self.wait()

    def clear(self):
        self.wait()
        self.eng.sem_clear(self.sem)
        self.n = 0


class Chip:

    def __init__(self, nc, ctx):
        self.nc, self.ctx = nc, ctx
        self.own, self.before = [], []

    def sb(self, name, shape, dt=F32, ctx=None):
        return (ctx or self.ctx).enter_context(self.nc.sbuf_tensor(name, shape, dt))

    def ps(self, name, shape, ctx, dt=F32):
        return ctx.enter_context(self.nc.psum_tensor(name, shape, dt))

    def sem(self, name):
        self.own.append(self.nc.alloc_semaphore(name=name))
        return self.own[-1]

    def end_phase(self):
        for h in self.own:
            self.nc.sync.sem_clear(h)
        for h in self.before:
            self.nc.release_semaphore(h)
        self.own, self.before = [], self.own


class Tile:

    def __init__(self, t, k, j, fixed):
        self.t, self.k, self.j, self.fixed = t, k, j, fixed

    def by(self, d):
        q = self.j + d
        return Tile(self.t + d, self.k + q // 2, q % 2, self.fixed)

    def real(self):
        return not self.fixed or 0 <= self.t < NT


def sweep(eng, slot, first, lo, hi, last):
    for t in range(first, lo):
        slot(Tile(t, t // 2, t % 2, True))
    with eng.Fori(0, (hi - lo) // 2) as i:
        for q in range(2):
            slot(Tile(i * 2 + (lo + q), i + (lo + q) // 2, (lo + q) % 2, False))
    for t in range(hi, last):
        slot(Tile(t, t // 2, t % 2, True))


def after(eng, sem, n):
    if not isinstance(n, int) or n > 0:
        eng.wait_ge(sem, n)


def wide(ap, shape):
    return ap.to_broadcast(shape)


def block_statistics(dve, step, src, w):
    for k in range(TB):
        step.did(dve.bn_stats(w["st"][:, k, :], src[:, k, :]))
    step.wait()
    for k in range(TB):
        m = dve.bn_aggr(w["mv"][:, k, :], w["st"][:, k, :])
    return m


def inverse_root(pool, step, w, done):
    v, r, a = (w[k][:] for k in ("v", "rstd", "a"))
    step.then(pool.tensor_scalar(v, w["mv"][:, :, 1], EPS, None, ALU.add))
    step.then(pool.tensor_scalar(r.bitcast(I32), v.bitcast(I32), -0.5, ROOT_SEED, ALU.mult, ALU.add))
    for k in range(3):
        step.then(pool.tensor_tensor(a, r, r, ALU.mult))
        step.then(pool.tensor_tensor(a, a, v, ALU.mult))
        step.then(pool.tensor_scalar(a, a, -0.5, 1.5, ALU.mult, ALU.add))
        m = pool.tensor_tensor(r, r, a, ALU.mult)
        if k < 2:
            step.then(m)
    m.then_inc(done, 1)


def normalise_block(dve, out, src, w):
    for k in range(TB):
        m = dve.tensor_scalar(out[:, k, :], src[:, k, :], w["mv"][:, k, 0:1], w["rstd"][:, k:k + 1], ALU.subtract, ALU.mult)
    return m


def setup(nc, C, A, G):
    with ExitStack() as ctx:
        vrow = C.sb("vrow", [NVEC, D], ctx=ctx)
        mk8 = C.sb("mk8", [P, NT, T], U8, ctx)
        tm8 = C.sb("tm8", [NT, P], U8, ctx)
        tmf = C.sb("tmf", [NT, P], ctx=ctx)
        kin = C.sb("kin", [P, 4, NS], ctx=ctx)
        film0 = C.sb("film0", [P, 512], ctx=ctx)
        frow0 = C.sb("frow0", [1, 512], ctx=ctx)
        kt = C.sb("kt", [P, 16, NS], ctx=ctx)
        zV = C.sb("zV", [P, 8, 2, NS], ctx=ctx)
        zU = C.sb("zU", [P, 8, 2, NS], ctx=ctx)
        big = C.sb("big", [P, 8, 2, NS], ctx=ctx)
        ctm = C.sb("ctm", [P, 2, 8, NS], ctx=ctx)
        kpad = C.sb("kpad", [P, P], ctx=ctx)
        st = C.sb("st", [P, NT, 6], ctx=ctx)
        w = {n: C.sb("w_" + n, [P, NT] + k, ctx=ctx) for n, k in (("mv", [2]), ("v", []), ("a", []), ("rstd", []))}
        shift = C.sb("shift", [P, NT], ctx=ctx)
        w2 = {"mv": C.sb("w_mv2", [P, NT, 2], ctx=ctx), "v": C.sb("w_v2", [P, NT], ctx=ctx), "a": w["a"], "rstd": G.rstd2}
        psv = C.ps("psv", [P, 512], ctx)
        pst = C.ps("pst", [P, 512], ctx)
        s = {n: C.sem("setup_" + n) for n in (
            "kin", "vec", "masks", "film", "rest", "zero", "ident", "vec_ps", "vec_sb",
            "exp", "args", "trig", "var", "root", "shift", "kpad", "kd", "dve", "act", "pool", "step", "tmf", "tm_ps")}
        x_loaded = [C.sem(f"setup_x{k}") for k in range(4)]

        with nc.Block() as block:

            @block.sync
            def _(sp):
                xv = A["x"].rearrange("(n b) t d -> (b t) n d", b=2)
                for k in range(4):
                    sp.dma_start(G.X[:, 8 * k:8 * k + 8, :], xv[:, 8 * k:8 * k + 8, :]).then_inc(x_loaded[k], 16)
                for k, name in enumerate(("L0_xattn_W_film_in", "L0_xattn_W_film_out")):
                    sp.dma_start(film0[:, 256 * k:256 * k + 256], A[name]).then_inc(s["film"], 16)
                for k, name in enumerate(("L0_xattn_b_film_in", "L0_xattn_b_film_out")):
                    sp.dma_start(frow0[:, 256 * k:256 * k + 256],
                                 A[name].rearrange("(a n) -> a n", a=1)).then_inc(s["film"], 16)
                sp.dma_start(G.mg[:], A["L0_xattn_mod_gate"].partition_broadcast(P)).then_inc(s["film"], 16)
                m = A["mask_BxS2_bf1"]
                for b2 in range(2):
                    src = bass.AP(m.tensor, b2 * T, [[0, T], [2 * T, NT], [1, T]])
                    sp.dma_start(mk8[T * b2:T * b2 + T, :, :], src).then_inc(s["masks"], 16)
                sp.dma_start(tm8[:], A["mask_BxS_bf1"].rearrange("(n b) t -> n (b t)", b=2)).then_inc(s["masks"], 16)
                loads = [(G.gin[:], A["L0_xattn_g_norm_in"].partition_broadcast(P)),
                         (G.bin[:], A["L0_xattn_b_norm_in"].partition_broadcast(P)),
                         (G.wq[:], A["L0_xattn_Wq"]), (G.wk[:], A["L0_xattn_Wk"]), (G.wv[:], A["L0_xattn_Wv"])]
                for dst, src in loads:
                    sp.dma_start(dst, src).then_inc(s["rest"], 16)
                sp.wait_ge(s["rest"], 16 * len(loads))
                sp.wait_ge(s["kpad"], 1)
                sp.dma_start(G.kd, kpad[:]).then_inc(s["kd"], 16)
                sp.wait_ge(s["kd"], 16)

            @block.gpsimd
            def _(pool):
                pool.memset(G.ident[:], 0.0).then_inc(s["zero"], 1)
                pool.memset(G.triu[:], 1.0).then_inc(s["zero"], 1)
                pool.memset(G.ones[:], 1.0).then_inc(s["zero"], 1)
                pool.memset(G.onesrow[:], 1.0).then_inc(s["zero"], 1)
                pool.wait_ge(s["zero"], 4)
                pool.affine_select(out=G.ident[:], in_=G.ident[:], compare_op=ALU.not_equal, fill=1.0,
                                   base=0, pattern=[[-1, P]], channel_multiplier=1).then_inc(s["ident"], 1)
                pool.affine_select(out=G.triu[:], in_=G.triu[:], compare_op=ALU.is_gt, fill=0.0,
                                   base=0, pattern=[[1, P]], channel_multiplier=-1).then_inc(s["ident"], 1)
                for e in range(NE):
                    pool.memset(G.iota8[:, e:e + 1], float(e - NE)).then_inc(s["ident"], 1)
                pool.memset(kpad[:, 0:T], 0.0).then_inc(s["ident"], 1)
                step = Steps(pool, s["step"])
                pool.wait_ge(s["var"], 1)
                inverse_root(pool, step, w, s["root"])
                pool.wait_ge(s["root"], 1)
                step.then(pool.tensor_tensor(shift[:], w["mv"][:, :, 0], w["rstd"][:], ALU.mult))
                pool.tensor_scalar(shift[:], shift[:], -1.0, None, ALU.mult).then_inc(s["shift"], 1)
                var2 = w2["mv"][:, :, 1]
                step.then(pool.tensor_tensor(var2, w["rstd"][:], w["rstd"][:], ALU.mult))
                step.then(pool.tensor_tensor(var2, var2, w["mv"][:, :, 1], ALU.mult))
                inverse_root(pool, step, w2, s["root"])
                pool.wait_ge(s["masks"], 48)
                pool.tensor_scalar(G.pen[:], mk8[:], -MASKED, MASKED, ALU.mult, ALU.add).then_inc(s["pool"], 1)
                pool.tensor_copy(tmf[:], tm8[:]).then_inc(s["tmf"], 1)
                pool.wait_ge(s["film"], 80)
                pool.tensor_scalar(G.film[:], film0[:], G.mg[:, 0:1], None, ALU.mult).then_inc(s["pool"], 1)
                pool.tensor_scalar(G.frow[:], frow0[:], G.mg[0:1, 0:1], None, ALU.mult).then_inc(s["pool"], 1)
                pool.wait_ge(s["pool"], 3)
                for k in range(2):
                    pool.tensor_scalar(G.frow[:, 256 * k:256 * k + D], G.frow[:, 256 * k:256 * k + D],
                                       1.0, None, ALU.add).then_inc(s["pool"], 1)
                pool.wait_ge(s["pool"], 5)

            @block.tensor
            def _(pe):
                pe.wait_ge(s["ident"], 1)
                pe.wait_ge(s["vec"], 16 * len(VEC))
                pe.transpose(psv[:, 0:NVEC], vrow[:], G.ident[0:NVEC, 0:NVEC]).then_inc(s["vec_ps"], 1)
                pe.wait_ge(s["tmf"], 1)
                pe.transpose(pst[:, 0:NT], tmf[:], G.ident[0:NT, 0:NT]).then_inc(s["tm_ps"], 1)

            @block.scalar
            def _(act):
                act.dma_start(kin[:, 0, :], A["L0_xattn_A_re"]).then_inc(s["kin"], 16)
                act.dma_start(kin[:, 1, :], A["L0_xattn_A_im"]).then_inc(s["kin"], 16)
                act.dma_start(kin[:, 2, :], A["L0_xattn_C_re"]).then_inc(s["kin"], 16)
                act.dma_start(kin[:, 3, :], A["L0_xattn_C_im"]).then_inc(s["kin"], 16)
                for name, (at, n) in VEC.items():
                    src = A[name]
                    if len(src.shape) == 1:
                        src = src.rearrange("(c p) -> c p", p=D)
                    else:
                        src = src.rearrange("e (c p) -> (e c) p", p=D)
                    act.dma_start(vrow[at:at + n, :], src).then_inc(s["vec"], 16)
                act.preload_act_table(ACT.Exp)
                act.wait_ge(s["vec_ps"], 1)
                act.activation(G.vec[:], psv[:, 0:NVEC], ACT.Copy).then_inc(s["vec_sb"], 1)
                act.wait_ge(s["vec_sb"], 1)
                at = VEC["L0_xattn_log_dt"][0]
                act.activation(G.dt[:], G.vec[:, at:at + 1], ACT.Exp).then_inc(s["exp"], 1)
                act.wait_ge(s["args"], 1)
                act.activation(kt[:, 3, :], kt[:, 0, :], ACT.Exp).then_inc(s["exp"], 1)
                act.wait_ge(s["args"], 2)
                act.activation(kt[:, 4:6, :], kt[:, 4:6, :], ACT.Sin).then_inc(s["trig"], 1)
                act.wait_ge(s["shift"], 1)
                for t in range(NT):
                    act.activation(G.XT[:, t, :], G.X[:, t, :], ACT.Identity, scale=w["rstd"][:, t:t + 1],
                                   bias=shift[:, t:t + 1])
                act.wait_ge(s["tm_ps"], 1)
                act.activation(G.tmask[:], pst[:, 0:NT], ACT.Copy, scale=1.0 / H0).then_inc(s["vec_sb"], 1)

            @block.vector
            def _(dve):
                step = Steps(dve, s["dve"])
                for k in range(4):
                    dve.wait_ge(x_loaded[k], 16)
                    for t in range(8 * k, 8 * k + 8):
                        step.did(dve.bn_stats(st[:, t, :], G.X[:, t, :]))
                step.wait()
                for t in range(NT):
                    m = dve.bn_aggr(w["mv"][:, t, :], st[:, t, :])
                m.then_inc(s["var"], 1)
                TT, TS = dve.tensor_tensor, dve.tensor_scalar
                dve.wait_ge(s["kin"], 64)
                dve.wait_ge(s["exp"], 1)
                TS(kt[:, 0, :], kin[:, 0, :], G.dt[:, 0:1], None, ALU.mult).then_inc(s["args"], 1)
                step.then(TS(kt[:, 1, :], kin[:, 1, :], G.dt[:, 0:1], None, ALU.mult))
                step.did(TS(kt[:, 6, :], kt[:, 1, :], 1.0 / TWO_PI, 0.25, ALU.mult, ALU.add))
                step.then(TS(kt[:, 7, :], kt[:, 1, :], 1.0 / TWO_PI, None, ALU.mult))
                step.then(TS(kt[:, 6:8, :], kt[:, 6:8, :], ROUND, None, ALU.add))
                step.then(TS(kt[:, 6:8, :], kt[:, 6:8, :], ROUND, None, ALU.subtract))
                c1 = 6.28125
                c2 = TWO_PI - c1
                th = wide(kt[:, 1:2, :], [P, 2, NS])
                step.then(dve.scalar_tensor_tensor(kt[:, 4:6, :], kt[:, 6:8, :], -c1, th, ALU.mult, ALU.add))
                step.then(dve.scalar_tensor_tensor(kt[:, 4:6, :], kt[:, 6:8, :], -c2, kt[:, 4:6, :], ALU.mult, ALU.add))
                step.then(TS(kt[:, 4, :], kt[:, 4, :], float(np.pi / 2), None, ALU.add))
                TS(kt[:, 4:6, :], kt[:, 4:6, :], float(np.float32(3.1415925)), float(np.float32(-3.1415925)),
                   ALU.min, ALU.max).then_inc(s["args"], 1)
                dve.wait_ge(s["exp"], 2)
                dve.wait_ge(s["trig"], 1)
                V = [(zV[:, b, 0, :], zV[:, b, 1, :]) for b in range(8)]
                dve.memset(zV[:, 0, 0, :], 1.0)
                dve.memset(zV[:, 0, 1, :], 0.0)
                TT(zV[:, 1, 0, :], kt[:, 3, :], kt[:, 4, :], ALU.mult)
                step.then(TT(zV[:, 1, 1, :], kt[:, 3, :], kt[:, 5, :], ALU.mult))

                def times(out, a, b, n=1):
                    t0, t1 = (ctm[:, k, 0:n, :] if n > 1 else ctm[:, k, 0, :] for k in range(2))
                    TT(t0, a[0], b[0], ALU.mult)
                    step.then(TT(t1, a[1], b[1], ALU.mult))
                    step.then(TT(out[0], t0, t1, ALU.subtract))
                    TT(t0, a[0], b[1], ALU.mult)
                    step.then(TT(t1, a[1], b[0], ALU.mult))
                    step.then(TT(out[1], t0, t1, ALU.add))

                def powers(z, a, n):
                    return tuple(z[:, a:a + n, k, :] for k in range(2))

                def same(z, n):
                    return tuple(wide(q.unsqueeze(1), [P, n, NS]) for q in z)

                z2, z4, z8, z16, z32 = ((kt[:, 6 + 2 * k, :], kt[:, 7 + 2 * k, :]) for k in range(5))
                times(z2, V[1], V[1])
                times(powers(zV, 2, 2), powers(zV, 0, 2), same(z2, 2), 2)
                times(z4, z2, z2)
                times(powers(zV, 4, 4), powers(zV, 0, 4), same(z4, 4), 4)
                times(z8, z4, z4)
                times(z16, z8, z8)
                times(z32, z16, z16)
                zm = (kt[:, 0, :], kt[:, 1, :])
                TS(zm[0], V[1][0], -1.0, None, ALU.add)
                dve.tensor_copy(zm[1], V[1][1])
                TT(ctm[:, 0, 0, :], kin[:, 0, :], kin[:, 0, :], ALU.mult)
                TT(ctm[:, 1, 0, :], kin[:, 1, :], kin[:, 1, :], ALU.mult)
                step.then(TS(kt[:, 2, :], kin[:, 1, :], -1.0, None, ALU.mult))
                step.then(TT(kt[:, 3, :], ctm[:, 0, 0, :], ctm[:, 1, 0, :], ALU.add))
                step.then(dve.reciprocal(kt[:, 3, :], kt[:, 3, :]))
                step.then(TS(kt[:, 3, :], kt[:, 3, :], 2.0, None, ALU.mult))
                prod = (kt[:, 4, :], kt[:, 5, :])
                times(prod, zm, (kin[:, 2, :], kin[:, 3, :]))
                U0 = (zU[:, 0, 0, :], zU[:, 0, 1, :])
                times((big[:, 0, 0, :], big[:, 0, 1, :]), prod, (kin[:, 0, :], kt[:, 2, :]))
                TT(U0[0], big[:, 0, 0, :], kt[:, 3, :], ALU.mult)
                step.then(TT(U0[1], big[:, 0, 1, :], kt[:, 3, :], ALU.mult))
                times((zU[:, 1, 0, :], zU[:, 1, 1, :]), U0, z8)
                times(powers(zU, 2, 2), powers(zU, 0, 2), same(z16, 2), 2)
                times(powers(zU, 4, 4), powers(zU, 0, 4), same(z32, 4), 4)
                step.then(TS(zV[:, :, 1, :], zV[:, :, 1, :], -1.0, None, ALU.mult))
                dve.wait_ge(s["ident"], 11)
                for a in range(8):
                    u = wide(zU[:, a:a + 1, :, :], [P, 8, 2, NS])
                    step.then(TT(big[:], zV[:], u, ALU.mult))
                    step.then(dve.tensor_reduce(kpad[:, T + 8 * a:T + 8 * a + 8],
                                                big[:].rearrange("p b c n -> p b (c n)"), AX.X, ALU.add))
                at = VEC["L0_xattn_D_skip"][0]
                TT(kpad[:, T:T + 1], kpad[:, T:T + 1], G.vec[:, at:at + 1], ALU.add).then_inc(s["kpad"], 1)
                dve.wait_ge(s["kpad"], 1)


def first_attention(nc, C, A, G):
    scale = 1.0 / float(np.sqrt(DH0).astype(np.float32))
    with ExitStack() as ctx:
        def two(name, shape):
            return [C.sb(f"{name}{j}", shape, ctx=ctx) for j in range(2)]

        xs, cs, cb = two("xs", [P, D]), two("cs", [P, DC]), two("cb", [P, DC])
        xf, cf = two("xf", [D, P]), two("cf", [DC, P])
        qt, kb = two("qt", [P, P]), two("kb", [P, 2, H0, T])
        sc, wk_, m8 = two("sc", [P, H0, T]), two("work", [P, H0, T]), two("m8", [P, H0, 4, 8])
        dd, ee, pr = two("dd", [P, H0, T]), two("ee", [P, H0, T]), two("pr", [P, H0, T])
        rs, at, abd = two("rs", [P, 2, H0]), two("at", [P, P]), two("abd", [P, P])
        us, ct, fi = two("us", [DC, P]), two("ct", [D, P]), two("fi", [P, 256])
        xn = C.sb("xn", [P, D], ctx=ctx)
        psa = [C.ps(f"psa{j}", [P, 512], ctx) for j in range(2)]
        pss = [C.ps(f"pss{j}", [P, 512], ctx) for j in range(2)]
        psb = [C.ps(f"psb{j}", [P, 512], ctx) for j in range(2)]
        psf = [C.ps(f"psf{j}", [P, 512], ctx) for j in range(2)]
        s = {n: C.sem("att0_" + n) for n in (
            "xs", "turned", "turned_sb", "qk", "qk_sb", "scores", "scores_sb", "max", "diff", "exp",
            "attn", "attn_turned", "attn_sb", "u", "u_sb", "c", "c_sb", "film", "film_sb", "mod",
            "ctx_kept", "zero", "weights", "dve", "pool")}
        loaded = [C.sem(f"att0_ctx_loaded{j}") for j in range(2)]
        again = [C.sem(f"att0_ctx_again{j}") for j in range(2)]
        ctx_v = A["ctx_768"].rearrange("b t d -> (b t) d")

        with nc.Block() as block:
            SWEEP = (-3, 5, 27)

            @block.sync
            def _(sp):
                def rows(t):
                    return ctx_v[bass.ds(t * P, P), :]

                def slot(x):
                    a, c = x.by(3), x.by(-1)
                    if a.real():
                        after(sp, s["turned"], a.t - 1)
                        sp.dma_start(cs[a.j][:], rows(a.t)).then_inc(loaded[a.j], 16)
                    if c.real():
                        after(sp, s["u"], c.t - 1)
                        sp.dma_start(cb[c.j][:], rows(c.t)).then_inc(again[c.j], 16)

                sweep(sp, slot, *SWEEP, NT + 1)

            @block.gpsimd
            def _(pool):
                step = Steps(pool, s["pool"])
                for j in range(2):
                    for m in (kb[j], abd[j], at[j]):
                        pool.memset(m[:], 0.0).then_inc(s["zero"], 1)

                def slot(x):
                    j, a, g, c, m = x.j, x.by(3), x.by(4), x.by(-4), x.by(-1)
                    if m.real():
                        pool.wait_ge(s["weights"], m.t + 1)
                        step.then(pool.tensor_tensor(pr[m.j][:], pr[m.j][:], wide(rs[m.j][:, 1, :].unsqueeze(2), [P, H0, T]), ALU.mult))
                        after(pool, s["attn_turned"], m.t - 1)
                        step.did(pool.tensor_tensor(pr[m.j][:, 0:2, :], pr[m.j][:, 0:2, :], pr[m.j][:, 2:4, :], ALU.add))
                        step.wait()
                        pool.tensor_tensor(at[m.j][:, 0:T], pr[m.j][:, 0, :], pr[m.j][:, 1, :], ALU.add).then_inc(s["attn"], 1)
                    if x.real():
                        pool.wait_ge(s["max"], x.t + 1)
                        pool.tensor_tensor(dd[j][:], sc[j][:], wide(m8[j][:, :, 0, 0:1], [P, H0, T]),
                                           ALU.subtract).then_inc(s["diff"], 1)
                    if g.real():
                        after(pool, s["turned"], g.t - 1)
                        pool.tensor_copy(xs[g.j][:], G.XT[:, g.t, :]).then_inc(s["xs"], 1)
                    if a.real():
                        pool.wait_ge(s["turned_sb"], a.t + 1)
                        pool.tensor_copy(G.ctxT[:, bass.ds(a.t * P, P)], cf[a.j][:]).then_inc(s["ctx_kept"], 1)
                    if c.real():
                        step.then(pool.tensor_tensor(xn[:], G.XT[:, c.t, :], wide(G.rstd2[:, bass.ds(c.t, 1)], [P, D]), ALU.mult))
                        step.then(pool.tensor_tensor(xn[:], xn[:], G.gin[:], ALU.mult))
                        step.then(pool.tensor_tensor(xn[:], xn[:], G.bin[:], ALU.add))
                        pool.wait_ge(s["film_sb"], c.t + 1)
                        step.then(pool.tensor_tensor(xn[:], xn[:], fi[c.j][:, 0:D], ALU.mult))
                        pool.tensor_tensor(G.XM[:, c.t, :], xn[:], fi[c.j][:, D:2 * D], ALU.add).then_inc(s["mod"], 1)
                    if m.real() or c.real():
                        step.clear()
                    if c.real():
                        pool.wait_ge(s["mod"], c.t + 1)

                for j in range(1):
                    pool.tensor_copy(xs[j][:], G.XT[:, j, :]).then_inc(s["xs"], 1)
                sweep(pool, slot, *SWEEP, NT + 4)

            @block.tensor
            def _(pe):
                pe.wait_ge(s["zero"], 6)

                def slot(x):
                    turn, qk, score, attn, vec, film = (x.by(d) for d in (3, 2, 1, -1, -2, -3))
                    if turn.real():
                        j = turn.j
                        pe.wait_ge(s["xs"], turn.t + 1)
                        after(pe, s["qk_sb"], turn.t - 1)
                        pe.transpose(psa[j][:, 0:P], xs[j][:], G.ident[:])
                        pe.wait_ge(loaded[j], (turn.k + 1) * 16)
                        pe.transpose(psa[j][0:DC, P:2 * P], cs[j][:], G.ident[:]).then_inc(s["turned"], 1)
                    if film.real():
                        j = film.j
                        pe.wait_ge(s["c_sb"], film.t + 1)
                        after(pe, s["film_sb"], film.t - 1)
                        pe.matmul(psf[j][:], ct[j][:], G.film[:], start=True, stop=False)
                        pe.matmul(psf[j][:], G.onesrow[:], G.frow[:], start=False, stop=True).then_inc(s["film"], 1)
                    if vec.real():
                        j = vec.j
                        pe.wait_ge(s["attn_sb"], vec.t + 1)
                        pe.wait_ge(again[j], (vec.k + 1) * 16)
                        pe.matmul(psb[j][0:DC, P:2 * P], cb[j][:], abd[j][:], start=True, stop=True).then_inc(s["u"], 1)
                    if qk.real():
                        j = qk.j
                        pe.wait_ge(s["turned_sb"], qk.t + 1)
                        pe.matmul(psa[j][:, 256:384], G.wq[:], xf[j][:], start=True, stop=True)
                        pe.matmul(psa[j][:, 384:512], G.wk[:], cf[j][:], start=True, stop=True).then_inc(s["qk"], 1)
                    if score.real():
                        j = score.j
                        pe.wait_ge(s["qk_sb"], score.t + 1)
                        after(pe, s["scores_sb"], score.t - 1)
                        for b2 in range(2):
                            mm = pe.matmul(pss[j][T * b2:T * b2 + T, 0:H0 * T], qt[j][:, T * b2:T * b2 + T],
                                           kb[j][:, b2, :, :], start=True, stop=True)
                        mm.then_inc(s["scores"], 1)
                    if vec.real():
                        pe.wait_ge(s["u_sb"], vec.t + 1)
                        pe.matmul(psb[vec.j][:, 256:384], G.wv[:], us[vec.j][:], start=True, stop=True).then_inc(s["c"], 1)
                    if attn.real():
                        pe.wait_ge(s["attn"], attn.t + 1)
                        after(pe, s["c_sb"], attn.t - 1)
                        pe.transpose(psb[attn.j][:, 0:P], at[attn.j][:], G.ident[:]).then_inc(s["attn_turned"], 1)

                sweep(pe, slot, *SWEEP, NT + 3)

            @block.scalar
            def _(act):
                act.preload_act_table(ACT.Exp)
                copy = lambda out, in_: act.activation(out, in_, ACT.Copy)

                def slot(x):
                    turn, qk, attn, vec, film = (x.by(d) for d in (3, 2, -1, -2, -3))
                    if turn.real():
                        j = turn.j
                        act.wait_ge(s["turned"], turn.t + 1)
                        after(act, s["ctx_kept"], turn.t - 1)
                        copy(xf[j][:], psa[j][:, 0:P])
                        copy(cf[j][:], psa[j][0:DC, P:2 * P]).then_inc(s["turned_sb"], 1)
                    if vec.real():
                        act.wait_ge(s["u"], vec.t + 1)
                        copy(us[vec.j][:], psb[vec.j][0:DC, P:2 * P]).then_inc(s["u_sb"], 1)
                    if x.real():
                        act.wait_ge(s["diff"], x.t + 1)
                        act.activation(ee[x.j][:], dd[x.j][:], ACT.Exp, scale=scale).then_inc(s["exp"], 1)
                    if qk.real():
                        j = qk.j
                        act.wait_ge(s["qk"], qk.t + 1)
                        after(act, s["scores"], qk.t - 1)
                        copy(qt[j][:], psa[j][:, 256:384])
                        for h in range(H0):
                            rows = slice(DH0 * h, DH0 * h + DH0)
                            m = copy(kb[j][rows, :, h, :], psa[j][rows, 384:512].rearrange("p (b g) -> p b g", b=2))
                        m.then_inc(s["qk_sb"], 1)
                    if film.real():
                        act.wait_ge(s["film"], film.t + 1)
                        after(act, s["mod"], film.t - 1)
                        copy(fi[film.j][:], psf[film.j][:, 0:256])
                        copy(G.FO[:, film.t, :], psf[film.j][:, 256:512]).then_inc(s["film_sb"], 1)
                    if vec.real():
                        act.wait_ge(s["c"], vec.t + 1)
                        copy(ct[vec.j][:], psb[vec.j][:, 256:384]).then_inc(s["c_sb"], 1)
                    if attn.real():
                        j = attn.j
                        act.wait_ge(s["attn_turned"], attn.t + 1)
                        copy(abd[j][0:T, 0:T], psb[j][0:T, 0:T])
                        copy(abd[j][T:P, T:P], psb[j][0:T, T:P]).then_inc(s["attn_sb"], 1)

                sweep(act, slot, *SWEEP, NT + 3)

            @block.vector
            def _(dve):
                dve.wait_ge(s["zero"], 6)
                step = Steps(dve, s["dve"])

                def select(x):
                    t, j = x.t, x.j
                    dve.wait_ge(s["scores"], t + 1)
                    dve.tensor_tensor(sc[j][:], pss[j][:, 0:H0 * T].rearrange("p (h g) -> p h g", h=H0),
                                      wide(G.pen[:, bass.ds(t, 1), :], [P, H0, T]), ALU.add).then_inc(s["scores_sb"], 1)
                    dve.wait_ge(s["scores_sb"], t + 1)
                    step.passed()
                    src = sc[j]
                    for r in range(KTOP // 8):
                        for h in range(H0):
                            mx = dve.max(m8[j][:, h, r, :], src[:, h, :])
                            if r == 0 and h == H0 - 1:
                                mx.then_inc(s["max"], 1)
                            else:
                                step.did(mx)
                        if r == 0:
                            dve.wait_ge(s["max"], t + 1)
                            step.passed()
                        else:
                            step.wait()
                        for h in range(H0):
                            step.did(dve.match_replace(wk_[j][:, h, :], m8[j][:, h, r, :], src[:, h, :], TAKEN))
                        step.wait()
                        src = wk_[j]
                    dve.wait_ge(s["exp"], t + 1)
                    flat = lambda m: m[j][:].rearrange("p h g -> p (h g)")
                    after(dve, s["attn"], t - 1)
                    step.then(dve.scalar_tensor_tensor(flat(pr), flat(wk_), TAKEN / 3, flat(ee), ALU.is_le, ALU.mult))
                    step.then(dve.tensor_reduce(rs[j][:, 0, :], pr[j][:], AX.X, ALU.add))
                    step.then(dve.reciprocal(rs[j][:, 1, :], rs[j][:, 0, :]))
                    dve.tensor_scalar(rs[j][:, 1, :], rs[j][:, 1, :], G.tmask[:, bass.ds(t, 1)], None, ALU.mult).then_inc(s["weights"], 1)
                    step.clear()

                sweep(dve, select, 0, 2, NT, NT)


def convolution(nc, C, A, G):
    CH = 16
    NG = D // CH
    with ExitStack() as ctx:
        toe = [C.sb(f"toe{j}", [P, CH, P], ctx=ctx) for j in range(2)]
        psy = [C.ps(f"psy{j}", [P, CH, NT], ctx) for j in range(2)]
        ym = [C.sb(f"ym{j}", [P, NT, CH], ctx=ctx) for j in range(2)]
        yn = [C.sb(f"yn{j}", [P, NT, CH], ctx=ctx) for j in range(2)]
        flip = C.sb("flip", [P, P], ctx=ctx)
        psr = [C.ps(f"psr{j}", [P, TB, D], ctx) for j in range(2)]
        s = {n: C.sem("conv_" + n) for n in ("zero", "flip", "y", "y_film", "y_sum", "step", "rev", "rev_sb")}
        loaded = [C.sem(f"conv_toeplitz_loaded{j}") for j in range(2)]
        with nc.Block() as block:

            @block.sync
            def _(sp):
                sp.wait_ge(s["zero"], 2)
                for g in range(NG):
                    j = g % 2
                    if g >= 2:
                        sp.wait_ge(s["y"], g - 1)
                    for b2 in range(2):
                        src = bass.AP(G.kd.tensor, g * (CH * P) + 1, [[1, T], [P, CH], [1, T]])
                        sp.dma_start(toe[j][T * b2:T * b2 + T, :, T * b2:T * b2 + T], src).then_inc(loaded[j], 16)

            @block.gpsimd
            def _(pool):
                pool.sem_inc(s["y_sum"], 2)
                pool.memset(flip[:], 0.0).then_inc(s["flip"], 1)
                pool.wait_ge(s["flip"], 1)
                for b2 in range(2):
                    half = flip[T * b2:T * b2 + T, T * b2:T * b2 + T]
                    pool.affine_select(out=half, in_=half, compare_op=ALU.not_equal, fill=1.0, base=1 - T,
                                       pattern=[[1, T]], channel_multiplier=1).then_inc(s["flip"], 1)
                    pool.wait_ge(s["flip"], 2 + b2)
                for j in range(2):
                    pool.memset(toe[j][:], 0.0).then_inc(s["zero"], 1)
                with pool.Fori(0, NG // 2) as i:
                    for j in range(2):
                        g = i * 2 + j
                        pool.wait_ge(s["y_film"], g + 3)
                        ch = bass.ds(g * CH, CH)
                        pool.tensor_tensor(yn[j][:], ym[j][:], G.FO[:, :, bass.ds(g * CH + D, CH)], ALU.add).then_inc(s["step"], 1)
                        pool.wait_ge(s["step"], g + 1)
                        pool.tensor_tensor(G.XT[:, :, ch], G.XT[:, :, ch], yn[j][:], ALU.add).then_inc(s["y_sum"], 1)
                pool.wait_ge(s["y_sum"], NG + 2)

            @block.tensor
            def _(pe):
                pe.wait_ge(s["flip"], 3)
                with pe.Fori(0, NBLK // 2) as i:
                    for j in range(2):
                        b = i * 2 + j
                        pe.wait_ge(s["rev_sb"], b + 1)
                        pe.matmul(psr[j][:], flip[:], G.XM[:, bass.ds(b * TB, TB), :], start=True, stop=True).then_inc(s["rev"], 1)
                pe.wait_ge(s["rev_sb"], NBLK + 2)
                with pe.Fori(0, NG // 2) as i:
                    for j in range(2):
                        g = i * 2 + j
                        pe.wait_ge(loaded[j], (i + 1) * 32)
                        pe.wait_ge(s["y_film"], g + 1)
                        for c in range(CH):
                            mm = pe.matmul(psy[j][:, c, :], toe[j][:, c, :], G.XM[:, :, bass.ds(g * CH + c, 1)],
                                           start=True, stop=True)
                        mm.then_inc(s["y"], 1)

            @block.scalar
            def _(act):
                act.sem_inc(s["rev_sb"], 2)
                act.preload_act_table(ACT.Copy)
                with act.Fori(0, NBLK // 2) as i:
                    for j in range(2):
                        b = i * 2 + j
                        act.wait_ge(s["rev"], b + 1)
                        act.activation(G.XM[:, bass.ds(b * TB, TB), :], psr[j][:], ACT.Copy).then_inc(s["rev_sb"], 1)

            @block.vector
            def _(dve):
                dve.sem_inc(s["y_film"], 2)
                with dve.Fori(0, NG // 2) as i:
                    for j in range(2):
                        g = i * 2 + j
                        dve.wait_ge(s["y"], g + 1)
                        dve.wait_ge(s["y_sum"], g + 1)
                        dve.tensor_tensor(ym[j][:], psy[j][:].rearrange("p c b -> p b c"),
                                          G.FO[:, :, bass.ds(g * CH, CH)], ALU.mult).then_inc(s["y_film"], 1)


def fold_weights(C, A, G, ctx):
    NC = HE // P

    def two(name, shape):
        return [C.sb(f"fold_{name}{j}", shape, ctx=ctx) for j in range(2)]

    wr = two("wr", [P, 2, NC, D])
    w2r = two("w2r", [D, HE])
    br = two("br", [P, 2, NC, R])
    b2r = two("b2r", [D, R])
    ar = two("ar", [R, 2, D])
    a2 = two("a2", [R, HE])
    bt = two("bt", [R, 2 * NC + 1, P])
    psb = C.ps("fold_psb", [P, 512], ctx)
    psb2 = C.ps("fold_psb2", [P, 512], ctx)
    s = {n: C.sem("fold_" + n) for n in ("bt", "bt_sb", "w", "w_sb")}
    loaded = [C.sem(f"fold_loaded{j}") for j in range(2)]

    def sync(sp):
        for e in range(NE):
            j = e % 2
            after(sp, s["w"], e - 1)
            for m, (W, Bn, An) in enumerate((("W1", "B1", "A1"), ("W3", "B3", "A3"))):
                sp.dma_start(wr[j][:, m, :, :], A["L1_ffn_" + W][e].rearrange("(c p) d -> p c d", p=P)).then_inc(loaded[j], 16)
                sp.dma_start(br[j][:, m, :, :], A["L1_ffn_" + Bn][e].rearrange("(c p) r -> p c r", p=P)).then_inc(loaded[j], 16)
                sp.dma_start(ar[j][:, m, :], A["L1_ffn_" + An][e]).then_inc(loaded[j], 16)
            sp.dma_start(w2r[j][:], A["L1_ffn_W2"][e]).then_inc(loaded[j], 16)
            sp.dma_start(b2r[j][:], A["L1_ffn_B2"][e]).then_inc(loaded[j], 16)
            sp.dma_start(a2[j][:], A["L1_ffn_A2"][e]).then_inc(loaded[j], 16)

    def tensor(pe, e):
        j = e % 2
        pe.wait_ge(loaded[j], (e // 2 + 1) * 9 * 16)
        after(pe, s["w_sb"], e)
        for m in range(2):
            for c in range(NC):
                k = m * NC + c
                pe.transpose(psb[0:R, k * P:(k + 1) * P], br[j][:, m, c, :], G.ident[:])
        pe.transpose(psb2[0:R, 0:P], b2r[j][:], G.ident[:]).then_inc(s["bt"], 1)
        pe.wait_ge(s["bt_sb"], e + 1)
        for m in range(2):
            for c in range(NC):
                k = m * NC + c
                o = psb[:, k * P:(k + 1) * P]
                pe.matmul(o, wr[j][:, m, c, :], G.ident[:], start=True, stop=False)
                pe.matmul(o, ar[j][:, m, :], bt[j][:, k, :], start=False, stop=True)
        for c in range(NC):
            o = psb2[:, c * D:(c + 1) * D]
            pe.matmul(o, w2r[j][:, c * P:(c + 1) * P], G.ident[:], start=True, stop=False)
            mm = pe.matmul(o, a2[j][:, c * P:(c + 1) * P], bt[j][:, 2 * NC, :], start=False, stop=True)
        mm.then_inc(s["w"], 1)

    def scalar(act, e):
        j = e % 2
        act.wait_ge(s["bt"], e + 1)
        act.activation(bt[j][:, 0:2 * NC, :], psb[0:R, :].rearrange("r (k p) -> r k p", p=P), ACT.Copy)
        act.activation(bt[j][:, 2 * NC, :], psb2[0:R, 0:P], ACT.Copy).then_inc(s["bt_sb"], 1)
        act.wait_ge(s["w"], e + 1)
        act.activation(G.w13[:, e, :, :, :].rearrange("d m c p -> d (m c p)"), psb[:], ACT.Copy)
        act.activation(G.w2[:, e, :, :].rearrange("p c d -> p (c d)"), psb2[:, 0:NC * D], ACT.Copy).then_inc(s["w_sb"], 1)

    return sync, tensor, scalar


def turn_rows(nc, C, A, G, tag, gather=False):
    with ExitStack() as ctx:
        def two(name, shape):
            return [C.sb(f"{tag}{name}{j}", shape, ctx=ctx) for j in range(2)]

        xs = two("xs", [P, TB, D])
        full = {n: C.sb(tag + n, [P, NT] + k, ctx=ctx) for n, k in (("st", [6]), ("mv", [2]), ("v", []), ("a", []), ("rstd", []))}

        def part(b, n=1):
            return {k: m[:, b * TB:(b + n) * TB] for k, m in full.items()}

        HALF = NBLK // 2
        rows = [G.XT[:], G.XF[:].rearrange("p (n d) -> p n d", d=D)]
        pst = [C.ps(f"{tag}pst{j}", [P, TB * P], ctx) for j in range(2)]
        s = {n: C.sem(tag + n) for n in ("sum0", "sum1", "var", "root", "xs", "turned", "turned_sb", "dve", "pool")}
        fetched = [C.sem(f"{tag}fetched{b}") for b in range(NBLK if gather else 0)]
        if gather:
            fold_sync, fold_tensor, fold_scalar = fold_weights(C, A, G, ctx)
        assert NE == NBLK
        with nc.Block() as block:

            if gather:
                @block.sync
                def _(sp):
                    fold_sync(sp)

            @block.gpsimd
            def _(pool):
                if gather:
                    for t in range(NT):
                        for k in range(2):
                            pool.indirect_dma_start(rows[k][:, t, :], None, G.slots_out,
                                                    bass.IndirectOffsetOnAxis(ap=G.slot_out[:, k, t:t + 1], axis=0)
                                                    ).then_inc(fetched[t // TB], 16)
                else:
                    step = Steps(pool, s["pool"])
                    for half in range(2):
                        pool.wait_ge(s["var"], (half + 1) * HALF)
                        inverse_root(pool, step, part(half * HALF, HALF), s["root"])

            @block.vector
            def _(dve):
                step = Steps(dve, s["dve"])

                def stats(b):
                    block_statistics(dve, step, G.X[:, b * TB:(b + 1) * TB, :], part(b)).then_inc(s["var"], 1)

                def give(b):
                    after(dve, s["turned"], b - 1)
                    normalise_block(dve, xs[b % 2], G.X[:, b * TB:(b + 1) * TB, :], part(b)).then_inc(s["xs"], 1)

                if gather:
                    for b in range(NBLK):
                        dve.wait_ge(fetched[b], TB * 2 * 16)
                        for k in range(2):
                            for t in range(b * TB, (b + 1) * TB):
                                m = dve.scalar_tensor_tensor(G.X[:, t, :], rows[k][:, t, :], G.prob[:, k, t:t + 1],
                                                             G.X[:, t, :], ALU.mult, ALU.add)
                            m.then_inc(s[f"sum{k}"], 1)
                            dve.wait_ge(s[f"sum{k}"], b + 1)
                        stats(b)
                        dve.wait_ge(s["var"], b + 1)
                        inverse_root(dve, step, part(b), s["root"])
                        dve.wait_ge(s["root"], b + 1)
                        give(b)
                else:
                    for b in range(NBLK):
                        stats(b)
                    for b in range(NBLK):
                        dve.wait_ge(s["root"], b // HALF + 1)
                        give(b)

            @block.tensor
            def _(pe):
                for b in range(NBLK):
                    if gather:
                        fold_tensor(pe, b)
                    pe.wait_ge(s["xs"], b + 1)
                    after(pe, s["turned_sb"], b - 1)
                    for k in range(TB):
                        mm = pe.transpose(pst[b % 2][:, k * P:(k + 1) * P], xs[b % 2][:, k, :], G.ident[:])
                    mm.then_inc(s["turned"], 1)

            @block.scalar
            def _(act):
                act.preload_act_table(ACT.Copy)
                for b in range(NBLK):
                    if gather:
                        fold_scalar(act, b)
                    act.wait_ge(s["turned"], b + 1)
                    act.activation(G.XF[:, b * TB * P:(b + 1) * TB * P], pst[b % 2][:], ACT.Copy).then_inc(s["turned_sb"], 1)


def two_largest(dve, step, C, G, lg, w, iota):
    full = [P, NT, NE]
    e, idx = w["e"], w["idx"]
    for k in range(2):
        oh = w["oh"][k]
        step.then(dve.tensor_reduce(w["m"][:, k, :], lg, AX.X, ALU.max))
        step.then(dve.tensor_tensor(e[:], lg, wide(w["m"][:, k, :].unsqueeze(2), full), ALU.is_equal))
        step.then(dve.tensor_tensor(e[:], e[:], wide(iota[:].unsqueeze(1), full), ALU.mult))
        step.then(dve.tensor_reduce(idx[:], e[:], AX.X, ALU.min))
        step.then(dve.tensor_tensor(oh[:], wide(iota[:].unsqueeze(1), full), wide(idx[:].unsqueeze(2), full), ALU.is_equal))
        if k == 0:
            step.then(dve.scalar_tensor_tensor(lg, oh[:].rearrange("p n e -> p (n e)").rearrange("p (n e) -> p n e", e=NE), TAKEN, lg, ALU.mult, ALU.add))
    step.then(dve.tensor_tensor(w["d"][:], w["m"][:, 1, :], w["m"][:, 0, :], ALU.subtract))


def weigh(dve, step, w):
    step.then(dve.tensor_scalar(w["p"][:, 0, :], w["d"][:], 1.0, None, ALU.add))
    step.then(dve.reciprocal(w["p"][:, 0, :], w["p"][:, 0, :]))
    step.then(dve.tensor_tensor(w["p"][:, 1, :], w["d"][:], w["p"][:, 0, :], ALU.mult))
    full = [P, NT, NE]
    a, b = w["oh"]
    step.then(dve.tensor_tensor(w["e"][:], b[:], wide(w["p"][:, 1, :].unsqueeze(2), full), ALU.mult))
    step.then(dve.tensor_tensor(w["gate"], a[:], wide(w["p"][:, 0, :].unsqueeze(2), full), ALU.mult))
    step.then(dve.tensor_tensor(w["gate"], w["gate"], w["e"][:], ALU.add))


def routing_memory(C, ctx, tag, G):
    w = {"m": C.sb(tag + "m", [P, 2, NT], ctx=ctx), "e": C.sb(tag + "e", [P, NT, NE], ctx=ctx),
         "idx": C.sb(tag + "idx", [P, NT], ctx=ctx), "d": C.sb(tag + "d", [P, NT], ctx=ctx),
         "oh": [C.sb(tag + f"oh{k}", [P, NT, NE], ctx=ctx) for k in range(2)],
         "p": C.sb(tag + "p", [P, 2, NT], ctx=ctx), "gate": G.gate[:]}
    return w


def first_mlp_and_router(nc, C, A, G, clear, load):
    gv, bv = VEC["L0_xattn_g_ffn"][0], VEC["L0_xattn_b_ffn"][0]
    b1, rb1 = VEC["L0_xattn_b1"][0], VEC["L0_ffn_rb1"][0]
    NH = HID // P
    with ExitStack() as ctx:
        def two(name, shape):
            return [C.sb(f"{name}{j}", shape, ctx=ctx) for j in range(2)]

        w1, rw1 = C.sb("w1", [D, HID], ctx=ctx), C.sb("rw1", [D, HID], ctx=ctx)
        w2, rw2 = C.sb("w2", [P, NH, D], ctx=ctx), C.sb("rw2", [P, NH, NE], ctx=ctx)
        b2, gout, bout, rb2 = (C.sb(n, [P, k], ctx=ctx) for n, k in (("b2", D), ("gout", D), ("bout", D), ("rb2", NE)))
        xs, xf, xf1 = two("mlp_xs", [P, TB, D]), two("mlp_xf", [D, TB * P]), two("rt_xf", [D, TB * P])
        hs, rs = two("mlp_hs", [P, NH, TB * P]), two("rt_rs", [P, NH, TB * P])
        nb = C.sb("mlp_nb", [P, TB, D], ctx=ctx)
        st = [{n: C.sb(f"mlp_ln{q}_{n}", sh, ctx=ctx) for n, sh in (("st", [P, TB, 6]), ("mv", [P, TB, 2]), ("v", [P, TB]),
               ("a", [P, TB]), ("rstd", [P, TB]))} for q in range(3)]
        lg = C.sb("rt_lg", [P, NT, NE], ctx=ctx)
        sel = C.sb("rt_sel", [P, NT, NE], ctx=ctx)
        run = [C.sb(f"rt_run{k}", [P, NT, NE], ctx=ctx) for k in range(2)]
        base = C.sb("rt_base", [P, NE], ctx=ctx)
        spare_i = C.sb("rt_spare_i", [P, 2, NT], dt=I32, ctx=ctx)
        spare = C.sb("rt_spare", [P, 2, NT], ctx=ctx)
        zeros = C.sb("rt_zeros", [P, 4, 2 * D], ctx=ctx)
        w = routing_memory(C, ctx, "rt_", G)
        pst = C.ps("mlp_pst", [P, TB * P], ctx)
        psh = [C.ps(f"mlp_psh{c}", [P, TB * P], ctx) for c in range(NH)]
        psy = [C.ps(f"mlp_psy{j}", [P, TB, D], ctx) for j in range(2)]
        psl = C.ps("rt_psl", [P, 2, NT, NE], ctx)
        s = {n: C.sem("mlp_" + n) for n in (
            "weights", "xs", "turned", "xf", "y", "y_taken", "biased", "xn", "turned1", "xf1", "logits",
            "d", "exp", "sel", "pos", "dve", "pool", "spare", "zeros", "cleared")}
        var, root = ([C.sem(f"mlp_{n}{q}") for q in range(3)] for n in ("var", "root"))
        h_ps, h_sb, r_ps, r_sb = ([C.sem(f"mlp_{n}{c}") for c in range(NH)] for n in ("h_ps", "h_sb", "r_ps", "r_sb"))

        def blk(t):
            return 0 <= t < NBLK

        with nc.Block() as block:

            @block.sync
            def _(sp):
                for dst, src in ((w1[:], A["L0_xattn_W1"]), (w2[:], A["L0_xattn_W2"].rearrange("(c p) d -> p c d", p=P)),
                                 (b2[:], A["L0_xattn_b2"].partition_broadcast(P)),
                                 (gout[:], A["L0_xattn_g_norm_out"].partition_broadcast(P)),
                                 (bout[:], A["L0_xattn_b_norm_out"].partition_broadcast(P)),
                                 (rw1[:], A["L0_ffn_rw1"]), (rw2[:], A["L0_ffn_rw2"].rearrange("(c p) e -> p c e", p=P)),
                                 (rb2[:], A["L0_ffn_rb2"].partition_broadcast(P))):
                    sp.dma_start(dst, src).then_inc(s["weights"], 16)
                sp.wait_ge(s["zeros"], 1)
                z = zeros[:].rearrange("p a d -> p (a d)")
                for k in range(NE * CAP // P // 8):
                    sp.dma_start(G.slots_in[k * 8 * P:(k + 1) * 8 * P, :].rearrange("(p r) d -> p (r d)", p=P), z).then_inc(s["cleared"], 16)
                load(sp)
                sp.wait_ge(s["cleared"], NE * CAP // P // 8 * 16)

            @block.gpsimd
            def _(pool):
                pool.memset(zeros[:], 0.0).then_inc(s["zeros"], 1)
                clear(pool)
                pool.iota(spare_i[:], pattern=[[P * NT, 2], [P, NT]], base=NE * CAP, channel_multiplier=1).then_inc(s["spare"], 1)
                pool.wait_ge(s["weights"], 8 * 16)
                step = Steps(pool, s["pool"])
                for t in range(-2, NBLK + 1):
                    for q, b in ((0, t + 2), (1, t - 1), (2, t - 1)):
                        if blk(b):
                            pool.wait_ge(var[q], b + 1)
                            inverse_root(pool, step, st[q], root[q])
                    if blk(t + 2):
                        rows = slice((t + 2) * TB, (t + 3) * TB)
                        pool.wait_ge(s["xs"], t + 3)
                        pool.tensor_tensor(G.XT[:, rows, :], G.XT[:, rows, :], wide(b2[:].unsqueeze(1), [P, TB, D]), ALU.add)
                        pool.tensor_tensor(G.X[:, rows, :], G.X[:, rows, :], wide(bout[:].unsqueeze(1), [P, TB, D]), ALU.add).then_inc(s["biased"], 1)

            @block.tensor
            def _(pe):
                pe.wait_ge(s["weights"], 8 * 16)
                for t in range(-1, NBLK + 3):
                    if blk(t + 1):
                        j = (t + 1) % 2
                        pe.wait_ge(s["xs"], t + 2)
                        after(pe, s["xf"], t + 1)
                        after(pe, s["xf1"], t - 2)
                        for k in range(TB):
                            mm = pe.transpose(pst[:, k * P:(k + 1) * P], xs[j][:, k, :], G.ident[:])
                        mm.then_inc(s["turned"], 1)
                    if blk(t):
                        pe.wait_ge(s["xf"], t + 1)
                        for c in range(NH):
                            after(pe, r_sb[c], t - 2)
                            pe.matmul(psh[c][:], w1[:, c * P:(c + 1) * P], xf[t % 2][:], start=True, stop=True).then_inc(h_ps[c], 1)
                    if blk(t - 3):
                        b = t - 3
                        for c in range(NH):
                            pe.wait_ge(r_sb[c], b + 1)
                            for k in range(TB):
                                mm = pe.matmul(psl[:, 0, b * TB + k, :], rs[b % 2][:, c, k * P:(k + 1) * P], rw2[:, c, :],
                                               start=(c == 0 and k == 0), stop=(c == NH - 1), skip_group_check=True)
                        mm.then_inc(s["logits"], 1)
                    if blk(t - 2):
                        b = t - 2
                        pe.wait_ge(s["xn"], b + 1)
                        after(pe, s["xf"], min(t + 2, NBLK))
                        for k in range(TB):
                            mm = pe.transpose(pst[:, k * P:(k + 1) * P], G.XT[:, b * TB + k, :], G.ident[:])
                        mm.then_inc(s["turned1"], 1)
                    if blk(t):
                        after(pe, s["y_taken"], t - 1)
                        for c in range(NH):
                            pe.wait_ge(h_sb[c], t + 1)
                            for k in range(TB):
                                mm = pe.matmul(psy[t % 2][:, k, :], hs[t % 2][:, c, k * P:(k + 1) * P], w2[:, c, :],
                                               start=(c == 0 and k == 0), stop=(c == NH - 1), skip_group_check=True)
                        mm.then_inc(s["y"], 1)
                    if blk(t - 2):
                        b = t - 2
                        pe.wait_ge(s["xf1"], b + 1)
                        for c in range(NH):
                            after(pe, h_sb[c], min(t + 1, NBLK))
                            pe.matmul(psh[c][:], rw1[:, c * P:(c + 1) * P], xf1[b % 2][:], start=True, stop=True).then_inc(r_ps[c], 1)
                pe.wait_ge(s["sel"], 1)
                pe.matmul(psl[:, 1, :, :], G.triu[:], sel[:], start=True, stop=False)
                pe.matmul(psl[:, 1, :, :], G.ones[:], run[1][:], start=False, stop=True).then_inc(s["pos"], 1)

            @block.scalar
            def _(act):
                act.preload_act_table(ACT.Gelu)
                for t in range(-1, NBLK + 2):
                    if blk(t + 1):
                        act.wait_ge(s["turned"], t + 2)
                        act.activation(xf[(t + 1) % 2][:], pst[:], ACT.Identity, scale=G.vec[:, gv:gv + 1],
                                       bias=G.vec[:, bv:bv + 1]).then_inc(s["xf"], 1)
                    if blk(t):
                        for c in range(NH):
                            act.wait_ge(h_ps[c], t + 1)
                            act.activation(hs[t % 2][:, c, :], psh[c][:], ACT.Gelu, bias=G.vec[:, b1 + c:b1 + c + 1]).then_inc(h_sb[c], 1)
                    if blk(t - 2):
                        b = t - 2
                        act.wait_ge(s["turned1"], b + 1)
                        act.activation(xf1[b % 2][:], pst[:], ACT.Identity).then_inc(s["xf1"], 1)
                        for c in range(NH):
                            act.wait_ge(r_ps[c], b + 1)
                            act.activation(rs[b % 2][:, c, :], psh[c][:], ACT.Relu, bias=G.vec[:, rb1 + c:rb1 + c + 1]).then_inc(r_sb[c], 1)
                act.wait_ge(s["d"], 1)
                act.activation(w["d"][:], w["d"][:], ACT.Exp).then_inc(s["exp"], 1)

            @block.vector
            def _(dve):
                step = Steps(dve, s["dve"])
                dve.wait_ge(s["weights"], 8 * 16)
                for t in range(-2, NBLK + 2):
                    close, last = t - 1, t - 2
                    if blk(last):
                        x, xt = (m[:, last * TB:(last + 1) * TB, :] for m in (G.X, G.XT))
                        dve.wait_ge(root[2], last + 1)
                        normalise_block(dve, xt, x, st[2]).then_inc(s["xn"], 1)
                    if blk(t + 2):
                        b = t + 2
                        x = G.XT[:, b * TB:(b + 1) * TB, :]
                        after(dve, s["xs"], b)
                        block_statistics(dve, step, x, st[0]).then_inc(var[0], 1)
                    if blk(close):
                        xt = G.XT[:, close * TB:(close + 1) * TB, :]
                        dve.wait_ge(s["y"], close + 1)
                        dve.wait_ge(s["biased"], close + 1)
                        dve.tensor_tensor(xt, xt, psy[close % 2][:], ALU.add).then_inc(s["y_taken"], 1)
                        dve.wait_ge(s["y_taken"], close + 1)
                        block_statistics(dve, step, xt, st[1]).then_inc(var[1], 1)
                    if blk(t + 2):
                        dve.wait_ge(root[0], b + 1)
                        after(dve, s["turned"], b - 1)
                        normalise_block(dve, xs[b % 2], x, st[0]).then_inc(s["xs"], 1)
                    if blk(close):
                        x = G.X[:, close * TB:(close + 1) * TB, :]
                        dve.wait_ge(root[1], close + 1)
                        step.then(normalise_block(dve, nb, xt, st[1]))
                        step.then(dve.tensor_tensor(nb[:], nb[:], wide(gout[:].unsqueeze(1), [P, TB, D]), ALU.mult))
                        step.then(dve.tensor_tensor(x, x, nb[:], ALU.add))
                        after(dve, s["xn"], close)
                        block_statistics(dve, step, x, st[2]).then_inc(var[2], 1)
                dve.wait_ge(s["logits"], NBLK)
                step.then(dve.tensor_tensor(lg[:], psl[:, 0, :, :], wide(rb2[:].unsqueeze(1), [P, NT, NE]), ALU.add))
                two_largest(dve, step, C, G, lg[:], w, G.iota8)
                dve.sem_inc(s["d"], 1)
                step.then(dve.tensor_tensor(sel[:], w["oh"][0][:], w["oh"][1][:], ALU.add))
                dve.memset(run[0][:, 0, :], 0.0)
                step.then(dve.tensor_copy(run[0][:, 1:NT, :], sel[:, 0:NT - 1, :]))
                src, k = 0, 1
                while k < NT:
                    dve.tensor_copy(run[1 - src][:, 0:k, :], run[src][:, 0:k, :])
                    step.then(dve.tensor_tensor(run[1 - src][:, k:NT, :], run[src][:, k:NT, :], run[src][:, 0:NT - k, :], ALU.add))
                    src, k = 1 - src, 2 * k
                assert src == 1
                dve.sem_inc(s["sel"], 1)
                dve.wait_ge(s["exp"], 1)
                weigh(dve, step, w)
                dve.wait_ge(s["pos"], 1)
                step.then(dve.tensor_scalar(w["e"][:], psl[:, 1, :, :], float(CAP), None, ALU.is_lt))
                step.then(dve.tensor_tensor(G.gate[:], G.gate[:], w["e"][:], ALU.mult))
                dve.wait_ge(s["spare"], 1)
                step.did(dve.tensor_copy(spare[:], spare_i[:]))
                step.then(dve.tensor_scalar(base[:], G.iota8[:], float(CAP), float(NE * CAP), ALU.mult, ALU.add))
                step.then(dve.tensor_tensor(sel[:], psl[:, 1, :, :], wide(base[:].unsqueeze(1), [P, NT, NE]), ALU.add))
                slot, keep = w["m"][:, 0, :], w["m"][:, 1, :]
                for k in range(2):
                    oh = w["oh"][k]
                    step.then(dve.tensor_tensor(lg[:], oh[:], sel[:], ALU.mult))
                    step.then(dve.tensor_reduce(slot, lg[:], AX.X, ALU.add))
                    step.then(dve.tensor_tensor(lg[:], oh[:], w["e"][:], ALU.mult))
                    step.then(dve.tensor_reduce(keep, lg[:], AX.X, ALU.add))
                    step.did(dve.tensor_tensor(G.prob[:, k, :], w["p"][:, k, :], keep, ALU.mult))
                    step.then(dve.tensor_tensor(slot, slot, keep, ALU.mult))
                    step.did(dve.tensor_copy(G.slot_out[:, k, :], slot))
                    step.then(dve.tensor_tensor(keep, spare[:, k, :], keep, ALU.mult))
                    step.then(dve.tensor_tensor(keep, spare[:, k, :], keep, ALU.subtract))
                    step.then(dve.tensor_tensor(slot, slot, keep, ALU.add))
                    step.then(dve.tensor_copy(G.slot_in[:, k, :], slot))


def prepare_biases(C, A, tag, name, ctx):
    gs = C.sb(tag + "gs", [P, NBLK, TB, 32], ctx=ctx)
    bd = C.sb(tag + "bd", [P, TB, D], ctx=ctx)
    zero, loaded = C.sem(tag + "zero"), C.sem(tag + "loaded")

    def clear(pool):
        pool.memset(bd[:], 0.0).then_inc(zero, 1)
        pool.memset(gs[:], 0.0).then_inc(zero, 1)

    def load(sp):
        sp.wait_ge(zero, 2)
        for k in range(TB):
            sp.dma_start(bd[32 * k:32 * k + NE, k, :], A[name]).then_inc(loaded, 16)
        sp.wait_ge(loaded, TB * 16)

    return (gs, bd), clear, load


def add_gated_biases(nc, C, G, tag, memory, beside=None):
    with ExitStack() as ctx:
        gs, bd = memory
        gt = C.sb(tag + "gt", [P, NBLK, P], ctx=ctx)
        pst = [C.ps(f"{tag}pst{j}", [P, NBLK // 2, P], ctx) for j in range(2)]
        psy = [C.ps(f"{tag}psy{j}", [P, TB, D], ctx) for j in range(6)]
        s = {n: C.sem(tag + n) for n in ("gs", "turned", "turned_sb", "y", "x")}
        with nc.Block() as block:

            if beside:
                @block.gpsimd
                def _(pool):
                    beside(pool)

            @block.tensor
            def _(pe):
                pe.wait_ge(s["gs"], 1)
                for half in range(2):
                    for k in range(NBLK // 2):
                        b = half * (NBLK // 2) + k
                        mm = pe.transpose(pst[half][:, k, :], gs[:, b, :, :].rearrange("p k e -> p (k e)"), G.ident[:])
                    mm.then_inc(s["turned"], 1)
                for b in range(NBLK):
                    pe.wait_ge(s["turned_sb"], b // (NBLK // 2) + 1)
                    after(pe, s["x"], b - len(psy) + 1)
                    pe.matmul(psy[b % len(psy)][:], gt[:, b, :], bd[:], start=True, stop=True).then_inc(s["y"], 1)

            @block.scalar
            def _(act):
                for half in range(2):
                    act.wait_ge(s["turned"], half + 1)
                    act.activation(gt[:, half * NBLK // 2:(half + 1) * NBLK // 2, :], pst[half][:], ACT.Copy).then_inc(s["turned_sb"], 1)

            @block.vector
            def _(dve):
                dve.tensor_copy(gs[:, :, :, 0:NE], G.gate[:].rearrange("p (b k) e -> p b k e", k=TB)).then_inc(s["gs"], 1)
                for b in range(NBLK):
                    dve.wait_ge(s["y"], b + 1)
                    rows = G.X[:, b * TB:(b + 1) * TB, :]
                    dve.tensor_tensor(rows, rows, psy[b % len(psy)][:], ALU.add).then_inc(s["x"], 1)


def send_rows(C, G):
    sent = C.sem("rows_sent")

    def send(pool):
        for t in range(NT):
            for k in range(2):
                pool.indirect_dma_start(G.slots_in, bass.IndirectOffsetOnAxis(ap=G.slot_in[:, k, t:t + 1], axis=0),
                                        G.XT[:, t, :], None).then_inc(sent, 16)
        pool.wait_ge(sent, 2 * NT * 16)

    return send


def first_experts(nc, C, A, G):
    eb1 = VEC["L0_ffn_eb1"][0]
    S = CAP // P
    with ExitStack() as ctx:
        w1 = [C.sb(f"ew1{j}", [D, HID], ctx=ctx) for j in range(2)]
        w2 = [C.sb(f"ew2{j}", [P, 4, D], ctx=ctx) for j in range(2)]
        xr = [C.sb(f"ex_rows{j}", [P, S, D], ctx=ctx) for j in range(2)]
        xt = [C.sb(f"ex_turned{j}", [D, CAP], ctx=ctx) for j in range(2)]
        hs = [C.sb(f"ex_hs{j}", [P, 4, CAP], ctx=ctx) for j in range(2)]
        ys = [C.sb(f"ex_ys{j}", [P, S, D], ctx=ctx) for j in range(2)]
        psh = [C.ps(f"ex_psh{c}", [P, CAP], ctx) for c in range(4)]
        pst = C.ps("ex_pst", [P, CAP], ctx)
        psy = [C.ps(f"ex_psy{j}", [P, S, D], ctx) for j in range(2)]
        s = {n: C.sem("ex_" + n) for n in ("turned", "turned_sb", "y", "y_sb")}
        h_ps = [C.sem(f"ex_h_ps{c}") for c in range(4)]
        h_sb = [C.sem(f"ex_h_sb{c}") for c in range(4)]
        loaded = [C.sem(f"ex_weights{j}") for j in range(2)]
        rows = [C.sem(f"ex_rows_loaded{j}") for j in range(2)]
        kept = [C.sem(f"ex_kept{j}") for j in range(2)]
        slots_in = G.slots_in[0:NE * CAP, :].rearrange("(e k p) d -> e p k d", p=P, k=S)
        slots_out = G.slots_out.rearrange("(e k p) d -> e p k d", p=P, k=S)
        with nc.Block() as block:

            @block.sync
            def _(sp):
                for e in range(NE):
                    j = e % 2
                    if e >= 2:
                        sp.wait_ge(s["y"], e - 1)
                    sp.dma_start(xr[j][:], slots_in[e]).then_inc(rows[j], 16)
                    sp.dma_start(w1[j][:], A["L0_ffn_ew1"][e]).then_inc(loaded[j], 16)
                    sp.dma_start(w2[j][:], A["L0_ffn_ew2"][e].rearrange("(c p) d -> p c d", p=P)).then_inc(loaded[j], 16)
                    if e >= 2:
                        sp.wait_ge(s["y_sb"], e - 1)
                        sp.dma_start(slots_out[e - 2], ys[j][:]).then_inc(kept[j], 16)
                for e in (NE - 2, NE - 1):
                    sp.wait_ge(s["y_sb"], e + 1)
                    sp.dma_start(slots_out[e], ys[e % 2][:]).then_inc(kept[e % 2], 16)
                for j in range(2):
                    sp.wait_ge(kept[j], NE // 2 * 16)

            @block.tensor
            def _(pe):
                def turn(e):
                    pe.wait_ge(rows[e % 2], (e // 2 + 1) * 16)
                    after(pe, s["turned_sb"], e)
                    for k in range(S):
                        mm = pe.transpose(pst[:, k * P:(k + 1) * P], xr[e % 2][:, k, :], G.ident[:])
                    mm.then_inc(s["turned"], 1)

                turn(0)
                for e in range(NE):
                    j = e % 2
                    pe.wait_ge(loaded[j], (e // 2 + 1) * 32)
                    pe.wait_ge(s["turned_sb"], e + 1)
                    for c in range(4):
                        after(pe, h_sb[c], e)
                        pe.matmul(psh[c][:], w1[j][:, c * P:(c + 1) * P], xt[j][:], start=True, stop=True).then_inc(h_ps[c], 1)
                    if e + 1 < NE:
                        turn(e + 1)
                    after(pe, s["y_sb"], e - 1)
                    for c in range(4):
                        pe.wait_ge(h_sb[c], e + 1)
                        for k in range(S):
                            mm = pe.matmul(psy[j][:, k, :], hs[j][:, c, k * P:(k + 1) * P], w2[j][:, c, :],
                                           start=(c == 0 and k == 0), stop=(c == 3), skip_group_check=True)
                    mm.then_inc(s["y"], 1)

            @block.scalar
            def _(act):
                act.preload_act_table(ACT.Relu)
                for e in range(NE):
                    after(act, s["y"], e - 1)
                    for c in range(4):
                        act.wait_ge(h_ps[c], e + 1)
                        v = eb1 + 4 * e + c
                        act.activation(hs[e % 2][:, c, :], psh[c][:], ACT.Relu, bias=G.vec[:, v:v + 1]).then_inc(h_sb[c], 1)

            @block.vector
            def _(dve):
                def keep_rows(e):
                    dve.wait_ge(s["y"], e + 1)
                    after(dve, kept[e % 2], e // 2 * 16)
                    dve.tensor_copy(ys[e % 2][:], psy[e % 2][:]).then_inc(s["y_sb"], 1)

                for e in range(NE):
                    dve.wait_ge(s["turned"], e + 1)
                    dve.tensor_copy(xt[e % 2][:], pst[:]).then_inc(s["turned_sb"], 1)
                    if e > 0:
                        keep_rows(e - 1)
                keep_rows(NE - 1)


def second_attention(nc, C, A, G):
    bqi, bki, bvi = (VEC["L1_xattn_" + n][0] for n in ("bq", "bk", "bv"))
    HG = 4
    W = 2 * (DH1 + 1)
    with ExitStack() as ctx:
        def two(name, shape):
            return [C.sb(f"a1_{name}{j}", shape, ctx=ctx) for j in range(2)]

        wq, wk, wv, wo = (C.sb("a1_w" + n, [k, D], ctx=ctx) for n, k in (("q", D), ("k", DC), ("v", DC), ("o", D)))
        bo = C.sb("a1_bo", [P, D], ctx=ctx)
        sca = C.sb("a1_scale", [P, 1], ctx=ctx)
        bqs = C.sb("a1_bqs", [P, 1], ctx=ctx)
        m4 = C.sb("a1_m4", [P, HG], ctx=ctx)
        bk4 = C.sb("a1_bk4", [P, HG], ctx=ctx)
        c2, vb = two("c2", [DC, P]), two("vb", [P, 2, H1 // 2, 2, DH1 + 1])
        qt, kb = two("qt", [P, P]), two("kb", [P, 2, HG, T])
        mx, dd, pp = two("mx", [P, H1]), two("dd", [P, H1, T]), two("pp", [P, H1, T])
        pt = two("pt", [P, H1 // 2, P])
        rc, oo, of = two("rc", [P, H1]), two("oo", [P, H1, DH1]), two("of", [P, P])
        psx = C.ps("a1_psx", [P, 512], ctx)
        pss = [C.ps(f"a1_pss{h}", [P, 2, 512], ctx) for h in range(2)]
        psp = [C.ps(f"a1_psp{h}", [P, 4, P], ctx) for h in range(2)]
        pso = C.ps("a1_pso", [P, 512], ctx)
        s = {n: C.sem("a1_" + n) for n in (
            "weights", "ready", "zero", "c2", "qk", "qk_sb", "v", "v_sb", "scores", "scores_sb", "exp",
            "turned", "turned_sb", "o", "o_sb", "o_turned", "of", "y", "x", "dve", "pool")}
        with nc.Block() as block:
            SWEEP = (-2, 3, 29, NT + 1)

            @block.sync
            def _(sp):
                for dst, name in ((wq, "Wq"), (wk, "Wk"), (wv, "Wv"), (wo, "Wo")):
                    sp.dma_start(dst[:], A["L1_xattn_" + name]).then_inc(s["weights"], 16)
                sp.dma_start(bo[:], A["L1_xattn_bo"].partition_broadcast(P)).then_inc(s["weights"], 16)
                sp.dma_start(sca[:], A["L1_xattn_scale"].partition_broadcast(P)).then_inc(s["weights"], 16)

            @block.gpsimd
            def _(pool):
                step = Steps(pool, s["pool"])
                step.then(pool.memset(m4[:], 1.0))
                for g in range(4):
                    rows = m4[32 * g:32 * g + 32, :]
                    step.then(pool.affine_select(out=rows, in_=rows, compare_op=ALU.is_ge, fill=0.0,
                                                 base=0, pattern=[[-DH1, HG]], channel_multiplier=1))
                    step.then(pool.affine_select(out=rows, in_=rows, compare_op=ALU.is_ge, fill=0.0,
                                                 base=DH1 - 1, pattern=[[DH1, HG]], channel_multiplier=-1))
                for j in range(2):
                    step.did(pool.memset(vb[j][:], 0.0))
                step.wait()
                for j in range(2):
                    step.did(pool.memset(vb[j][0:T, :, :, 0, DH1:DH1 + 1], 1.0))
                    step.did(pool.memset(vb[j][T:P, :, :, 1, DH1:DH1 + 1], 1.0))
                step.wait()
                pool.sem_inc(s["zero"], 1)

                def slot(x):
                    g = x.by(1)
                    if g.real():
                        after(pool, s["v"], g.t - 1)
                        pool.tensor_copy(c2[g.j][:], G.ctxT[:, bass.ds(g.t * P, P)]).then_inc(s["c2"], 1)

                sweep(pool, slot, *SWEEP)

            @block.tensor
            def _(pe):
                pe.wait_ge(s["weights"], 96)

                def scores(g, half):
                    if not g.real():
                        return
                    j = g.j
                    if half == 0:
                        pe.wait_ge(s["qk_sb"], g.t + 1)
                    after(pe, s["scores_sb"], g.t * 2 + half - 1)
                    for b in range(2):
                        for h in range(2):
                            rows = slice(64 * half + 32 * h, 64 * half + 32 * h + 32)
                            mm = pe.matmul(pss[half][T * b:T * b + T, h, 0:HG * T], qt[j][rows, T * b:T * b + T],
                                           kb[j][rows, b, :, :], start=True, stop=True)
                    mm.then_inc(s["scores"], 1)

                def slot(x):
                    a, g, c = x.by(2), x.by(1), x.by(-1)
                    scores(g, 0)
                    if c.real():
                        pe.wait_ge(s["o_sb"], c.t + 1)
                        pe.transpose(pso[:, 384:512], oo[c.j][:].rearrange("p h d -> p (h d)"), G.ident[:]).then_inc(s["o_turned"], 1)
                    if a.real():
                        tok = bass.ds(a.t * P, P)
                        after(pe, s["v_sb"], a.t - 1)
                        after(pe, s["qk_sb"], a.t)
                        pe.matmul(psx[:, 0:P], wq[:], G.XF[:, tok], start=True, stop=True)
                        pe.matmul(psx[:, P:2 * P], wk[:], G.ctxT[:, tok], start=True, stop=True).then_inc(s["qk"], 1)
                    if g.real():
                        pe.wait_ge(s["c2"], g.t + 1)
                        after(pe, s["v_sb"], g.t)
                        pe.matmul(psx[:, 2 * P:3 * P], c2[g.j][:], wv[:], start=True, stop=True).then_inc(s["v"], 1)
                    if c.real():
                        pe.wait_ge(s["of"], c.t + 1)
                        pe.matmul(pso[:, 384:512], of[c.j][:], wo[:], start=True, stop=True).then_inc(s["y"], 1)
                    if x.real():
                        for half in range(2):
                            pe.wait_ge(s["exp"], x.t * 2 + half + 1)
                            after(pe, s["turned_sb"], x.t * 2 + half - 1)
                            for k in range(4):
                                h = 8 * half + 2 * k
                                mm = pe.transpose(psp[half][:, k, :], pp[x.j][:, h:h + 2, :].rearrange("p h k -> p (h k)"), G.ident[:])
                            mm.then_inc(s["turned"], 1)
                    scores(g, 1)
                    if x.real():
                        pe.wait_ge(s["turned_sb"], x.t * 2 + 2)
                        pe.wait_ge(s["v_sb"], x.t + 1)
                        after(pe, s["x"], x.t)
                        for k in range(H1 // 2):
                            mm = pe.matmul(pso[:, 2 * W * k:2 * W * k + 2 * W], pt[x.j][:, k, :], vb[x.j][:, :, k, :, :],
                                           start=True, stop=True)
                        mm.then_inc(s["o"], 1)

                sweep(pe, slot, *SWEEP)

            @block.scalar
            def _(act):
                act.preload_act_table(ACT.Exp)
                act.wait_ge(s["ready"], 1)
                act.wait_ge(s["zero"], 1)
                ident = ACT.Identity

                def exp(x, half):
                    if x.real():
                        act.wait_ge(s["scores_sb"], x.t * 2 + half + 1)
                        h = slice(8 * half, 8 * half + 8)
                        act.activation(pp[x.j][:, h, :], dd[x.j][:, h, :], ACT.Exp).then_inc(s["exp"], 1)

                def slot(x):
                    a, g, c = x.by(2), x.by(1), x.by(-1)
                    exp(x, 1)
                    if c.real():
                        act.wait_ge(s["o_turned"], c.t + 1)
                        act.activation(of[c.j][:], pso[:, 384:512], ident, bias=G.vec[:, bvi:bvi + 1]).then_inc(s["of"], 1)
                    if g.real():
                        act.wait_ge(s["v"], g.t + 1)
                    if a.real():
                        act.wait_ge(s["qk"], a.t + 1)
                        act.activation(qt[a.j][:], psx[:, 0:P], ident, scale=sca[:, 0:1], bias=bqs[:, 0:1])
                        k = psx[:, P:2 * P].rearrange("p (b k) -> p b k", b=2)
                        for h in range(HG):
                            m = act.activation(kb[a.j][:, :, h, :], k, ident, scale=m4[:, h:h + 1], bias=bk4[:, h:h + 1])
                        m.then_inc(s["qk_sb"], 1)
                    if g.real():
                        v = psx[:, 2 * P:3 * P].rearrange("p (k c d) -> p k c d", c=2, d=DH1)
                        for b in range(2):
                            for odd in range(2):
                                m = act.activation(vb[g.j][T * odd:T * odd + T, b, :, odd, 0:DH1],
                                                   v[T * b:T * b + T, :, odd, :], ACT.Copy)
                        m.then_inc(s["v_sb"], 1)
                    if x.real():
                        for half in range(2):
                            act.wait_ge(s["turned"], x.t * 2 + half + 1)
                            act.activation(pt[x.j][:, 4 * half:4 * half + 4, :], psp[half][:], ACT.Copy).then_inc(s["turned_sb"], 1)
                    exp(g, 0)

                sweep(act, slot, *SWEEP)

            @block.vector
            def _(dve):
                step = Steps(dve, s["dve"])
                dve.wait_ge(s["weights"], 96)
                dve.wait_ge(s["zero"], 1)
                dve.tensor_scalar(bqs[:], G.vec[:, bqi:bqi + 1], sca[:, 0:1], None, ALU.mult)
                step.then(dve.tensor_scalar(bk4[:], m4[:], G.vec[:, bki:bki + 1], None, ALU.mult))
                dve.sem_inc(s["ready"], 1)
                step.then(dve.tensor_tensor(G.X[:], G.X[:], wide(bo[:].unsqueeze(1), [P, NT, D]), ALU.add))
                step.clear()

                def centre(g, half):
                    if not g.real():
                        return
                    heads = slice(8 * half, 8 * half + 8)
                    dve.wait_ge(s["scores"], g.t * 2 + half + 1)
                    src = pss[half][:, :, 0:HG * T].rearrange("p g (h k) -> p g h k", h=HG)
                    m = mx[g.j][:, heads].rearrange("p (g h) -> p g h", g=2)
                    step.then(dve.tensor_reduce(m, src, AX.X, ALU.max))
                    after(dve, s["exp"], g.t * 2 + half - 3)
                    out = dd[g.j][:, heads, :].rearrange("p (g h) k -> p g h k", g=2)
                    dve.tensor_tensor(out, src, wide(m.unsqueeze(3), [P, 2, HG, T]), ALU.subtract).then_inc(s["scores_sb"], 1)

                def slot(x):
                    g, c = x.by(1), x.by(-1)
                    if c.real():
                        dve.wait_ge(s["o"], c.t + 1)
                        o = pso[:, 0:2 * W * (H1 // 2)].rearrange("p (k b c d) -> p b k c d", b=2, c=2, d=DH1 + 1)
                        r = rc[c.j][:].rearrange("p (k c) -> p k c", c=2)
                        y = oo[c.j][:].rearrange("p (k c) d -> p k c d", c=2)
                        for b in range(2):
                            rows = slice(T * b, T * b + T)
                            step.did(dve.reciprocal(r[rows], o[rows, b, :, :, DH1]))
                        step.wait()
                        for b in range(2):
                            rows = slice(T * b, T * b + T)
                            m = dve.tensor_tensor(y[rows], o[rows, b, :, :, 0:DH1], wide(r[rows].unsqueeze(3), [T, H1 // 2, 2, DH1]), ALU.mult)
                        m.then_inc(s["o_sb"], 1)
                    centre(g, 0)
                    if c.real():
                        dve.wait_ge(s["y"], c.t + 1)
                        row = G.X[:, c.t, :]
                        dve.tensor_tensor(row, row, pso[:, 384:512], ALU.add).then_inc(s["x"], 1)
                    centre(g, 1)
                    if g.real() or c.real():
                        step.clear()

                sweep(dve, slot, *SWEEP)


def second_router(nc, C, A, G, clear, load):
    with ExitStack() as ctx:
        wg = C.sb("g1_wg", [NE, D], ctx=ctx)
        wgt = C.sb("g1_wgt", [D, NE], ctx=ctx)
        lg = C.sb("g1_lg", [P, NT, NE], ctx=ctx)
        w = routing_memory(C, ctx, "g1_", G)
        psw = C.ps("g1_psw", [P, NE], ctx)
        psl = C.ps("g1_psl", [P, NT, NE], ctx)
        s = {n: C.sem("g1_" + n) for n in ("wg", "wg_ps", "wg_sb", "logits", "d", "exp", "dve")}
        with nc.Block() as block:

            @block.sync
            def _(sp):
                sp.dma_start(wg[:], A["L1_ffn_Wg"]).then_inc(s["wg"], 16)
                load(sp)

            @block.gpsimd
            def _(pool):
                clear(pool)

            @block.tensor
            def _(pe):
                pe.wait_ge(s["wg"], 16)
                pe.transpose(psw[:], wg[:], G.ident[0:NE, 0:NE]).then_inc(s["wg_ps"], 1)
                pe.wait_ge(s["wg_sb"], 1)
                for t in range(NT):
                    mm = pe.matmul(psl[:, t, :], G.XF[:, t * P:(t + 1) * P], wgt[:], start=True, stop=True)
                mm.then_inc(s["logits"], 1)

            @block.scalar
            def _(act):
                act.preload_act_table(ACT.Exp)
                act.wait_ge(s["wg_ps"], 1)
                act.activation(wgt[:], psw[:], ACT.Copy).then_inc(s["wg_sb"], 1)
                act.wait_ge(s["d"], 1)
                act.activation(w["d"][:], w["d"][:], ACT.Exp).then_inc(s["exp"], 1)

            @block.vector
            def _(dve):
                step = Steps(dve, s["dve"])
                dve.wait_ge(s["logits"], 1)
                step.then(dve.tensor_copy(lg[:], psl[:]))
                two_largest(dve, step, C, G, lg[:], w, G.iota8)
                dve.sem_inc(s["d"], 1)
                dve.wait_ge(s["exp"], 1)
                weigh(dve, step, w)


def second_experts(nc, C, A, G):
    b1i, b3i = VEC["L1_ffn_b1"][0], VEC["L1_ffn_b3"][0]
    NC = HE // P
    with ExitStack() as ctx:
        def two(name, shape, dt=F32):
            return [C.sb(f"e1_{name}{j}", shape, dt, ctx=ctx) for j in range(2)]

        wh, wl = (two(n, [D, 2, NC, P], F32R) for n in ("wh", "wl"))
        XH, XL = C.sb("e1_XH", [D, B * T], F32R, ctx=ctx), C.sb("e1_XL", [D, B * T], F32R, ctx=ctx)
        sg = two("sg", [P, NC, TB * P])
        hh = two("hh", [P, NC, TB * P])
        psh = [[C.ps(f"e1_ps{m}{c}", [P, TB * P], ctx) for c in range(NC)] for m in (1, 3)]
        psy = [C.ps(f"e1_psy{j}", [P, TB, D], ctx) for j in range(2)]
        s = {n: C.sem("e1_" + n) for n in ("w_high", "w_low", "x_high", "x_low", "y", "y_sum", "stored")}
        h_ps = [[C.sem(f"e1_h{m}_ps{c}") for c in range(NC)] for m in (1, 3)]
        silu = [C.sem(f"e1_silu{c}") for c in range(NC)]
        hh_sb = [C.sem(f"e1_hh{c}") for c in range(NC)]
        with nc.Block() as block:
            def experts(eng, slot, cut=None):
                if cut:
                    cut(0)
                for e in range(NE):
                    for b in range(2):
                        slot(e, b, e * NBLK + b, b % 2)
                    if cut and e + 1 < NE:
                        cut(e + 1)
                    with eng.Fori(0, (NBLK - 2) // 2) as i:
                        for j in range(2):
                            slot(e, i * 2 + (2 + j), i * 2 + (e * NBLK + 2 + j), j)

            @block.sync
            def _(sp):
                ov = G.out.rearrange("(n b) t d -> (b t) n d", b=2)
                for b in range(NBLK):
                    rows = slice(b * TB, (b + 1) * TB)
                    sp.wait_ge(s["y_sum"], (NE - 1) * NBLK + b + 1)
                    sp.dma_start(ov[:, rows, :], G.X[:, rows, :]).then_inc(s["stored"], 16)
                sp.wait_ge(s["stored"], NBLK * 16)

            @block.tensor
            def _(pe):
                def product(e, n, j):
                    after(pe, s["y_sum"], n - 1)
                    for c in range(NC):
                        pe.wait_ge(hh_sb[c], n + 1)
                        for k in range(TB):
                            mm = pe.matmul(psy[j][:, k, :], hh[j][:, c, k * P:(k + 1) * P], G.w2[:, e, c, :],
                                           start=(c == 0 and k == 0), stop=(c == NC - 1), skip_group_check=True)
                    mm.then_inc(s["y"], 1)

                def slot(e, b, n, j):
                    if isinstance(b, int) and b == 0:
                        pe.wait_ge(s["w_low"], e + 1)
                    if e == 0:
                        pe.wait_ge(s["x_low"], b + 1)
                    x, xl = (m[:, bass.ds(b * TB * P, TB * P)] for m in (XH, XL))
                    for c in range(NC):
                        for m in range(2):
                            after(pe, hh_sb[c], n)
                            pe.matmul(psh[m][c][:], wh[e % 2][:, m, c, :], x, start=True, stop=False)
                            pe.matmul(psh[m][c][:], wh[e % 2][:, m, c, :], xl, start=False, stop=False)
                            pe.matmul(psh[m][c][:], wl[e % 2][:, m, c, :], x, start=False, stop=True).then_inc(h_ps[m][c], 1)
                    if isinstance(b, int) and b == 0:
                        if e > 0:
                            product(e - 1, n - 1, 1 - j)
                    else:
                        product(e, n - 1, 1 - j)

                experts(pe, slot)
                product(NE - 1, NE * NBLK - 1, 1)

            @block.scalar
            def _(act):
                act.preload_act_table(ACT.Silu)

                def slot(e, b, n, j):
                    for c in range(NC):
                        k = b1i + NC * e + c
                        act.wait_ge(h_ps[0][c], n + 1)
                        act.activation(sg[j][:, c, :], psh[0][c][:], ACT.Silu, bias=G.vec[:, k:k + 1]).then_inc(silu[c], 1)

                experts(act, slot)

            @block.gpsimd
            def _(pool):
                for b in range(NBLK):
                    t = slice(b * TB * P, (b + 1) * TB * P)
                    pool.wait_ge(s["x_high"], b + 1)
                    pool.tensor_tensor(XL[:, t], G.XF[:, t], XH[:, t].bitcast(F32), ALU.subtract).then_inc(s["x_low"], 1)
                for e in range(NE):
                    pool.wait_ge(s["w_high"], e + 1)
                    pool.tensor_tensor(wl[e % 2][:], G.w13[:, e, :, :, :], wh[e % 2][:].bitcast(F32), ALU.subtract).then_inc(s["w_low"], 1)

            @block.vector
            def _(dve):
                def cut(e):
                    dve.tensor_copy(wh[e % 2][:], G.w13[:, e, :, :, :]).then_inc(s["w_high"], 1)

                def take(e, b, n, j):
                    dve.wait_ge(s["y"], n + 1)
                    if e > 0:
                        after(dve, s["y_sum"], n + 1 - NBLK)
                    for k in range(TB):
                        row = G.X[:, bass.ds(b * TB + k, 1), :].rearrange("p a d -> p (a d)")
                        gate = G.gate[:, bass.ds(b * TB + k, 1), e:e + 1].rearrange("p a e -> p (a e)")
                        st = dve.scalar_tensor_tensor(row, psy[j][:, k, :], gate, row, ALU.mult, ALU.add)
                    st.then_inc(s["y_sum"], 1)

                def slot(e, b, n, j):
                    for c in range(NC):
                        k = b3i + NC * e + c
                        dve.wait_ge(h_ps[1][c], n + 1)
                        dve.wait_ge(silu[c], n + 1)
                        dve.scalar_tensor_tensor(hh[j][:, c, :], psh[1][c][:], G.vec[:, k:k + 1], sg[j][:, c, :],
                                                 ALU.add, ALU.mult).then_inc(hh_sb[c], 1)
                    if isinstance(b, int) and b == 0:
                        if e > 0:
                            take(e - 1, NBLK - 1, n - 1, 1 - j)
                    else:
                        take(e, b - 1, n - 1, 1 - j)

                for b in range(NBLK):
                    t = slice(b * TB * P, (b + 1) * TB * P)
                    dve.tensor_copy(XH[:, t], G.XF[:, t]).then_inc(s["x_high"], 1)
                experts(dve, slot, cut)
                take(NE - 1, NBLK - 1, NE * NBLK - 1, 1)


class Globals:
    pass


def program(nc, A, out, last=99):
    with ExitStack() as ctx:
        C, G = Chip(nc, ctx), Globals()
        G.kd = nc.dram_tensor("s4d_kernel", (D, P), F32, kind="Internal").ap()
        G.slots_in = nc.dram_tensor("slots_in", (NE * CAP + 2 * B * T, D), F32, kind="Internal").ap()
        G.slots_out = nc.dram_tensor("slots_out", (NE * CAP, D), F32, kind="Internal").ap()
        G.out = out
        G.X = C.sb("X", [P, NT, D])
        G.XT = C.sb("XT", [P, NT, D])
        G.ctxT = C.sb("ctxT", [DC, B * T])
        G.ident = C.sb("ident", [P, P])
        G.triu = C.sb("triu", [P, P])
        G.ones = C.sb("ones", [P, P])
        G.onesrow = C.sb("onesrow", [1, P])
        G.iota8 = C.sb("iota8", [P, NE])
        G.vec = C.sb("vec", [P, NVEC])
        G.tmask = C.sb("tmask", [P, NT])
        G.mg = C.sb("mg", [P, 1])
        G.dt = C.sb("dt", [P, 1])
        G.rstd2 = C.sb("rstd2", [P, NT])
        with ExitStack() as early:
            G.XM = C.sb("XM", [P, NT, D], ctx=early)
            G.FO = C.sb("FO", [P, NT, 256], ctx=early)
            G.pen = C.sb("pen", [P, NT, T], ctx=early)
            G.gin = C.sb("gin", [P, D], ctx=early)
            G.bin = C.sb("bin", [P, D], ctx=early)
            G.wq = C.sb("wq", [P, P], ctx=early)
            G.wk = C.sb("wk", [DC, P], ctx=early)
            G.wv = C.sb("wv", [DC, D], ctx=early)
            G.film = C.sb("film", [P, 512], ctx=early)
            G.frow = C.sb("frow", [1, 512], ctx=early)
            setup(nc, C, A, G)
            C.end_phase()
            if last >= 1:
                first_attention(nc, C, A, G)
                C.end_phase()
            if last >= 2:
                convolution(nc, C, A, G)
                C.end_phase()
        with ExitStack() as late:
            G.XF = C.sb("XF", [D, B * T], ctx=late)
            G.gate = C.sb("gate", [P, NT, NE], ctx=late)
            G.slot_in = C.sb("slot_in", [P, 2, NT], dt=U32, ctx=late)
            G.slot_out = C.sb("slot_out", [P, 2, NT], dt=U32, ctx=late)
            G.prob = C.sb("prob", [P, 2, NT], ctx=late)
            G.w13 = C.sb("w13_folded", [D, NE, 2, HE // P, P], ctx=late)
            G.w2 = C.sb("w2_folded", [P, NE, HE // P, D], ctx=late)
            if last >= 3:
                with ExitStack() as ctx2:
                    memory, clear, load = prepare_biases(C, A, "gb0_", "L0_ffn_eb2", ctx2)
                    first_mlp_and_router(nc, C, A, G, clear, load)
                    C.end_phase()
                    add_gated_biases(nc, C, G, "gb0_", memory, send_rows(C, G))
                    C.end_phase()
            if last >= 6:
                first_experts(nc, C, A, G)
                C.end_phase()
            if last >= 7:
                turn_rows(nc, C, A, G, "turn2_", gather=True)
                C.end_phase()
                second_attention(nc, C, A, G)
                C.end_phase()
            if last >= 8:
                turn_rows(nc, C, A, G, "turn3_")
                C.end_phase()
                with ExitStack() as ctx2:
                    memory, clear, load = prepare_biases(C, A, "gb1_", "L1_ffn_b2", ctx2)
                    second_router(nc, C, A, G, clear, load)
                    C.end_phase()
                    add_gated_biases(nc, C, G, "gb1_", memory)
                    C.end_phase()
            if last >= 9:
                second_experts(nc, C, A, G)
                C.end_phase()


_OUT = ((B, T, D), "float32")


def kernel(**inputs):
    import concourse.bacc as bacc
    from concourse.bass_utils import run_bass_kernel_spmd

    nc = bacc.Bacc("TRN2", target_bir_lowering=False, num_devices=1)
    arrays, args = {}, {}
    for name, a in inputs.items():
        a = np.ascontiguousarray(a)
        arrays[f"in_{name}"] = a
        args[name] = nc.dram_tensor(f"in_{name}", a.shape, mybir.dt.from_np(a.dtype), kind="ExternalInput").ap()
    out = nc.dram_tensor("out_0_dram", _OUT[0], mybir.dt.from_np(np.dtype(_OUT[1])), kind="ExternalOutput").ap()
    program(nc, args, out)
    r = run_bass_kernel_spmd(nc, [arrays], core_ids=[0])
    return r.results[0]["out_0_dram"]
```
